# Optimizing a Trainium2 kernel written in Bass

```python
import numpy as np
import jax
import jax.numpy as jnp

def _softmax(x, axis=-1):
    return jax.nn.softmax(x, axis=axis)

def _gelu(x):
    return jax.nn.gelu(x, approximate=True)

def _silu(x):
    return jax.nn.silu(x)

def _sigmoid(x):
    return jax.nn.sigmoid(x)

def _layernorm(x, axis=-1, eps=1e-05):
    m = jnp.mean(x, axis=axis, keepdims=True)
    v = jnp.var(x, axis=axis, keepdims=True)
    return (x - m) / jnp.sqrt(v + eps)

def _scatter_add(tgt, idx, src, axis=0):
    return tgt.at[idx].add(src)

def _segment_sum(src, seg, n):
    return jax.ops.segment_sum(src, seg, n)
kernel_name = 'mk_gnn_ffn_d2_gnn_r32_0a91ad'

def setup_inputs(seed: int=0):
    np.random.seed(seed)
    _w = jnp.asarray

    def _rec_inputs():
        import jax
        import jax.numpy as jnp
        _gk = jax.random.key(seed)
        x = -0.0003713 + 1 * jax.random.normal(jax.random.fold_in(_gk, 1), (3125, 256), jnp.float32)
        src = jax.random.randint(jax.random.fold_in(_gk, 2), (50000,), 0, 3125, jnp.int32)
        dst = jax.random.randint(jax.random.fold_in(_gk, 3), (50000,), 0, 3125, jnp.int32)
        _o = jnp.argsort(dst, stable=True)
        src = src[_o]
        dst = dst[_o]
        edge_type_16 = jax.random.randint(jax.random.fold_in(_gk, 12), (50000,), 0, 16, jnp.int32)
        return (x, src, dst, edge_type_16)
    x, src, dst, edge_type_16 = _rec_inputs()

    def _L0_gnn_setup():
        import jax, jax.numpy as jnp
        import numpy as np
        N_NODES = 50000
        N_EDGES = 25000
        D = 256
        L = 3
        key = jax.random.key(seed)
        k1, k2, k3, k4, k5 = jax.random.split(key, 5)
        features = jax.random.normal(k1, (N_NODES, D), dtype=jnp.float32)
        scale = 1.0 / np.sqrt(D)
        W_self = jax.random.normal(k2, (L, D, D), dtype=jnp.float32) * scale
        W_neigh = jax.random.normal(k3, (L, D, D), dtype=jnp.float32) * scale
        bias = jnp.zeros((L, D), dtype=jnp.float32)
        src = jax.random.randint(k4, (N_EDGES,), 0, N_NODES, dtype=jnp.int32)
        dst = jax.random.randint(k5, (N_EDGES,), 0, N_NODES, dtype=jnp.int32)
        return {'features': features, 'W_self': W_self, 'W_neigh': W_neigh, 'bias': bias, 'src': src, 'dst': dst}
    _L0_gnn_all = _L0_gnn_setup()
    _L0_gnn_in = {k: v for k, v in _L0_gnn_all.items() if k in ('W_self', 'W_neigh', 'bias')}
    del _L0_gnn_all

    def _L0_ffn_setup():
        import jax, jax.numpy as jnp
        import numpy as np
        E = 8
        K = 2
        D = 256
        H = 512
        DOUT = 256
        EPS = 1e-05
        key = jax.random.key(seed)
        ks = jax.random.split(key, 9)
        s = 0.02
        return {'x': jax.random.normal(ks[0], (4, 256, D), jnp.float32), 'gamma': 1.0 + 0.05 * jax.random.normal(ks[1], (D,), jnp.float32), 'beta': 0.05 * jax.random.normal(ks[2], (D,), jnp.float32), 'Wr': 0.01 * jax.random.normal(ks[3], (D, E), jnp.float32), 'br': jnp.zeros((E,), jnp.float32), 'W1': s * jax.random.normal(ks[4], (E, D, H), jnp.float32), 'b1': s * jax.random.normal(ks[5], (E, H), jnp.float32), 'W2': s * jax.random.normal(ks[6], (E, H, DOUT), jnp.float32), 'b2': s * jax.random.normal(ks[7], (E, DOUT), jnp.float32)}
    _L0_ffn_all = _L0_ffn_setup()
    _L0_ffn_in = {k: v for k, v in _L0_ffn_all.items() if k in ('gamma', 'beta', 'Wr', 'br', 'W1', 'b1', 'W2', 'b2')}
    del _L0_ffn_all

    def _L1_gnn_setup():
        import jax, jax.numpy as jnp
        import numpy as np
        N_NODES = 50000
        N_EDGES = 25000
        HDIM = 256
        NUMRELS = 16

        def _gru_cell(x, h, w_ih, w_hh, b_ih, b_hh):
            gi = x @ w_ih.T + b_ih
            gh = h @ w_hh.T + b_hh
            i_r, i_z, i_n = jnp.split(gi, 3, axis=-1)
            h_r, h_z, h_n = jnp.split(gh, 3, axis=-1)
            r = jax.nn.sigmoid(i_r + h_r)
            z = jax.nn.sigmoid(i_z + h_z)
            n = jnp.tanh(i_n + r * h_n)
            return (1.0 - z) * n + z * h
        key = jax.random.key(seed)
        ks = jax.random.split(key, 9)
        h = jax.random.normal(ks[0], (N_NODES, HDIM), dtype=jnp.float32)
        relvectors = jax.random.normal(ks[1], (NUMRELS, HDIM), dtype=jnp.float32)
        s = 1.0 / np.sqrt(HDIM)
        w_ih = jax.random.uniform(ks[2], (3 * HDIM, HDIM), minval=-s, maxval=s, dtype=jnp.float32)
        w_hh = jax.random.uniform(ks[3], (3 * HDIM, HDIM), minval=-s, maxval=s, dtype=jnp.float32)
        b_ih = jax.random.uniform(ks[4], (3 * HDIM,), minval=-s, maxval=s, dtype=jnp.float32)
        b_hh = jax.random.uniform(ks[5], (3 * HDIM,), minval=-s, maxval=s, dtype=jnp.float32)
        edge_src = jax.random.randint(ks[6], (N_EDGES,), 0, N_NODES, dtype=jnp.int32)
        edge_dst = jax.random.randint(ks[7], (N_EDGES,), 0, N_NODES, dtype=jnp.int32)
        edge_rel = jax.random.randint(ks[8], (N_EDGES,), 0, NUMRELS, dtype=jnp.int32)
        return {'h': h, 'relvectors': relvectors, 'w_ih': w_ih, 'w_hh': w_hh, 'b_ih': b_ih, 'b_hh': b_hh, 'edge_src': edge_src, 'edge_dst': edge_dst, 'edge_rel': edge_rel}
    _L1_gnn_all = _L1_gnn_setup()
    _L1_gnn_in = {k: v for k, v in _L1_gnn_all.items() if k in ('relvectors', 'w_ih', 'w_hh', 'b_ih', 'b_hh')}
    del _L1_gnn_all

    def _L1_ffn_setup():
        import jax, jax.numpy as jnp
        import numpy as np
        B, S, H, F, E, K = (8, 128, 256, 512, 16, 2)
        EPS = 1e-05
        key = jax.random.key(seed)
        ks = jax.random.split(key, 9)
        sc = 0.02
        return {'x': jax.random.normal(ks[0], (B, S, H), dtype=jnp.float32), 'gate_w': jax.random.normal(ks[1], (H, E), dtype=jnp.float32) * sc, 'gate_b': jnp.zeros((E,), dtype=jnp.float32), 'w1': jax.random.normal(ks[2], (E, H, F), dtype=jnp.float32) * sc, 'b1': jnp.zeros((E, F), dtype=jnp.float32), 'w2': jax.random.normal(ks[3], (E, F, H), dtype=jnp.float32) * sc, 'b2': jnp.zeros((E, H), dtype=jnp.float32), 'gamma': jnp.ones((H,), dtype=jnp.float32), 'beta': jnp.zeros((H,), dtype=jnp.float32)}
    _L1_ffn_all = _L1_ffn_setup()
    _L1_ffn_in = {k: v for k, v in _L1_ffn_all.items() if k in ('gate_w', 'gate_b', 'w1', 'b1', 'w2', 'b2', 'gamma', 'beta')}
    del _L1_ffn_all
    return {'x': x, 'src': src, 'dst': dst, 'edge_type_16': edge_type_16, 'L0_gnn_W_self': _L0_gnn_in['W_self'], 'L0_gnn_W_neigh': _L0_gnn_in['W_neigh'], 'L0_gnn_bias': _L0_gnn_in['bias'], 'L0_ffn_gamma': _L0_ffn_in['gamma'], 'L0_ffn_beta': _L0_ffn_in['beta'], 'L0_ffn_Wr': _L0_ffn_in['Wr'], 'L0_ffn_br': _L0_ffn_in['br'], 'L0_ffn_W1': _L0_ffn_in['W1'], 'L0_ffn_b1': _L0_ffn_in['b1'], 'L0_ffn_W2': _L0_ffn_in['W2'], 'L0_ffn_b2': _L0_ffn_in['b2'], 'L1_gnn_relvectors': _L1_gnn_in['relvectors'], 'L1_gnn_w_ih': _L1_gnn_in['w_ih'], 'L1_gnn_w_hh': _L1_gnn_in['w_hh'], 'L1_gnn_b_ih': _L1_gnn_in['b_ih'], 'L1_gnn_b_hh': _L1_gnn_in['b_hh'], 'L1_ffn_gate_w': _L1_ffn_in['gate_w'], 'L1_ffn_gate_b': _L1_ffn_in['gate_b'], 'L1_ffn_w1': _L1_ffn_in['w1'], 'L1_ffn_b1': _L1_ffn_in['b1'], 'L1_ffn_w2': _L1_ffn_in['w2'], 'L1_ffn_b2': _L1_ffn_in['b2'], 'L1_ffn_gamma': _L1_ffn_in['gamma'], 'L1_ffn_beta': _L1_ffn_in['beta']}

def reference(x, src, dst, edge_type_16, L0_gnn_W_self, L0_gnn_W_neigh, L0_gnn_bias, L0_ffn_gamma, L0_ffn_beta, L0_ffn_Wr, L0_ffn_br, L0_ffn_W1, L0_ffn_b1, L0_ffn_W2, L0_ffn_b2, L1_gnn_relvectors, L1_gnn_w_ih, L1_gnn_w_hh, L1_gnn_b_ih, L1_gnn_b_hh, L1_ffn_gate_w, L1_ffn_gate_b, L1_ffn_w1, L1_ffn_b1, L1_ffn_w2, L1_ffn_b2, L1_ffn_gamma, L1_ffn_beta):
    import jax
    import jax.numpy as jnp

    def _L0_gnn_ref(features, W_self, W_neigh, bias, src, dst):
        import jax, jax.numpy as jnp
        import numpy as np
        N_NODES = 50000
        N_EDGES = 25000
        D = 256
        L = 3
        "3-layer GraphSAGE encoder (DGL SAGEConv, mean aggregator), eval mode.\n\n            Per layer: h_neigh = mean over in-neighbors of h (messages src -> dst);\n                       out = h @ W_self + h_neigh @ W_neigh + bias; relu except last.\n            feat_drop / wrapper dropout are identity in eval mode. The wrapper's relu\n            after layers 0,1 is idempotent with SAGEConv's internal relu.\n            "
        n = features.shape[0]
        ones = jnp.ones(src.shape[0], dtype=features.dtype)
        deg = jax.ops.segment_sum(ones, dst, num_segments=n)
        inv_deg = jnp.where(deg > 0, 1.0 / jnp.maximum(deg, 1.0), 0.0)[:, None]
        h = features
        for l in range(L):
            agg = jax.ops.segment_sum(h[src], dst, num_segments=n) * inv_deg
            h = h @ W_self[l] + agg @ W_neigh[l] + bias[l]
            if l < L - 1:
                h = jax.nn.relu(h)
        return h

    def _L0_ffn_ref(x, gamma, beta, Wr, br, W1, b1, W2, b2):
        import jax, jax.numpy as jnp
        import numpy as np
        E = 8
        K = 2
        D = 256
        H = 512
        DOUT = 256
        EPS = 1e-05
        mu = jnp.mean(x, axis=-1, keepdims=True)
        var = jnp.mean(jnp.square(x - mu), axis=-1, keepdims=True)
        xn = (x - mu) * jax.lax.rsqrt(var + EPS) * gamma + beta
        logits = jnp.einsum('bsd,de->bse', xn, Wr) + br
        top_vals, top_idx = jax.lax.top_k(logits, K)
        w = jax.nn.softmax(top_vals, axis=-1)
        w_full = jnp.einsum('bsk,bske->bse', w, jax.nn.one_hot(top_idx, E, dtype=w.dtype))
        y = jnp.zeros(x.shape[:-1] + (DOUT,), x.dtype)
        for e in range(E):
            h = jax.nn.gelu(jnp.einsum('bsd,dh->bsh', xn, W1[e]) + b1[e], approximate=False)
            y_e = jnp.einsum('bsh,hd->bsd', h, W2[e]) + b2[e]
            y = y + y_e * w_full[..., e, None]
        return y

    def _L1_gnn_ref(h, relvectors, w_ih, w_hh, b_ih, b_hh, edge_src, edge_dst, edge_rel):
        import jax, jax.numpy as jnp
        import numpy as np
        N_NODES = 50000
        N_EDGES = 25000
        HDIM = 256
        NUMRELS = 16

        def _gru_cell(x, h, w_ih, w_hh, b_ih, b_hh):
            gi = x @ w_ih.T + b_ih
            gh = h @ w_hh.T + b_hh
            i_r, i_z, i_n = jnp.split(gi, 3, axis=-1)
            h_r, h_z, h_n = jnp.split(gh, 3, axis=-1)
            r = jax.nn.sigmoid(i_r + h_r)
            z = jax.nn.sigmoid(i_z + h_z)
            n = jnp.tanh(i_n + r * h_n)
            return (1.0 - z) * n + z * h
        msg = h[edge_src] + relvectors[edge_rel]
        red = jax.ops.segment_sum(msg, edge_dst, num_segments=h.shape[0])
        return _gru_cell(red, h, w_ih, w_hh, b_ih, b_hh)

    def _L1_ffn_ref(x, gate_w, gate_b, w1, b1, w2, b2, gamma, beta):
        import jax, jax.numpy as jnp
        import numpy as np
        B, S, H, F, E, K = (8, 128, 256, 512, 16, 2)
        EPS = 1e-05
        gate_logits = x @ gate_w + gate_b
        topk_vals, topk_idx = jax.lax.top_k(gate_logits, K)
        topk_w = jax.nn.softmax(topk_vals, axis=-1)
        h = jax.nn.relu(jnp.einsum('bsh,ehf->bsef', x, w1) + b1)
        expert_out = jnp.einsum('bsef,efh->bseh', h, w2) + b2
        sel = jnp.take_along_axis(expert_out, topk_idx[:, :, :, None], axis=2)
        moe = jnp.sum(topk_w[..., None] * sel, axis=2)
        y = x + moe
        mu = jnp.mean(y, axis=-1, keepdims=True)
        var = jnp.var(y, axis=-1, keepdims=True)
        return (y - mu) / jnp.sqrt(var + EPS) * gamma + beta
    x = x + _L0_gnn_ref(_layernorm(x, axis=-1), L0_gnn_W_self, L0_gnn_W_neigh, L0_gnn_bias, src, dst)
    x = x + _L0_ffn_ref(_layernorm(x, axis=-1)[None], L0_ffn_gamma, L0_ffn_beta, L0_ffn_Wr, L0_ffn_br, L0_ffn_W1, L0_ffn_b1, L0_ffn_W2, L0_ffn_b2)[0]
    x = x + _L1_gnn_ref(_layernorm(x, axis=-1), L1_gnn_relvectors, L1_gnn_w_ih, L1_gnn_w_hh, L1_gnn_b_ih, L1_gnn_b_hh, src, dst, edge_type_16)
    x = x + _L1_ffn_ref(_layernorm(x, axis=-1)[None], L1_ffn_gate_w, L1_ffn_gate_b, L1_ffn_w1, L1_ffn_b1, L1_ffn_w2, L1_ffn_b2, L1_ffn_gamma, L1_ffn_beta)[0]
    return x

_drawn_inputs = setup_inputs


def setup_inputs(seed=0):
    import zlib

    import numpy as np

    out = dict(_drawn_inputs(seed))
    spreads = {'L0_gnn_bias': (0.0, 0.1),
     'L0_ffn_br': (0.0, 0.1),
     'L1_ffn_gate_b': (0.0, 0.397),
     'L1_ffn_b1': (0.0, 0.8),
     'L1_ffn_b2': (0.0, 0.318),
     'L1_ffn_gamma': (1.0, 0.2),
     'L1_ffn_beta': (0.0, 0.1)}
    factors = {'L0_ffn_gamma': 6.946,
     'L0_ffn_beta': 5.843,
     'L0_ffn_b1': 8.0,
     'L0_ffn_b2': 4.103,
     'L1_gnn_b_ih': 8.0,
     'L1_gnn_b_hh': 8.0}
    for name, (base, spread) in spreads.items():
        noise = np.random.default_rng([zlib.crc32(name.encode()), seed]).standard_normal(out[name].shape)
        drawn = base * np.exp(spread * noise) if base else spread * noise
        out[name] = jnp.asarray(drawn.astype(out[name].dtype))
    for name, factor in factors.items():
        out[name] = (out[name] * factor).astype(out[name].dtype)
    return out
```

```python
from contextlib import ExitStack, contextmanager

import numpy as np

import concourse.bass as bass
from concourse import mybir

F32 = mybir.dt.float32
F16 = mybir.dt.float16
I32 = mybir.dt.int32
ALU = mybir.AluOpType
ACT = mybir.ActivationFunctionType
AX = mybir.AxisListType

P = 128
N_NODES = 3125
D = 256
KD = D // P
N_EDGES = 50000
N_REL = 16
NT = -(-N_NODES // P)
NP = NT * P
LAST = N_NODES - (NT - 1) * P
ET = -(-N_EDGES // P)
EG = 4
FULL_ET = N_EDGES // P
EDGE_TAIL = N_EDGES - FULL_ET * P
TT = 32
MID = NP // 2
NOWHERE = 4000
HID = 512
KH = HID // P
LAYERS = 3
EPS = 1e-5
LO_SCALE = 2048.0
BANK = 512
CHUNKS = BANK // P
NBANKS = -(-NT // CHUNKS)


class Scratch:
    pass


class Resident:
    pass


class Plan:
    pass


def max_tiles(experts):
    return 2 * NP // P + experts


@contextmanager
def semaphores(nc, tag):
    held = []

    def sem(name):
        held.append(nc.alloc_semaphore(tag + name))
        return held[-1]

    yield sem
    nc.clear_and_free_semaphores(held)
    nc.all_engine_barrier()


def at_start(k):
    return isinstance(k, int) and k == 0


def tile_loop(engine, step):
    step(0, 0)
    step(0, 1)
    with engine.Fori(1, NT // 2) as k:
        step(k, 0)
        step(k, 1)
    step(NT // 2, 0)


def rows(t):
    return bass.ds(t * P, P)


def uses(b):
    return NT // 2 + (1 - b)


def index_edges(nc, ins, cst, dr):
    with ExitStack() as ctx:
        sb = lambda n, s, d=F32: ctx.enter_context(nc.sbuf_tensor(n, s, d))
        sem = ctx.enter_context(semaphores(nc, "graph_"))
        raw = sb("edges_raw", [P, 3, EG, P], I32)
        val = sb("edges_val", [P, 3, EG, P])
        low = sb("dst_low", [P, EG])
        high = sb("dst_high", [P, EG])
        diag = sb("range_diag", [P, 2, EG, P])
        ones = sb("range_ones", [P, TT])
        upto = sb("range_upto", [TT, TT])
        number = sb("range_number", [TT, EG * P])
        first_node = sb("first_node", [TT, 1])
        last_node = sb("last_node", [TT, 1])
        inside = sb("range_inside", [TT, EG * P])
        key = sb("range_key", [TT, EG * P])
        after = sb("range_after", [TT, 1])
        left = sb("range_left", [TT, 1])
        left_i = sb("range_left_i", [TT, 1], I32)
        col = sb("range_col", [TT, 3])
        ps_edges = ctx.enter_context(nc.psum_tensor("ps_edges", [P, 3, EG * P], F32))
        ps_low = ctx.enter_context(nc.psum_tensor("ps_low", [TT, EG * P], F32))
        ps_high = ctx.enter_context(nc.psum_tensor("ps_high", [TT, EG * P], F32))
        ps_before = ctx.enter_context(nc.psum_tensor("ps_before", [TT, BANK], F32))
        ps_tab = ctx.enter_context(nc.psum_tensor("ps_tab", [TT, BANK], F32))

        padded, loaded, consts = sem("edge_padded"), sem("edge_loaded"), sem("edge_consts")
        valued, ranged = sem("edge_valued"), sem("edge_ranged")
        turned, copied = sem("edge_turned"), sem("edge_copied")
        spread, counted = sem("edge_spread"), sem("edge_counted")
        summed, tabled = sem("edge_summed"), sem("edge_tabled")
        turned_tab = sem("edge_turned_tab")
        names = ("src", "dst", "edge_type_16")
        FG = FULL_ET // P
        REST = FULL_ET - FG * P

        with nc.Block() as block:

            @block.sync
            def _(sp):
                sp.wait_ge(padded, 1)
                for a, n in enumerate(names):
                    sp.dma_start(raw[:, a, 0:FG, :], ins[n][0:FG * P * P].rearrange(
                        "(g p e) -> p g e", g=FG, p=P)).then_inc(loaded, 16)
                    sp.dma_start(raw[0:REST, a, FG, :], ins[n][FG * P * P:FULL_ET * P].rearrange(
                        "(p e) -> p e", e=P)).then_inc(loaded, 16)
                    sp.dma_start(raw[REST:REST + 1, a, FG, 0:EDGE_TAIL], ins[n][FULL_ET * P:N_EDGES].rearrange(
                        "(p e) -> p e", p=1)).then_inc(loaded, 16)

            @block.gpsimd
            def _(pool):
                nc.gpsimd.memset(raw[:, :, FG, :], NOWHERE).then_inc(padded, 1)
                nc.gpsimd.memset(ones[:], 1.0)
                nc.gpsimd.memset(upto[:], 1.0)
                nc.gpsimd.memset(cst.ident[:], 0.0)
                nc.gpsimd.memset(cst.ones[:], 1.0)
                nc.gpsimd.memset(cst.before[:], 1.0)
                nc.gpsimd.memset(cst.lo_scale[:], LO_SCALE)
                nc.gpsimd.iota(cst.node_of[:], [[1, NP]], base=-MID, channel_multiplier=0,
                               allow_small_or_imprecise_dtypes=True)
                nc.gpsimd.iota(number[:], [[1, EG * P]], base=0, channel_multiplier=0,
                               allow_small_or_imprecise_dtypes=True)
                nc.gpsimd.iota(first_node[:], [[0, 1]], base=-MID, channel_multiplier=P,
                               allow_small_or_imprecise_dtypes=True)
                nc.gpsimd.iota(last_node[:], [[0, 1]], base=P - 1 - MID, channel_multiplier=P,
                               allow_small_or_imprecise_dtypes=True)
                pool.drain()
                nc.gpsimd.affine_select(out=cst.ident[:], in_=cst.ident[:], compare_op=ALU.not_equal, fill=1.0,
                                        base=0, pattern=[[-1, P]], channel_multiplier=1)
                nc.gpsimd.affine_select(out=cst.before[:], in_=cst.before[:], compare_op=ALU.is_gt, fill=0.0,
                                        base=0, pattern=[[1, P]], channel_multiplier=-1)
                nc.gpsimd.affine_select(out=upto[:], in_=upto[:], compare_op=ALU.is_gt, fill=0.0,
                                        base=0, pattern=[[1, TT]], channel_multiplier=-1).then_inc(consts, 1)

            @block.vector
            def _(dve):
                dve.wait_ge(loaded, 16 * 9)
                nc.vector.tensor_scalar(val[:, 0:2], raw[:, 0:2], -float(MID), None, ALU.add)
                nc.vector.tensor_copy(val[:, 2], raw[:, 2]).then_inc(valued, 1)
                dve.drain()
                nc.vector.tensor_reduce(low[:], val[:, 1], AX.X, ALU.min)
                nc.vector.tensor_reduce(high[:], val[:, 1], AX.X, ALU.max)
                dve.wait_ge(consts, 1)
                dve.drain()
                for side, v in enumerate((low, high)):
                    for g in range(EG):
                        last = nc.vector.tensor_scalar(diag[:, side, g, :], cst.ident[:], v[:, g:g + 1], None, ALU.mult)
                last.then_inc(ranged, 1)
                dve.wait_ge(turned, 1)
                nc.vector.tensor_copy(cst.edge[:], ps_edges[:]).then_inc(copied, 1)
                dve.wait_ge(spread, 1)
                nc.vector.tensor_scalar(key[:], ps_high[:], first_node[:, 0:1], None, ALU.is_ge)
                dve.drain()
                nc.vector.scalar_tensor_tensor(inside[:], ps_low[:], last_node[:, 0:1], key[:], ALU.is_le, ALU.mult)
                dve.drain()
                nc.vector.scalar_tensor_tensor(key[:], inside[:], -1000.0, number[:], ALU.mult, ALU.add)
                dve.drain()
                nc.vector.tensor_reduce(left[:], key[:], AX.X, ALU.min)
                dve.drain()
                nc.vector.tensor_scalar(col[:, 0:1], left[:], 1000.0, float(ET - 1), ALU.add, ALU.min)
                nc.vector.scalar_tensor_tensor(key[:], number[:], 1.0, inside[:], ALU.add, ALU.mult)
                dve.drain()
                nc.vector.tensor_reduce(after[:], key[:], AX.X, ALU.max)
                dve.drain()
                nc.vector.scalar_tensor_tensor(left[:], col[:, 0:1], -1.0, after[:], ALU.mult, ALU.add)
                dve.drain()
                nc.vector.tensor_scalar(left_i[:], left[:], -1.0, None, ALU.add)
                dve.drain()
                nc.vector.tensor_scalar(left_i[:], left_i[:], 1, None, ALU.arith_shift_right)
                dve.drain()
                nc.vector.tensor_scalar(col[:, 1:2], left_i[:], 1.0, 1.0, ALU.max, ALU.add).then_inc(counted, 1)
                dve.wait_ge(summed, 1)
                nc.vector.tensor_copy(col[:, 2:3], ps_before[:, 0:1]).then_inc(tabled, 1)
                dve.wait_ge(turned_tab, 1)
                nc.vector.tensor_copy(cst.ranges[:], ps_tab[0:3, 0:TT])

            @block.tensor
            def _(pe):
                pe.wait_ge(consts, 1)
                pe.wait_ge(valued, 1)
                for a in range(3):
                    for g in range(EG):
                        last = nc.tensor.transpose(ps_edges[:, a, g * P:(g + 1) * P], val[:, a, g, :], cst.ident[:])
                last.then_inc(turned, 1)
                pe.wait_ge(ranged, 1)
                for side, ps in enumerate((ps_low, ps_high)):
                    for g in range(EG):
                        last = nc.tensor.matmul(ps[:, g * P:(g + 1) * P], ones[:], diag[:, side, g, :],
                                                start=True, stop=True)
                last.then_inc(spread, 1)
                pe.wait_ge(counted, 1)
                nc.tensor.matmul(ps_before[:, 0:1], upto[:], col[:, 1:2], start=True, stop=True).then_inc(summed, 1)
                pe.wait_ge(tabled, 1)
                nc.tensor.transpose(ps_tab[0:3, 0:TT], col[:], cst.ident[0:TT, 0:TT]).then_inc(turned_tab, 1)


def build_counts(nc, ins, cst, dr):
    with ExitStack() as ctx:
        sb = lambda n, s, d=F32: ctx.enter_context(nc.sbuf_tensor(n, s, d))
        sem = ctx.enter_context(semaphores(nc, "graph_"))
        is_src = [sb(f"is_src{h}", [P, NP], F16) for h in range(2)]
        is_dst = [sb(f"is_dst{h}", [P, P], F16) for h in range(2)]
        is_rel = [sb(f"is_rel{h}", [P, N_REL + 1], F16) for h in range(2)]
        zeros = sb("zeros", [P, D])
        degree = sb("degree", [P, NT])
        some = sb("degree_some", [P, NT])
        acc = ctx.enter_context(nc.psum_tensor("ps_counts", [P, NBANKS * BANK], F32))
        acc_rel = ctx.enter_context(nc.psum_tensor("ps_rel", [P, BANK], F32))
        hot, spent, moved = sem("hot"), sem("hot_spent"), sem("counts_moved")
        zeroed, filled = sem("zeroed"), sem("filled")

        with nc.Block() as block:

            @block.sync
            def _(sp):
                sp.wait_ge(zeroed, 1)
                sp.dma_start(dr.x0[0:N_NODES, :], ins["x"]).then_inc(filled, 16)
                sp.dma_start(dr.x0[N_NODES:NP, :], zeros[0:NP - N_NODES, :]).then_inc(filled, 16)
                with sp.Fori(0, dr.slots.shape[0] // P) as q:
                    sp.dma_start(dr.slots[rows(q), :], zeros[:]).then_inc(filled, 16)
                sp.wait_ge(filled, 16 * (2 + dr.slots.shape[0] // P))

            @block.vector
            def _(dve):
                nc.vector.memset(zeros[:], 0.0).then_inc(zeroed, 1)
                for h in range(2):
                    nc.vector.memset(is_rel[h][:, N_REL:], 1.0)
                with dve.Fori(0, NT) as t:
                    first = dve.value_load(cst.ranges[0:1, bass.ds(t, 1)], min_val=0, max_val=ET - 1)
                    pairs = dve.value_load(cst.ranges[1:2, bass.ds(t, 1)], min_val=2, max_val=ET)
                    done = dve.value_load(cst.ranges[2:3, bass.ds(t, 1)], min_val=0, max_val=NT * ET)
                    with dve.Fori(0, pairs) as n:
                        for h in range(2):
                            j = nc.s_assert_within(first + n * 2 + h, 0, EG * P - 1, 
                                                   skip_runtime_bounds_check_because="edge tiles end below")
                            dve.wait_ge(spent, (done + n) * 2 + h + 1)
                            nc.vector.tensor_scalar(is_src[h][:], cst.node_of[:], cst.edge[:, 0, bass.ds(j, 1)],
                                                    None, ALU.is_equal)
                            nc.vector.tensor_scalar(is_dst[h][:], cst.node_of[:, bass.ds(t * P, P)],
                                                    cst.edge[:, 1, bass.ds(j, 1)], None, ALU.is_equal)
                            nc.vector.tensor_scalar(is_rel[h][:, 0:N_REL], cst.node_of[:, MID:MID + N_REL],
                                                    cst.edge[:, 2, bass.ds(j, 1)], None, ALU.is_equal).then_inc(hot, 1)
                dve.wait_ge(moved, (NBANKS + 1) * (NT + 1))
                nc.vector.tensor_scalar(degree[:], cst.rel_count[:, :, N_REL], 1.0, None, ALU.max)
                nc.vector.tensor_scalar(some[:], cst.rel_count[:, :, N_REL], 1.0, None, ALU.min)
                dve.drain()
                nc.vector.reciprocal(degree[:], degree[:])
                dve.drain()
                nc.vector.tensor_tensor(cst.inv_deg[:], degree[:], some[:], ALU.mult)

            @block.tensor
            def _(pe):
                pe.sem_inc(spent, 2)

                def edge_tile(t, done, n, h, first):
                    pe.wait_ge(hot, (done + n) * 2 + h + 1)
                    for c in range(NT):
                        if first and c % CHUNKS == 0:
                            pe.wait_ge(moved, t * (NBANKS + 1) + (c // CHUNKS + 1))
                        nc.tensor.matmul(acc[:, c * P:(c + 1) * P], is_src[h][:, c * P:(c + 1) * P], is_dst[h][:],
                                         start=first and c % CHUNKS == 0, stop=True, skip_group_check=True)
                    if first:
                        pe.wait_ge(moved, (t + 1) * (NBANKS + 1))
                    nc.tensor.matmul(acc_rel[:, 0:N_REL + 1], is_dst[h][:], is_rel[h][:], start=first, stop=True,
                                     skip_group_check=True).then_inc(spent, 1)

                with pe.Fori(0, NT) as t:
                    pairs = pe.value_load(cst.ranges[1:2, bass.ds(t, 1)], min_val=2, max_val=ET)
                    done = pe.value_load(cst.ranges[2:3, bass.ds(t, 1)], min_val=0, max_val=NT * ET)
                    edge_tile(t, done, 0, 0, True)
                    edge_tile(t, done, 0, 1, False)
                    with pe.Fori(1, pairs) as n:
                        edge_tile(t, done, n, 0, False)
                        edge_tile(t, done, n, 1, False)

            @block.scalar
            def _(act):
                act.sem_inc(moved, NBANKS + 1)
                with act.Fori(0, NT) as t:
                    pairs = act.value_load(cst.ranges[1:2, bass.ds(t, 1)], min_val=2, max_val=ET)
                    done = act.value_load(cst.ranges[2:3, bass.ds(t, 1)], min_val=0, max_val=NT * ET)
                    act.wait_ge(spent, (done + pairs) * 2 + 2)
                    row = cst.counts[:, bass.ds(t, 1), :, :].rearrange("p a s n -> p (a s n)")
                    for b in range(NBANKS):
                        lo, hi = b * BANK, min((b + 1) * BANK, NP)
                        nc.scalar.copy(row[:, lo:hi], acc[:, lo:hi]).then_inc(moved, 1)
                    nc.scalar.copy(cst.rel_count[:, bass.ds(t, 1), :].rearrange("p a r -> p (a r)"),
                                   acc_rel[:, 0:N_REL + 1]).then_inc(moved, 1)


def normalize(nc, dve, out, src, small, var_ready, std_ready, count):
    nc.vector.bn_stats(small[:, 0:6], src)
    dve.drain()
    nc.vector.bn_aggr(small[:, 6:8], small[:, 0:6])
    dve.drain()
    nc.vector.tensor_scalar(small[:, 8:9], small[:, 7:8], EPS, None, ALU.add).then_inc(var_ready, 1)
    dve.wait_ge(std_ready, count)
    nc.vector.reciprocal(small[:, 10:11], small[:, 9:10])
    dve.drain()
    return nc.vector.tensor_scalar(out, src, small[:, 6:7], small[:, 10:11], ALU.subtract, ALU.mult)


def project(nc, ins, cst, dr, layer, source, parts):
    norm = layer == 0
    with ExitStack() as ctx:
        tag = f"proj{layer}_"
        sb = lambda n, s, d=F32: ctx.enter_context(nc.sbuf_tensor(tag + n, s, d))
        sem = ctx.enter_context(semaphores(nc, tag))
        weights = sb("weights", [P, KD, 2 * D])
        bias = sb("bias", [P, D])
        h = [sb(f"h{b}", [P, D]) for b in range(2)]
        hn = [sb(f"hn{b}", [P, D]) for b in range(2)] if norm else h
        hT = [sb(f"hT{b}", [P, KD, P]) for b in range(2)]
        rest = [sb(f"rest{b}", [P, D]) for b in range(2)]
        own = [sb(f"own{b}", [P, D]) for b in range(2)]
        small = sb("small", [P, 12])
        ps_t = [ctx.enter_context(nc.psum_tensor(tag + f"ps_t{b}", [P, KD, P], F32)) for b in range(2)]
        ps_o = [ctx.enter_context(nc.psum_tensor(tag + f"ps_o{b}", [P, 2 * D], F32)) for b in range(2)]
        w_loaded = sem("w_loaded")
        h_loaded = [sem(f"h_loaded{b}") for b in range(2)]
        stored = [sem(f"stored{b}") for b in range(2)]
        var_ready, std_ready, normed = sem("var_ready"), sem("std_ready"), sem("normed")
        turned, hT_ready, product = sem("turned"), sem("hT_ready"), sem("product")
        hi_ready, rest_ready, own_ready, lo_ready = sem("hi_ready"), sem("rest_ready"), sem("own_ready"), sem("lo_ready")

        with nc.Block() as block:

            @block.sync
            def _(sp):
                for k in range(KD):
                    sp.dma_start(weights[:, k, 0:D], ins["L0_gnn_W_self"][layer, rows(k), :]).then_inc(w_loaded, 16)
                    sp.dma_start(weights[:, k, D:2 * D], ins["L0_gnn_W_neigh"][layer, rows(k), :]).then_inc(w_loaded, 16)
                sp.dma_start(bias[:], ins["L0_gnn_bias"][layer].partition_broadcast(P)).then_inc(w_loaded, 16)

                def step(k, b):
                    t = k * 2 + b
                    if not at_start(k):
                        sp.wait_ge(normed if norm else turned, t - 1)
                    sp.dma_start(h[b][:], source[rows(t), :]).then_inc(h_loaded[b], 16)

                tile_loop(sp, step)

            @block.tensor
            def _(pe):
                pe.wait_ge(w_loaded, 16 * (2 * KD + 1))

                def step(k, b):
                    t = k * 2 + b
                    if norm:
                        pe.wait_ge(normed, t + 1)
                    else:
                        pe.wait_ge(h_loaded[b], (k + 1) * 16)
                    for c in range(KD):
                        last = nc.tensor.transpose(ps_t[b][:, c, :], hn[b][:, c * P:(c + 1) * P], cst.ident[:])
                    last.then_inc(turned, 1)
                    pe.wait_ge(hT_ready, t + 1)
                    if not at_start(k):
                        pe.wait_ge(own_ready, t - 1)
                    for c in range(KD):
                        last = nc.tensor.matmul(ps_o[b][:], hT[b][:, c, :], weights[:, c, :],
                                                start=c == 0, stop=c == KD - 1)
                    last.then_inc(product, 1)

                tile_loop(pe, step)

            @block.scalar
            def _(act):
                def step(k, b):
                    t = k * 2 + b
                    if norm:
                        act.wait_ge(var_ready, t + 1)
                        nc.scalar.activation(small[:, 9:10], small[:, 8:9], ACT.Sqrt).then_inc(std_ready, 1)
                    act.wait_ge(turned, t + 1)
                    nc.scalar.copy(hT[b][:], ps_t[b][:]).then_inc(hT_ready, 1)
                    act.wait_ge(product, t + 1)
                    nc.scalar.copy(parts[:, bass.ds(t, 1), 0:D].rearrange("p a d -> p (a d)"),
                                   ps_o[b][:, D:2 * D]).then_inc(hi_ready, 1)

                tile_loop(act, step)

            @block.vector
            def _(dve):
                def load_norm(k, b):
                    t = k * 2 + b
                    dve.wait_ge(h_loaded[b], (k + 1) * 16)
                    if not at_start(k):
                        dve.wait_ge(turned, t - 1)
                    normalize(nc, dve, hn[b][:], h[b][:], small, var_ready, std_ready, t + 1).then_inc(normed, 1)

                def step(k, b):
                    t = k * 2 + b
                    if norm:
                        load_norm(k, b)
                    dve.wait_ge(product, t + 1)
                    dve.wait_ge(hi_ready, t + 1)
                    if not at_start(k):
                        dve.wait_ge(lo_ready, t - 1)
                    nc.vector.tensor_tensor(rest[b][:], ps_o[b][:, D:2 * D],
                                            parts[:, bass.ds(t, 1), 0:D].rearrange("p a d -> p (a d)"),
                                            ALU.subtract).then_inc(rest_ready, 1)
                    if not at_start(k):
                        dve.wait_ge(stored[b], k * 16)
                    dve.wait_ge(w_loaded, 16 * (2 * KD + 1))
                    nc.vector.tensor_tensor(own[b][:], ps_o[b][:, 0:D], bias[:], ALU.add).then_inc(own_ready, 1)

                tile_loop(dve, step)

            @block.gpsimd
            def _(pool):
                def step(k, b):
                    t = k * 2 + b
                    pool.wait_ge(rest_ready, t + 1)
                    nc.gpsimd.tensor_tensor(parts[:, bass.ds(t, 1), D:2 * D].rearrange("p a d -> p (a d)"),
                                            rest[b][:], cst.lo_scale[:], ALU.mult).then_inc(lo_ready, 1)
                    pool.wait_ge(own_ready, t + 1)
                    pool.dma_start(dr.own[rows(t), :], own[b][:]).then_inc(stored[b], 16)

                tile_loop(pool, step)
                for b in range(2):
                    pool.wait_ge(stored[b], 16 * uses(b))


def aggregate(nc, ins, cst, dr, tag, parts, target, relu=False, residual=None, relations=False):
    with ExitStack() as ctx:
        sb = lambda n, s, d=F32: ctx.enter_context(nc.sbuf_tensor(tag + n, s, d))
        sem = ctx.enter_context(semaphores(nc, tag))
        own = [sb(f"own{b}", [P, D]) for b in range(2)]
        before = [sb(f"before{b}", [P, D]) for b in range(2)] if residual is not None else None
        total = [sb(f"total{b}", [P, D]) for b in range(2)]
        out = [sb(f"out{b}", [P, D]) for b in range(2)]
        ps = [ctx.enter_context(nc.psum_tensor(tag + f"ps{b}", [P, 2 * D], F32)) for b in range(2)]
        loaded = [sem(f"loaded{b}") for b in range(2)]
        stored = [sem(f"stored{b}") for b in range(2)]
        summed, taken, ready, rel_ready = sem("summed"), sem("taken"), sem("ready"), sem("rel_ready")
        if relations:
            vectors = sb("vectors", [N_REL, D])
            rel_in = [sb(f"rel_in{b}", [P, N_REL]) for b in range(2)]
            rel_T = [sb(f"rel_T{b}", [N_REL, P]) for b in range(2)]
            ps_rel = [ctx.enter_context(nc.psum_tensor(tag + f"ps_rel{b}", [N_REL, BANK], F32)) for b in range(2)]
            v_loaded, rel_copied, rel_turned = sem("v_loaded"), sem("rel_copied"), sem("rel_turned")
        per_tile = 1 + (residual is not None)

        with nc.Block() as block:

            @block.sync
            def _(sp):
                if relations:
                    sp.dma_start(vectors[:], ins["L1_gnn_relvectors"]).then_inc(v_loaded, 16)
                    return

                def step(k, b):
                    t = k * 2 + b
                    if not at_start(k):
                        sp.wait_ge(ready, t - 1)
                    sp.dma_start(own[b][:], dr.own[rows(t), :]).then_inc(loaded[b], 16)
                    if residual is not None:
                        sp.dma_start(before[b][:], residual[rows(t), :]).then_inc(loaded[b], 16)

                tile_loop(sp, step)

            @block.tensor
            def _(pe):
                if relations:
                    pe.wait_ge(v_loaded, 16)

                def step(k, b):
                    t = k * 2 + b
                    if relations:
                        pe.wait_ge(rel_copied, t + 1)
                        nc.tensor.transpose(ps_rel[b][:, 0:P], rel_in[b][:], cst.ident[:]).then_inc(rel_turned, 1)
                    if not at_start(k):
                        pe.wait_ge(taken, t - 1)
                    for s in range(NT):
                        last = nc.tensor.matmul(ps[b][:], cst.counts[:, bass.ds(t, 1), s, :].rearrange("p a n -> p (a n)"),
                                                parts[:, s, :], start=s == 0, stop=s == NT - 1 and not relations,
                                                skip_group_check=True)
                    if relations:
                        pe.wait_ge(rel_ready, t + 1)
                        last = nc.tensor.matmul(ps[b][:, 0:D], rel_T[b][:], vectors[:], start=False, stop=True,
                                                skip_group_check=True)
                    last.then_inc(summed, 1)

                tile_loop(pe, step)

            @block.scalar
            def _(act):
                def step(k, b):
                    t = k * 2 + b
                    if relations:
                        if not at_start(k):
                            act.wait_ge(rel_turned, t - 1)
                        nc.scalar.copy(rel_in[b][:], cst.rel_count[:, bass.ds(t, 1), 0:N_REL].rearrange(
                            "p a r -> p (a r)")).then_inc(rel_copied, 1)
                        act.wait_ge(rel_turned, t + 1)
                        if not at_start(k):
                            act.wait_ge(summed, t - 1)
                        nc.scalar.copy(rel_T[b][:], ps_rel[b][:, 0:P]).then_inc(rel_ready, 1)

                if relations:
                    tile_loop(act, step)

            @block.vector
            def _(dve):
                def step(k, b):
                    t = k * 2 + b
                    dve.wait_ge(summed, t + 1)
                    if not at_start(k):
                        dve.wait_ge(stored[b], k * 16)
                    if relations:
                        nc.vector.tensor_copy(total[b][:], ps[b][:, 0:D])
                        dve.drain()
                        nc.vector.scalar_tensor_tensor(out[b][:], ps[b][:, D:2 * D], 1.0 / LO_SCALE, total[b][:],
                                                       ALU.mult, ALU.add).then_inc(taken, 1)
                        return
                    nc.vector.tensor_copy(total[b][:], ps[b][:, 0:D])
                    dve.drain()
                    nc.vector.scalar_tensor_tensor(total[b][:], ps[b][:, D:2 * D], 1.0 / LO_SCALE, total[b][:],
                                                   ALU.mult, ALU.add).then_inc(taken, 1)
                    dve.drain()
                    dve.wait_ge(loaded[b], (k + 1) * (16 * per_tile))
                    last = nc.vector.scalar_tensor_tensor(out[b][:], total[b][:], cst.inv_deg[:, bass.ds(t, 1)], own[b][:],
                                                          ALU.mult, ALU.add)
                    if relu:
                        dve.drain()
                        last = nc.vector.tensor_scalar(out[b][:], out[b][:], 0.0, None, ALU.max)
                    if residual is not None:
                        dve.drain()
                        last = nc.vector.tensor_tensor(out[b][:], out[b][:], before[b][:], ALU.add)
                    last.then_inc(ready, 1)

                tile_loop(dve, step)

            @block.gpsimd
            def _(pool):
                def step(k, b):
                    t = k * 2 + b
                    pool.wait_ge(taken if relations else ready, t + 1)
                    pool.dma_start(target[rows(t), :], out[b][:]).then_inc(stored[b], 16)

                tile_loop(pool, step)
                for b in range(2):
                    pool.wait_ge(stored[b], 16 * uses(b))


def route(nc, cst, dr, tag, source, experts, router, router_bias, gamma, beta, tokens, plan):
    norms = 2 if gamma is not None else 1
    with ExitStack() as ctx:
        sb = lambda n, s, d=F32: ctx.enter_context(nc.sbuf_tensor(tag + n, s, d))
        sem = ctx.enter_context(semaphores(nc, tag))
        pb = lambda n, s: ctx.enter_context(nc.psum_tensor(tag + n, s, F32))
        E = experts
        weights = sb("router", [P, KD, E])
        bias = sb("bias", [P, E])
        scale, shift = (sb("gamma", [P, D]), sb("beta", [P, D])) if gamma is not None else (None, None)
        x = [sb(f"x{b}", [P, D]) for b in range(2)]
        xn = [sb(f"xn{b}", [P, D]) for b in range(2)]
        xT = [sb(f"xT{b}", [P, KD, P]) for b in range(2)]
        inner = sb("inner", [P, D])
        small = sb("small", [P, 12])
        logit = sb("logit", [P, NT, E])
        expert_no = sb("expert_no", [P, NT, E])
        first_of = sb("first_of", [P, E, NT])
        top = [sb(f"top{c}", [P, NT]) for c in range(2)]
        least = sb("least", [P, NT])
        key = sb("key", [P, NT, E])
        chosen = [sb(f"chosen{c}", [P, NT, E]) for c in range(2)]
        either = sb("either", [P, NT, E])
        ratio = sb("ratio", [P, NT])
        sums = sb("sums", [P, E, NT])
        upto = sb("upto", [P, E, NT])
        tiles = sb("tiles", [P, E])
        tiles_i = sb("tiles_i", [P, E], I32)
        ends = sb("ends", [P, E])
        ones = sb("ones_e", [P, E])
        base = sb("base", [P, E])
        slot = sb("slot", [P, NT, E])
        slot_f = [sb(f"slot_f{c}", [P, NT]) for c in range(2)]
        ps_t = [pb(f"ps_t{b}", [P, KD, P]) for b in range(2)]
        ps_l = [pb(f"ps_l{b}", [P, BANK]) for b in range(2)]
        ps_rank, ps_sum = pb("ps_rank", [P, BANK]), pb("ps_sum", [P, BANK])
        w_loaded, consts = sem("w_loaded"), sem("consts")
        loaded = [sem(f"loaded{b}") for b in range(2)]
        var_ready, std_ready, normed, kept = sem("var_ready"), sem("std_ready"), sem("normed"), sem("kept")
        turned, xT_ready, scored, logit_ready = sem("turned"), sem("xT_ready"), sem("scored"), sem("logit_ready")
        gap_ready, exp_ready, picked, ranked, slotted = (sem("gap_ready"), sem("exp_ready"), sem("picked"),
                                                         sem("ranked"), sem("slotted"))
        scattered = sem("scattered")
        n_w = 2 + 2 * (gamma is not None)

        with nc.Block() as block:

            @block.sync
            def _(sp):
                sp.dma_start(weights[:], router.rearrange("(k p) e -> p k e", p=P)).then_inc(w_loaded, 16)
                sp.dma_start(bias[:], router_bias.partition_broadcast(P)).then_inc(w_loaded, 16)
                if gamma is not None:
                    sp.dma_start(scale[:], gamma.partition_broadcast(P)).then_inc(w_loaded, 16)
                    sp.dma_start(shift[:], beta.partition_broadcast(P)).then_inc(w_loaded, 16)

                def step(k, b):
                    t = k * 2 + b
                    if not at_start(k):
                        sp.wait_ge(normed, t - 1)
                    sp.dma_start(x[b][:], source[rows(t), :]).then_inc(loaded[b], 16)

                tile_loop(sp, step)

            @block.scalar
            def _(act):
                def step(k, b):
                    t = k * 2 + b
                    for n in range(norms):
                        act.wait_ge(var_ready, t * norms + n + 1)
                        nc.scalar.activation(small[:, 9:10], small[:, 8:9], ACT.Sqrt).then_inc(std_ready, 1)
                    act.wait_ge(turned, t + 1)
                    nc.scalar.copy(xT[b][:], ps_t[b][:]).then_inc(xT_ready, 1)

                tile_loop(act, step)
                act.wait_ge(gap_ready, 1)
                nc.scalar.activation(ratio[:], ratio[:], ACT.Exp).then_inc(exp_ready, 1)

            @block.tensor
            def _(pe):
                pe.wait_ge(w_loaded, 16 * n_w)

                def step(k, b):
                    t = k * 2 + b
                    pe.wait_ge(normed, t + 1)
                    for c in range(KD):
                        last = nc.tensor.transpose(ps_t[b][:, c, :], xn[b][:, c * P:(c + 1) * P], cst.ident[:])
                    last.then_inc(turned, 1)
                    pe.wait_ge(xT_ready, t + 1)
                    if not at_start(k):
                        pe.wait_ge(logit_ready, t - 1)
                    for c in range(KD):
                        last = nc.tensor.matmul(ps_l[b][:, 0:E], xT[b][:, c, :], weights[:, c, :],
                                                start=c == 0, stop=c == KD - 1)
                    last.then_inc(scored, 1)

                tile_loop(pe, step)
                pe.wait_ge(picked, 1)
                flat = either[:].rearrange("p t e -> p (t e)")
                nc.tensor.matmul(ps_rank[:, 0:NT * E], cst.before[:], flat, start=True, stop=True)
                nc.tensor.matmul(ps_sum[:, 0:NT * E], cst.ones[:], flat, start=True, stop=True).then_inc(ranked, 1)

            @block.vector
            def _(dve):
                dve.wait_ge(w_loaded, 16 * n_w)

                def step(k, b):
                    t = k * 2 + b
                    dve.wait_ge(loaded[b], (k + 1) * 16)
                    if not at_start(k):
                        dve.wait_ge(turned, t - 1)
                        dve.wait_ge(kept, t - 1)
                    if gamma is None:
                        normalize(nc, dve, xn[b][:], x[b][:], small, var_ready, std_ready, t + 1).then_inc(normed, 1)
                    else:
                        normalize(nc, dve, inner[:], x[b][:], small, var_ready, std_ready, t * 2 + 1)
                        dve.drain()
                        normalize(nc, dve, inner[:], inner[:], small, var_ready, std_ready, t * 2 + 2)
                        dve.drain()
                        nc.vector.tensor_tensor(inner[:], inner[:], scale[:], ALU.mult)
                        dve.drain()
                        nc.vector.tensor_tensor(xn[b][:], inner[:], shift[:], ALU.add).then_inc(normed, 1)
                    dve.wait_ge(scored, t + 1)
                    nc.vector.tensor_tensor(logit[:, bass.ds(t, 1), :].rearrange("p a e -> p (a e)"), ps_l[b][:, 0:E],
                                            bias[:], ALU.add).then_inc(logit_ready, 1)

                tile_loop(dve, step)
                dve.wait_ge(consts, 1)
                wide = lambda a: a.unsqueeze(2).to_broadcast([P, NT, E])
                dve.drain()
                for c in range(2):
                    nc.vector.tensor_reduce(top[c][:], logit[:], AX.X, ALU.max)
                    dve.drain()
                    nc.vector.tensor_tensor(key[:], logit[:], wide(top[c][:]), ALU.is_equal)
                    dve.drain()
                    nc.vector.scalar_tensor_tensor(key[:], key[:], -100.0, expert_no[:], ALU.mult, ALU.add)
                    dve.drain()
                    nc.vector.tensor_reduce(least[:], key[:], AX.X, ALU.min)
                    dve.drain()
                    nc.vector.tensor_tensor(chosen[c][:], key[:], wide(least[:]), ALU.is_equal)
                    dve.drain()
                    if c == 0:
                        nc.vector.scalar_tensor_tensor(logit[:], chosen[c][:], -3e38, logit[:], ALU.mult, ALU.add)
                        dve.drain()
                nc.vector.tensor_tensor(either[:], chosen[0][:], chosen[1][:], ALU.add).then_inc(picked, 1)
                nc.vector.tensor_tensor(ratio[:], top[1][:], top[0][:], ALU.subtract).then_inc(gap_ready, 1)
                dve.wait_ge(exp_ready, 1)
                nc.vector.tensor_scalar(least[:], ratio[:], 1.0, None, ALU.add)
                dve.drain()
                nc.vector.reciprocal(plan.weight[0][:], least[:])
                dve.drain()
                nc.vector.tensor_tensor(plan.weight[1][:], plan.weight[0][:], ratio[:], ALU.mult)
                dve.wait_ge(ranked, 1)
                nc.vector.tensor_copy(sums[:].rearrange("p e t -> p t e"),
                                      ps_sum[:, 0:NT * E].rearrange("p (t e) -> p t e", e=E))
                dve.drain()
                nc.vector.tensor_tensor_scan(upto[:].rearrange("p e t -> p (e t)"), first_of[:].rearrange("p e t -> p (e t)"),
                                             sums[:].rearrange("p e t -> p (e t)"), 0.0, ALU.mult, ALU.add)
                dve.drain()
                nc.vector.tensor_scalar(tiles_i[:], upto[:, :, NT - 1], float(P - 1), None, ALU.add)
                dve.drain()
                nc.vector.tensor_scalar(tiles_i[:], tiles_i[:], P.bit_length() - 1, None, ALU.arith_shift_right)
                dve.drain()
                nc.vector.tensor_scalar(tiles[:], tiles_i[:], 1.0, None, ALU.max)
                dve.drain()
                nc.vector.tensor_tensor_scan(ends[:], ones[:], tiles[:], 0.0, ALU.mult, ALU.add)
                dve.drain()
                nc.vector.tensor_copy(plan.ends[:], ends[0:1, :])
                nc.vector.tensor_tensor(base[:], ends[:], tiles[:], ALU.subtract)
                dve.drain()
                nc.vector.tensor_copy(plan.starts[:], base[0:1, :])
                nc.vector.tensor_tensor(upto[:], upto[:], sums[:], ALU.subtract)
                dve.drain()
                nc.vector.scalar_tensor_tensor(upto[:], base[:].unsqueeze(2).to_broadcast([P, E, NT]), float(P), upto[:],
                                               ALU.mult, ALU.add)
                dve.drain()
                nc.vector.tensor_tensor(slot[:], ps_rank[:, 0:NT * E].rearrange("p (t e) -> p t e", e=E),
                                        upto[:].rearrange("p e t -> p t e"), ALU.add)
                dve.drain()
                for c in range(2):
                    nc.vector.tensor_tensor(key[:], slot[:], chosen[c][:], ALU.mult)
                    dve.drain()
                    nc.vector.tensor_reduce(slot_f[c][:], key[:], AX.X, ALU.add)
                    dve.drain()
                    nc.vector.tensor_copy(plan.slot[c][:], slot_f[c][:]).then_inc(slotted, 1)

            @block.gpsimd
            def _(pool):
                nc.gpsimd.iota(expert_no[:], [[0, NT], [1, E]], base=0, channel_multiplier=0,
                               allow_small_or_imprecise_dtypes=True)
                nc.gpsimd.memset(ones[:], 1.0)
                nc.gpsimd.memset(first_of[:], 1.0)
                pool.drain()
                nc.gpsimd.memset(first_of[:, :, 0:1], 0.0).then_inc(consts, 1)

                def step(k, b):
                    t = k * 2 + b
                    pool.wait_ge(normed, t + 1)
                    nc.gpsimd.tensor_copy(tokens[:, bass.ds(t, 1), :].rearrange("p a d -> p (a d)"),
                                          xn[b][:]).then_inc(kept, 1)

                tile_loop(pool, step)
                pool.wait_ge(kept, NT)
                for c in range(2):
                    pool.wait_ge(slotted, c + 1)
                    for t in range(NT):
                        pool.indirect_dma_start(dr.slots, bass.IndirectOffsetOnAxis(ap=plan.slot[c][:, t:t + 1], axis=0),
                                                tokens[:, t, :], None).then_inc(scattered, 16)
                pool.wait_ge(scattered, 16 * 2 * NT)


def run_experts(nc, cst, dr, tag, experts, w1, b1, w2, b2, function, plan):
    with ExitStack() as ctx:
        sb = lambda n, s, d=F32: ctx.enter_context(nc.sbuf_tensor(tag + n, s, d))
        sem = ctx.enter_context(semaphores(nc, tag))
        pb = lambda n, s: ctx.enter_context(nc.psum_tensor(tag + n, s, F32))
        E = experts
        up = [sb(f"up{b}", [P, KD, HID]) for b in range(2)]
        down = [sb(f"down{b}", [P, KH, D]) for b in range(2)]
        b1_rows = sb("b1_rows", [E * KH, P])
        b1_col = sb("b1_col", [P, E * KH])
        b2_all = sb("b2_all", [P, E, D])
        x = sb("x", [P, D])
        xT = sb("xT", [P, KD, P])
        hT = sb("hT", [P, KH, P])
        y = sb("y", [P, D])
        ps_x, ps_y, ps_b = pb("ps_x", [P, KD, P]), pb("ps_y", [P, BANK]), pb("ps_b", [P, BANK])
        ps_h = [pb(f"ps_h{c}", [P, BANK]) for c in range(KH)]
        b_loaded, b1_turned, b1_ready = sem("b_loaded"), sem("b1_turned"), sem("b1_ready")
        w_loaded = [sem(f"w_loaded{b}") for b in range(2)]
        x_loaded, x_turned, xT_ready = sem("x_loaded"), sem("x_turned"), sem("xT_ready")
        h_ready, hT_ready, y_product, y_ready = sem("h_ready"), sem("hT_ready"), sem("y_product"), sem("y_ready")
        y_stored, y_free = sem("y_stored"), sem("y_free")
        most = max_tiles(E)

        def bounds(engine, e):
            return (engine.value_load(plan.starts[0:1, bass.ds(e, 1)], min_val=0, max_val=most - 1),
                    engine.value_load(plan.ends[0:1, bass.ds(e, 1)], min_val=1, max_val=most))

        def expert_loop(engine, step):
            with engine.Fori(0, E // 2) as k:
                for b in range(2):
                    step(k * 2 + b, k, b, *bounds(engine, k * 2 + b))

        with nc.Block() as block:

            @block.sync
            def _(sp):
                def load(e, b):
                    sp.dma_start(up[b][:], w1[bass.ds(e, 1)].rearrange("a (k p) h -> p (a k) h", p=P)).then_inc(w_loaded[b], 16)
                    sp.dma_start(down[b][:], w2[bass.ds(e, 1)].rearrange("a (k p) d -> p (a k) d", p=P)).then_inc(w_loaded[b], 16)

                def store_tiles(start, end):
                    with sp.Fori(start, end) as q:
                        sp.wait_ge(y_ready, q + 2)
                        sp.dma_start(dr.slots[rows(q), :], y[:]).then_inc(y_stored, 16)
                        sp.wait_ge(y_stored, (q + 1) * 16)
                        sp.sem_inc(y_free, 1)

                sp.sem_inc(y_free, 1)
                load(0, 0)
                sp.dma_start(b1_rows[:], b1.rearrange("e (k p) -> (e k) p", p=P)).then_inc(b_loaded, 16)
                sp.dma_start(b2_all[:], b2.partition_broadcast(P)).then_inc(b_loaded, 16)
                with sp.Fori(0, E // 2 - 1) as k:
                    for b in range(2):
                        load(k * 2 + (b + 1), 1 - b)
                        store_tiles(*bounds(sp, k * 2 + b))
                load(E - 1, 1)
                store_tiles(*bounds(sp, E - 2))
                store_tiles(*bounds(sp, E - 1))

            @block.gpsimd
            def _(pool):
                total = pool.value_load(plan.ends[0:1, E - 1:E], min_val=1, max_val=most)
                pool.dma_start(x[:], dr.slots[0:P, :]).then_inc(x_loaded, 16)
                with pool.Fori(1, total + 1) as q:
                    pool.wait_ge(x_turned, q)
                    pool.dma_start(x[:], dr.slots[rows(q), :]).then_inc(x_loaded, 16)
                pool.wait_ge(x_loaded, total * 16 + 16)

            @block.tensor
            def _(pe):
                pe.wait_ge(b_loaded, 32)
                nc.tensor.transpose(ps_b[:, 0:E * KH], b1_rows[:], cst.ident[0:E * KH, 0:E * KH]).then_inc(b1_turned, 1)

                def turn(q):
                    pe.wait_ge(x_loaded, q * 16 + 16)
                    for c in range(KD):
                        last = nc.tensor.transpose(ps_x[:, c, :], x[:, c * P:(c + 1) * P], cst.ident[:])
                    last.then_inc(x_turned, 1)

                turn(0)

                def step(e, k, b, start, end):
                    with pe.Fori(start, end) as q:
                        pe.wait_ge(w_loaded[b], k * 32 + 32)
                        pe.wait_ge(xT_ready, q + 1)
                        for c in range(KH):
                            for i in range(KD):
                                last = nc.tensor.matmul(ps_h[c][:, 0:P], up[b][:, i, c * P:(c + 1) * P], xT[:, i, :],
                                                        start=i == 0, stop=i == KD - 1)
                            last.then_inc(h_ready, 1)
                        turn(q + 1)
                        pe.wait_ge(y_ready, q + 1)
                        for c in range(KH):
                            pe.wait_ge(hT_ready, q * KH + (c + 1))
                            last = nc.tensor.matmul(ps_y[:, 0:D], hT[:, c, :], down[b][:, c, :],
                                                    start=c == 0, stop=c == KH - 1)
                        last.then_inc(y_product, 1)

                expert_loop(pe, step)

            @block.scalar
            def _(act):
                act.wait_ge(b1_turned, 1)
                nc.scalar.copy(b1_col[:], ps_b[:, 0:E * KH])
                act.drain()

                def step(e, k, b, start, end):
                    with act.Fori(start, end) as q:
                        for c in range(KH):
                            act.wait_ge(h_ready, q * KH + (c + 1))
                            nc.scalar.activation(hT[:, c, :], ps_h[c][:, 0:P], function,
                                                 bias=b1_col[:, bass.ds(e * KH + c, 1)]).then_inc(hT_ready, 1)

                expert_loop(act, step)

            @block.vector
            def _(dve):
                dve.sem_inc(y_ready, 1)
                dve.wait_ge(b_loaded, 32)
                dve.wait_ge(x_turned, 1)
                nc.vector.tensor_copy(xT[:], ps_x[:]).then_inc(xT_ready, 1)

                def step(e, k, b, start, end):
                    with dve.Fori(start, end) as q:
                        dve.wait_ge(x_turned, q + 2)
                        nc.vector.tensor_copy(xT[:], ps_x[:]).then_inc(xT_ready, 1)
                        dve.wait_ge(y_product, q + 1)
                        dve.wait_ge(y_free, q + 1)
                        nc.vector.tensor_tensor(y[:], ps_y[:, 0:D], b2_all[:, bass.ds(e, 1), :].rearrange(
                            "p a d -> p (a d)"), ALU.add).then_inc(y_ready, 1)

                expert_loop(dve, step)


def combine(nc, cst, dr, tag, plan, source, target, parts=None, normed_out=None, tokens=None, gamma=None, beta=None,
            output=None):
    final = output is not None
    with ExitStack() as ctx:
        sb = lambda n, s, d=F32: ctx.enter_context(nc.sbuf_tensor(tag + n, s, d))
        sem = ctx.enter_context(semaphores(nc, tag))
        x = [sb(f"x{b}", [P, D]) for b in range(2)]
        y = [[sb(f"y{b}_{c}", [P, D]) for c in range(2)] for b in range(2)]
        mixed = [sb(f"mixed{b}", [P, D]) for b in range(2)]
        out = [sb(f"out{b}", [P, D]) for b in range(2)]
        hn = [sb(f"hn{b}", [P, D]) for b in range(2)]
        rest = [sb(f"rest{b}", [P, D]) for b in range(2)]
        small = sb("small", [P, 12])
        scale, shift = (sb("gamma", [P, D]), sb("beta", [P, D])) if final else (None, None)
        w_loaded = sem("w_loaded")
        loaded = [sem(f"loaded{b}") for b in range(2)]
        got = [sem(f"got{b}") for b in range(2)]
        stored = [sem(f"stored{b}") for b in range(2)]
        var_ready, std_ready, ready = sem("var_ready"), sem("std_ready"), sem("ready")
        taken, hi_ready, rest_ready, lo_ready = sem("taken"), sem("hi_ready"), sem("rest_ready"), sem("lo_ready")
        stores = 1 if final else 2

        with nc.Block() as block:

            @block.sync
            def _(sp):
                if final:
                    sp.dma_start(scale[:], gamma.partition_broadcast(P)).then_inc(w_loaded, 16)
                    sp.dma_start(shift[:], beta.partition_broadcast(P)).then_inc(w_loaded, 16)

                def load(t, b):
                    sp.dma_start(x[b][:], source[rows(t), :]).then_inc(loaded[b], 16)

                def store(t, b):
                    sp.wait_ge(ready, t + 1)
                    if final:
                        if isinstance(t, int) and t == NT - 1:
                            sp.dma_start(output[t * P:N_NODES, :], out[b][0:LAST, :]).then_inc(stored[b], 16)
                        else:
                            sp.dma_start(output[rows(t), :], out[b][:]).then_inc(stored[b], 16)
                    else:
                        sp.dma_start(target[rows(t), :], out[b][:]).then_inc(stored[b], 16)
                        sp.dma_start(normed_out[rows(t), :], hn[b][:]).then_inc(stored[b], 16)

                load(0, 0)
                load(1, 1)
                with sp.Fori(0, NT // 2 - 1) as k:
                    store(k * 2, 0)
                    load(k * 2 + 2, 0)
                    store(k * 2 + 1, 1)
                    load(k * 2 + 3, 1)
                store(NT - 3, 0)
                load(NT - 1, 0)
                store(NT - 2, 1)
                store(NT - 1, 0)
                for b in range(2):
                    sp.wait_ge(stored[b], 16 * stores * uses(b))

            @block.gpsimd
            def _(pool):
                for t in range(NT):
                    b = t % 2
                    if t >= 2:
                        pool.wait_ge(taken, t - 1)
                    for c in range(2):
                        pool.indirect_dma_start(y[b][c][:], None, dr.slots,
                                                bass.IndirectOffsetOnAxis(ap=plan.slot[c][:, t:t + 1], axis=0)).then_inc(got[b], 16)

            @block.scalar
            def _(act):
                def step(k, b):
                    t = k * 2 + b
                    act.wait_ge(var_ready, t + 1)
                    nc.scalar.activation(small[:, 9:10], small[:, 8:9], ACT.Sqrt).then_inc(std_ready, 1)
                    if not final:
                        act.wait_ge(ready, t + 1)
                        nc.scalar.copy(parts[:, bass.ds(t, 1), 0:D].rearrange("p a d -> p (a d)"), hn[b][:]).then_inc(hi_ready, 1)
                        act.wait_ge(rest_ready, t + 1)
                        nc.scalar.activation(parts[:, bass.ds(t, 1), D:2 * D].rearrange("p a d -> p (a d)"), rest[b][:],
                                             ACT.Copy, scale=LO_SCALE).then_inc(lo_ready, 1)

                tile_loop(act, step)

            @block.vector
            def _(dve):
                if final:
                    dve.wait_ge(w_loaded, 32)

                def step(k, b):
                    t = k * 2 + b
                    dve.wait_ge(got[b], k * 32 + 32)
                    nc.vector.tensor_scalar(mixed[b][:], y[b][0][:], plan.weight[0][:, bass.ds(t, 1)], None, ALU.mult)
                    dve.drain()
                    nc.vector.scalar_tensor_tensor(mixed[b][:], y[b][1][:], plan.weight[1][:, bass.ds(t, 1)], mixed[b][:],
                                                   ALU.mult, ALU.add).then_inc(taken, 1)
                    dve.drain()
                    dve.wait_ge(loaded[b], k * 16 + 16)
                    if not at_start(k):
                        dve.wait_ge(stored[b], k * (16 * stores))
                    if final:
                        nc.vector.tensor_tensor(mixed[b][:], mixed[b][:], tokens[:, bass.ds(t, 1), :].rearrange(
                            "p a d -> p (a d)"), ALU.add)
                        dve.drain()
                        normalize(nc, dve, mixed[b][:], mixed[b][:], small, var_ready, std_ready, t + 1)
                        dve.drain()
                        nc.vector.tensor_tensor(mixed[b][:], mixed[b][:], scale[:], ALU.mult)
                        dve.drain()
                        nc.vector.tensor_tensor(mixed[b][:], mixed[b][:], shift[:], ALU.add)
                        dve.drain()
                        nc.vector.tensor_tensor(out[b][:], mixed[b][:], x[b][:], ALU.add).then_inc(ready, 1)
                    else:
                        nc.vector.tensor_tensor(out[b][:], mixed[b][:], x[b][:], ALU.add)
                        dve.drain()
                        normalize(nc, dve, hn[b][:], out[b][:], small, var_ready, std_ready, t + 1).then_inc(ready, 1)
                        dve.wait_ge(hi_ready, t + 1)
                        if not at_start(k):
                            dve.wait_ge(lo_ready, t - 1)
                        nc.vector.tensor_tensor(rest[b][:], hn[b][:], parts[:, bass.ds(t, 1), 0:D].rearrange(
                            "p a d -> p (a d)"), ALU.subtract).then_inc(rest_ready, 1)

                tile_loop(dve, step)


def gru(nc, ins, cst, dr, sums, states, source, target):
    G = 3 * D
    with ExitStack() as ctx:
        sb = lambda n, s, d=F32: ctx.enter_context(nc.sbuf_tensor("gru_" + n, s, d))
        sem = ctx.enter_context(semaphores(nc, "gru_"))
        pb = lambda n, s: ctx.enter_context(nc.psum_tensor("gru_" + n, s, F32))
        w_rows = sb("w_rows", [P, 2, G // P, D])
        wT = sb("wT", [P, 2, KD, G])
        bias = sb("bias", [P, 2, G])
        both = sb("both", [P, 2 * D])
        x = [[sb(f"x{b}_{i}", [P, D]) for i in range(2)] for b in range(2)]
        before = [sb(f"before{b}", [P, D]) for b in range(2)]
        xT = [sb(f"xT{b}", [P, 2, KD, P]) for b in range(2)]
        pre = [sb(f"pre{b}", [P, 2 * D]) for b in range(2)]
        gate = [sb(f"gate{b}", [P, 2 * D]) for b in range(2)]
        hidden = [sb(f"hidden{b}", [P, D]) for b in range(2)]
        cand = [sb(f"cand{b}", [P, D]) for b in range(2)]
        new = [sb(f"new{b}", [P, D]) for b in range(2)]
        out = [sb(f"out{b}", [P, D]) for b in range(2)]
        ps_t = [pb(f"ps_t{b}", [P, 2, KD, P]) for b in range(2)]
        ps_g = [pb(f"ps_g{b}", [P, 2 * D]) for b in range(2)]
        ps_n = [pb(f"ps_n{b}", [P, 2, D]) for b in range(2)]
        w_loaded, w_turned, w_ready = sem("w_loaded"), sem("w_turned"), sem("w_ready")
        loaded = [sem(f"loaded{b}") for b in range(2)]
        stored = [sem(f"stored{b}") for b in range(2)]
        turned, xT_ready, product = sem("turned"), sem("xT_ready"), sem("product")
        pre_ready, gate_ready, cand_ready, new_ready, ready = (sem("pre_ready"), sem("gate_ready"), sem("cand_ready"),
                                                              sem("new_ready"), sem("ready"))
        GC = G // P

        with nc.Block() as block:

            @block.sync
            def _(sp):
                for i, n in enumerate(("L1_gnn_w_ih", "L1_gnn_w_hh")):
                    sp.dma_start(w_rows[:, i], ins[n].rearrange("(g p) d -> p g d", p=P)).then_inc(w_loaded, 16)
                for i, n in enumerate(("L1_gnn_b_ih", "L1_gnn_b_hh")):
                    sp.dma_start(bias[:, i], ins[n].partition_broadcast(P)).then_inc(w_loaded, 16)

                def step(k, b):
                    t = k * 2 + b
                    if not at_start(k):
                        sp.wait_ge(ready, t - 1)
                    sp.dma_start(x[b][0][:], sums[rows(t), :]).then_inc(loaded[b], 16)
                    sp.dma_start(x[b][1][:], states[rows(t), :]).then_inc(loaded[b], 16)
                    sp.dma_start(before[b][:], source[rows(t), :]).then_inc(loaded[b], 16)

                tile_loop(sp, step)

            @block.tensor
            def _(pe):
                pe.wait_ge(w_loaded, 64)
                n = 0
                for i in range(2):
                    for g in range(GC):
                        if n >= 2:
                            pe.wait_ge(w_ready, n - 1)
                        for c in range(KD):
                            last = nc.tensor.transpose(ps_t[n % 2][:, 0, c, :], w_rows[:, i, g, c * P:(c + 1) * P], cst.ident[:])
                        last.then_inc(w_turned, 1)
                        n += 1
                pe.wait_ge(w_ready, 2 * GC)

                def step(k, b):
                    t = k * 2 + b
                    pe.wait_ge(loaded[b], k * 48 + 48)
                    for i in range(2):
                        for c in range(KD):
                            last = nc.tensor.transpose(ps_t[b][:, i, c, :], x[b][i][:, c * P:(c + 1) * P], cst.ident[:])
                    last.then_inc(turned, 1)
                    pe.wait_ge(xT_ready, t + 1)
                    if not at_start(k):
                        pe.wait_ge(cand_ready, t - 1)
                    for i in range(2):
                        for c in range(KD):
                            nc.tensor.matmul(ps_g[b][:], xT[b][:, i, c, :], wT[:, i, c, 0:2 * D],
                                             start=i == 0 and c == 0, stop=i == 1 and c == KD - 1)
                    for i in range(2):
                        for c in range(KD):
                            last = nc.tensor.matmul(ps_n[b][:, i, :], xT[b][:, i, c, :], wT[:, i, c, 2 * D:G],
                                                    start=c == 0, stop=c == KD - 1)
                    last.then_inc(product, 1)

                tile_loop(pe, step)

            @block.scalar
            def _(act):
                n = 0
                for i in range(2):
                    for g in range(GC):
                        act.wait_ge(w_turned, n + 1)
                        nc.scalar.copy(wT[:, i, :, g * P:(g + 1) * P], ps_t[n % 2][:, 0]).then_inc(w_ready, 1)
                        n += 1

                def step(k, b):
                    t = k * 2 + b
                    act.wait_ge(turned, t + 1)
                    nc.scalar.copy(xT[b][:], ps_t[b][:]).then_inc(xT_ready, 1)
                    act.wait_ge(pre_ready, t + 1)
                    nc.scalar.activation(gate[b][:], pre[b][:], ACT.Sigmoid).then_inc(gate_ready, 1)
                    act.wait_ge(cand_ready, t + 1)
                    nc.scalar.activation(new[b][:], cand[b][:], ACT.Tanh).then_inc(new_ready, 1)

                tile_loop(act, step)

            @block.vector
            def _(dve):
                dve.wait_ge(w_loaded, 64)
                nc.vector.tensor_tensor(both[:], bias[:, 0, 0:2 * D], bias[:, 1, 0:2 * D], ALU.add)
                dve.drain()

                def step(k, b):
                    t = k * 2 + b
                    dve.wait_ge(product, t + 1)
                    nc.vector.tensor_tensor(pre[b][:], ps_g[b][:], both[:], ALU.add).then_inc(pre_ready, 1)
                    nc.vector.tensor_tensor(hidden[b][:], ps_n[b][:, 1, :], bias[:, 1, 2 * D:G], ALU.add)
                    nc.vector.tensor_tensor(cand[b][:], ps_n[b][:, 0, :], bias[:, 0, 2 * D:G], ALU.add)
                    dve.drain()
                    dve.wait_ge(gate_ready, t + 1)
                    nc.vector.tensor_tensor(hidden[b][:], hidden[b][:], gate[b][:, 0:D], ALU.mult)
                    dve.drain()
                    nc.vector.tensor_tensor(cand[b][:], cand[b][:], hidden[b][:], ALU.add).then_inc(cand_ready, 1)
                    dve.wait_ge(new_ready, t + 1)
                    nc.vector.tensor_tensor(hidden[b][:], x[b][1][:], new[b][:], ALU.subtract)
                    dve.drain()
                    nc.vector.tensor_tensor(hidden[b][:], hidden[b][:], gate[b][:, D:2 * D], ALU.mult)
                    nc.vector.tensor_tensor(cand[b][:], new[b][:], before[b][:], ALU.add)
                    dve.drain()
                    if not at_start(k):
                        dve.wait_ge(stored[b], k * 16)
                    nc.vector.tensor_tensor(out[b][:], hidden[b][:], cand[b][:], ALU.add).then_inc(ready, 1)

                tile_loop(dve, step)

            @block.gpsimd
            def _(pool):
                def step(k, b):
                    t = k * 2 + b
                    pool.wait_ge(ready, t + 1)
                    pool.dma_start(target[rows(t), :], out[b][:]).then_inc(stored[b], 16)

                tile_loop(pool, step)
                for b in range(2):
                    pool.wait_ge(stored[b], 16 * uses(b))


def four_blocks(nc, ins, out):
    scratch = lambda n, r, c=D: nc.dram_tensor(n, [r, c], F32, kind="Internal").ap()
    dr = Scratch()
    dr.x0, dr.x1, dr.x2, dr.x3 = (scratch(f"x{i}", NP) for i in range(4))
    dr.h1, dr.h2 = scratch("h1", NP), scratch("h2", NP)
    dr.own, dr.hn, dr.red = scratch("own", NP), scratch("hn", NP), scratch("red", NP)
    dr.slots = scratch("slots", (max_tiles(16) + 1) * P)
    with ExitStack() as ctx:
        sb = lambda n, s, d=F32: ctx.enter_context(nc.sbuf_tensor(n, s, d))
        cst = Resident()
        cst.ident, cst.ones, cst.before = sb("ident", [P, P]), sb("ones", [P, P]), sb("before", [P, P])
        cst.lo_scale = sb("lo_scale", [P, D])
        with ExitStack() as graph:
            gb = lambda n, s, d=F32: graph.enter_context(nc.sbuf_tensor(n, s, d))
            cst.counts = gb("counts", [P, NT, NT, P], F16)
            cst.rel_count = gb("rel_count", [P, NT, N_REL + 1])
            cst.inv_deg = gb("inv_deg", [P, NT])
            with ExitStack() as edges:
                eb = lambda n, s, d=F32: edges.enter_context(nc.sbuf_tensor(n, s, d))
                cst.edge = eb("edge", [P, 3, EG * P])
                cst.node_of = eb("node_of", [P, NP], F16)
                cst.ranges = eb("ranges", [3, TT], I32)
                index_edges(nc, ins, cst, dr)
                build_counts(nc, ins, cst, dr)
            with nc.sbuf_tensor("parts", [P, NT, 2 * D], F16) as parts:
                sources, targets = (dr.x0, dr.h1, dr.h2), (dr.h1, dr.h2, dr.x1)
                for layer in range(LAYERS):
                    project(nc, ins, cst, dr, layer, sources[layer], parts)
                    last = layer == LAYERS - 1
                    aggregate(nc, ins, cst, dr, f"agg{layer}_", parts, targets[layer], relu=not last,
                              residual=dr.x0 if last else None)

            def plan_for(stack, tag, experts):
                pb = lambda n, s, d=F32: stack.enter_context(nc.sbuf_tensor(tag + n, s, d))
                plan = Plan()
                plan.weight = [pb(f"weight{c}", [P, NT]) for c in range(2)]
                plan.slot = [pb(f"slot{c}", [P, NT], I32) for c in range(2)]
                plan.starts, plan.ends = pb("starts", [1, experts], I32), pb("ends", [1, experts], I32)
                return plan

            E0 = ins["L0_ffn_Wr"].shape[1]
            with ExitStack() as mix:
                plan = plan_for(mix, "mix0_", E0)
                with nc.sbuf_tensor("tokens0", [P, NT, D], F32) as tokens:
                    route(nc, cst, dr, "route0_", dr.x1, E0, ins["L0_ffn_Wr"], ins["L0_ffn_br"],
                          ins["L0_ffn_gamma"], ins["L0_ffn_beta"], tokens, plan)
                run_experts(nc, cst, dr, "experts0_", E0, ins["L0_ffn_W1"], ins["L0_ffn_b1"], ins["L0_ffn_W2"],
                            ins["L0_ffn_b2"], ACT.Gelu, plan)
                with nc.sbuf_tensor("parts_rel", [P, NT, 2 * D], F16) as parts:
                    combine(nc, cst, dr, "combine0_", plan, dr.x1, dr.x2, parts=parts, normed_out=dr.hn)
                    aggregate(nc, ins, cst, dr, "agg_rel_", parts, dr.red, relations=True)
        gru(nc, ins, cst, dr, dr.red, dr.hn, dr.x2, dr.x3)
        E1 = ins["L1_ffn_gate_w"].shape[1]
        with ExitStack() as mix:
            plan = plan_for(mix, "mix1_", E1)
            tokens = mix.enter_context(nc.sbuf_tensor("tokens1", [P, NT, D], F32))
            route(nc, cst, dr, "route1_", dr.x3, E1, ins["L1_ffn_gate_w"], ins["L1_ffn_gate_b"], None, None, tokens, plan)
            run_experts(nc, cst, dr, "experts1_", E1, ins["L1_ffn_w1"], ins["L1_ffn_b1"], ins["L1_ffn_w2"],
                        ins["L1_ffn_b2"], ACT.Relu, plan)
            combine(nc, cst, dr, "combine1_", plan, dr.x3, None, tokens=tokens, gamma=ins["L1_ffn_gamma"],
                    beta=ins["L1_ffn_beta"], output=out)


_OUTPUT = "blocks_out"


def kernel(**inputs):
    from concourse import bacc
    from concourse.bass_utils import run_bass_kernel_spmd

    nc = bacc.Bacc("TRN2", target_bir_lowering=False, num_devices=1)
    arrays, ins = {}, {}
    for name, value in inputs.items():
        a = np.ascontiguousarray(value)
        arrays[f"in_{name}"] = a
        ins[name] = nc.dram_tensor(f"in_{name}", a.shape, mybir.dt.from_np(a.dtype), kind="ExternalInput").ap()
    out = nc.dram_tensor(_OUTPUT, (N_NODES, D), F32, kind="ExternalOutput").ap()
    four_blocks(nc, ins, out)
    ran = run_bass_kernel_spmd(nc, [arrays], core_ids=[0])
    return ran.results[0][_OUTPUT]
```

```python
from contextlib import ExitStack, contextmanager

import numpy as np

import concourse.bass as bass
from concourse import mybir

F32 = mybir.dt.float32
F16 = mybir.dt.float16
I32 = mybir.dt.int32
ALU = mybir.AluOpType
ACT = mybir.ActivationFunctionType
AX = mybir.AxisListType

P = 128
N_NODES = 3125
D = 256
KD = D // P
N_EDGES = 50000
N_REL = 16
NT = -(-N_NODES // P)
NP = NT * P
LAST = N_NODES - (NT - 1) * P
ET = -(-N_EDGES // P)
EG = 4
FULL_ET = N_EDGES // P
EDGE_TAIL = N_EDGES - FULL_ET * P
WIN = 32
WT = P // WIN
NW = NP // WIN
GROUP = 6
REST_BITS = 0
REST = 1 << REST_BITS
NOWHERE = 4000
HID = 512
KH = HID // P
LAYERS = 3
EPS = 1e-5
LO_SCALE = 2048.0
BANK = 512


class Scratch:
    pass


class Resident:
    pass


class Plan:
    pass


def max_tiles(experts):
    return 2 * NP // P + experts


@contextmanager
def semaphores(nc, tag):
    held = []

    def sem(name):
        held.append(nc.alloc_semaphore(tag + name))
        return held[-1]

    yield sem
    nc.clear_and_free_semaphores(held)
    nc.all_engine_barrier()


def at_start(k):
    return isinstance(k, int) and k == 0


def tile_loop(engine, step, n=2, ahead=0, behind=0):
    first = max(1, -(-behind // n))
    whole = (NT - ahead) // n
    for t in range(first * n):
        step(t // n, t % n)
    with engine.Fori(first, whole) as k:
        for b in range(n):
            step(k, b)
    for t in range(whole * n, NT):
        step(t // n, t % n)


def past(t):
    return isinstance(t, int) and t >= NT


def early(t):
    return isinstance(t, int) and t < 0


def rows(t):
    return bass.ds(t * P, P)


def tile_of(a, t):
    return a[:, bass.ds(t, 1), :].rearrange("p a d -> p (a d)")


def uses(b, n=2):
    return (NT - b + n - 1) // n


def index_edges(nc, ins, cst, dr):
    with ExitStack() as ctx:
        sb = lambda n, s, d=F32: ctx.enter_context(nc.sbuf_tensor(n, s, d))
        sem = ctx.enter_context(semaphores(nc, "edge_"))
        free = cst.counts[:].rearrange("p t s n -> p (t s n)").bitcast(I32)
        words = EG * P
        columns = lambda first, n: free[:, first * words:(first + n) * words].rearrange("p (a g e) -> p a g e", a=n, g=EG)
        raw, part, val = columns(0, 3), columns(3, 4), columns(7, 4).bitcast(F32)
        low = sb("dst_low", [P, EG])
        high = sb("dst_high", [P, EG])
        diag = columns(11, 2).bitcast(F32)
        number = sb("range_number", [P, EG * P])
        first_node = sb("first_node", [P, 1])
        last_node = sb("last_node", [P, 1])
        inside = sb("range_inside", [P, EG * P])
        key = sb("range_key", [P, EG * P])
        after = sb("range_after", [P, 1])
        left = sb("range_left", [P, 1])
        left_i = sb("range_left_i", [P, 1], I32)
        beyond = sb("range_beyond", [P, 1])
        table = sb("range_table", [P, 3, P])
        col = sb("range_col", [P, 3])
        ps_edges = ctx.enter_context(nc.psum_tensor("ps_edges", [P, 4, EG * P], F32))
        ps_low = ctx.enter_context(nc.psum_tensor("ps_low", [P, EG * P], F32))
        ps_high = ctx.enter_context(nc.psum_tensor("ps_high", [P, EG * P], F32))
        ps_before = ctx.enter_context(nc.psum_tensor("ps_before", [P, BANK], F32))
        ps_tab = ctx.enter_context(nc.psum_tensor("ps_tab", [P, BANK], F32))

        padded, loaded, consts = sem("padded"), sem("loaded"), sem("consts")
        valued, ranged = sem("valued"), sem("ranged")
        turned, spread, counted = sem("turned"), sem("spread"), sem("counted")
        summed, tabled, turned_tab = sem("summed"), sem("tabled"), sem("turned_tab")
        names = ("src", "dst", "edge_type_16")
        FG = FULL_ET // P
        LEFT = FULL_ET - FG * P

        with nc.Block() as block:

            @block.sync
            def _(sp):
                sp.wait_ge(padded, 1)
                for a, n in enumerate(names):
                    sp.dma_start(raw[:, a, 0:FG, :], ins[n][0:FG * P * P].rearrange(
                        "(g p e) -> p g e", g=FG, p=P)).then_inc(loaded, 16)
                    sp.dma_start(raw[0:LEFT, a, FG, :], ins[n][FG * P * P:FULL_ET * P].rearrange(
                        "(p e) -> p e", e=P)).then_inc(loaded, 16)
                    sp.dma_start(raw[LEFT:LEFT + 1, a, FG, 0:EDGE_TAIL], ins[n][FULL_ET * P:N_EDGES].rearrange(
                        "(p e) -> p e", p=1)).then_inc(loaded, 16)

            @block.gpsimd
            def _(pool):
                iota = lambda out, pattern, base, step: nc.gpsimd.iota(
                    out, pattern, base=base, channel_multiplier=step, allow_small_or_imprecise_dtypes=True)
                nc.gpsimd.memset(raw[:, :, FG, :], NOWHERE).then_inc(padded, 1)
                nc.gpsimd.memset(cst.ident[:], 0.0)
                nc.gpsimd.memset(cst.ones[:], 1.0)
                nc.gpsimd.memset(cst.before[:], 1.0)
                nc.gpsimd.memset(cst.lo_scale[:], LO_SCALE)
                nc.gpsimd.memset(cst.eps[:], EPS)
                nc.gpsimd.memset(cst.base[:], 0.0)
                nc.gpsimd.memset(cst.win_node[:], -2.0 * NOWHERE)
                pool.drain()
                nc.gpsimd.affine_select(out=cst.ident[:], in_=cst.ident[:], compare_op=ALU.not_equal, fill=1.0,
                                        base=0, pattern=[[-1, P]], channel_multiplier=1)
                nc.gpsimd.affine_select(out=cst.before[:], in_=cst.before[:], compare_op=ALU.is_gt, fill=0.0,
                                        base=0, pattern=[[1, P]], channel_multiplier=-1)
                iota(cst.place_no[:], [[1, NT * WIN]], 0, 0)
                iota(cst.row_no[:], [[1, P]], 0, 0)
                iota(cst.rel_no[:], [[1, N_REL]], 0, 0)
                iota(cst.base[:, :, 0], [[P, NW]], 0, 0)
                iota(cst.base[:, :, 2], [[WIN, NW]], 0, 0)
                for q in range(WT):
                    iota(cst.win_node[:, q, q * WIN:(q + 1) * WIN], [[1, WIN]], 0, 0)
                iota(number[:], [[1, EG * P]], 0, 0)
                iota(first_node[:], [[0, 1]], 0, WIN)
                iota(last_node[:], [[0, 1]], WIN - 1, WIN).then_inc(consts, 1)

            @block.vector
            def _(dve):
                dve.wait_ge(loaded, 16 * 9)
                bits, wbits = P.bit_length() - 1, WIN.bit_length() - 1
                shift = (ALU.logical_shift_right, ALU.logical_shift_left)
                nc.vector.tensor_copy(val[:, 2], raw[:, 1])
                nc.vector.tensor_scalar(part[:, 0], raw[:, 0], P - 1, None, ALU.bitwise_and)
                nc.vector.tensor_scalar(part[:, 1], raw[:, 1], wbits, bits, *shift)
                nc.vector.tensor_scalar(part[:, 2], raw[:, 0], bits, wbits, *shift)
                nc.vector.tensor_scalar(part[:, 3], raw[:, 1], WIN - 1, None, ALU.bitwise_and)
                nc.vector.tensor_copy(val[:, 3], raw[:, 2])
                dve.drain()
                nc.vector.tensor_tensor(val[:, 0], part[:, 0], part[:, 1], ALU.add)
                nc.vector.tensor_tensor(val[:, 1], part[:, 2], part[:, 3], ALU.add).then_inc(valued, 1)
                nc.vector.tensor_reduce(low[:], val[:, 2], AX.X, ALU.min)
                nc.vector.tensor_reduce(high[:], val[:, 2], AX.X, ALU.max)
                dve.drain()
                dve.wait_ge(consts, 1)
                for side, v in enumerate((low, high)):
                    for g in range(EG):
                        last = nc.vector.tensor_scalar(diag[:, side, g, :], cst.ident[:], v[:, g:g + 1], None, ALU.mult)
                last.then_inc(ranged, 1)
                dve.wait_ge(turned, 1)
                nc.vector.tensor_copy(cst.edge[:], ps_edges[:])
                dve.wait_ge(spread, 1)
                nc.vector.tensor_scalar(key[:], ps_high[:], first_node[:, 0:1], None, ALU.is_ge)
                dve.drain()
                nc.vector.scalar_tensor_tensor(inside[:], ps_low[:], last_node[:, 0:1], key[:], ALU.is_le, ALU.mult)
                dve.drain()
                nc.vector.scalar_tensor_tensor(key[:], inside[:], -1000.0, number[:], ALU.mult, ALU.add)
                dve.drain()
                nc.vector.tensor_reduce(left[:], key[:], AX.X, ALU.min)
                dve.drain()
                nc.vector.tensor_scalar(col[:, 0:1], left[:], 1000.0, float(ET - 1), ALU.add, ALU.min)
                nc.vector.scalar_tensor_tensor(key[:], number[:], 1.0, inside[:], ALU.add, ALU.mult)
                dve.drain()
                nc.vector.tensor_reduce(after[:], key[:], AX.X, ALU.max)
                dve.drain()
                nc.vector.scalar_tensor_tensor(left[:], col[:, 0:1], -1.0, after[:], ALU.mult, ALU.add)
                dve.drain()
                nc.vector.tensor_scalar(left_i[:], left[:], float(REST - 1 - GROUP), None, ALU.add)
                dve.drain()
                nc.vector.tensor_scalar(left_i[:], left_i[:], REST_BITS, None, ALU.arith_shift_right)
                dve.drain()
                nc.vector.tensor_scalar(beyond[:], left_i[:], 0.0, None, ALU.max).then_inc(counted, 1)
                dve.wait_ge(summed, 1)
                nc.vector.tensor_copy(col[:, 1:2], ps_before[:, 0:1])
                nc.vector.tensor_tensor(col[:, 2:3], ps_before[:, 0:1], beyond[:], ALU.add)
                dve.drain()
                for c in range(3):
                    last = nc.vector.tensor_scalar(table[:, c, :], cst.ident[:], col[:, c:c + 1], None, ALU.mult)
                last.then_inc(tabled, 1)
                dve.wait_ge(turned_tab, 1)
                rows_of = ps_tab[0:1, 0:3 * P].rearrange("p (c w) -> p w c", c=3)
                nc.vector.tensor_copy(cst.ranges[:], rows_of)
                nc.vector.tensor_copy(cst.upto[:], ps_tab[0:1, 2 * P:2 * P + NW])

            @block.tensor
            def _(pe):
                pe.wait_ge(consts, 1)
                pe.wait_ge(valued, 1)
                for a in range(4):
                    for g in range(EG):
                        last = nc.tensor.transpose(ps_edges[:, a, g * P:(g + 1) * P], val[:, a, g, :], cst.ident[:])
                last.then_inc(turned, 1)
                pe.wait_ge(ranged, 1)
                for side, ps in enumerate((ps_low, ps_high)):
                    for g in range(EG):
                        last = nc.tensor.matmul(ps[:, g * P:(g + 1) * P], cst.ones[:], diag[:, side, g, :],
                                                start=True, stop=True)
                last.then_inc(spread, 1)
                pe.wait_ge(counted, 1)
                nc.tensor.matmul(ps_before[:, 0:1], cst.before[:], beyond[:], start=True, stop=True).then_inc(summed, 1)
                pe.wait_ge(tabled, 1)
                nc.tensor.matmul(ps_tab[:, 0:3 * P], cst.ones[:], table[:].rearrange("p c w -> p (c w)"),
                                 start=True, stop=True).then_inc(turned_tab, 1)


def build_counts(nc, ins, cst, dr):
    with ExitStack() as ctx:
        sb = lambda n, s, d=F32: ctx.enter_context(nc.sbuf_tensor(n, s, d))
        sem = ctx.enter_context(semaphores(nc, "graph_"))
        PLACES = NT * WIN
        keys = [sb(f"keys{b}", [P, 4, GROUP]) for b in range(2)]
        is_place = [sb(f"is_place{b}", [P, GROUP, PLACES], F16) for b in range(2)]
        is_row = [sb(f"is_row{b}", [P, GROUP, P], F16) for b in range(2)]
        is_node = [sb(f"is_node{b}", [P, GROUP, WIN], F16) for b in range(2)]
        is_rel = [sb(f"is_rel{b}", [P, GROUP, N_REL + 1], F16) for b in range(2)]
        is_tile_node = sb("is_tile_node", [P, REST, P], F16)
        nodes = sb("nodes", [P, P])
        part_no, passed = sb("part_no", [1, 1]), sb("passed", [1, NW])
        at_window, at_window_i = sb("at_window", [1, 1]), sb("at_window_i", [1, 1], I32)
        zeros = sb("zeros", [P, D])
        degree = sb("degree", [P, NT])
        some = sb("degree_some", [P, NT])
        acc = [[ctx.enter_context(nc.psum_tensor(f"ps_counts{b}_{i}", [P, BANK], F32)) for i in range(2)] for b in range(2)]
        acc_rel = [ctx.enter_context(nc.psum_tensor(f"ps_rel{b}", [P, BANK], F32)) for b in range(2)]
        SPLIT = ((0, BANK), (BANK, PLACES))
        MOVES = len(SPLIT) + 1
        keyed, hot, spent, moved = sem("keyed"), sem("hot"), sem("spent"), sem("moved")
        picked, part_keyed, part_hot, part_spent, part_added = (sem("picked"), sem("part_keyed"), sem("part_hot"),
                                                                sem("part_spent"), sem("part_added"))
        part_begun, part_copied = sem("part_begun"), sem("part_copied")
        part_counts, part_rel = sb("part_counts", [P, PLACES]), sb("part_rel", [P, N_REL + 1])
        zeroed, filled = sem("zeroed"), sem("filled")
        known = "the table is made on the chip"
        MOST = NW * (ET // REST)

        def windows(engine, step):
            with engine.Fori(0, NT) as t:
                for q in range(WT):
                    step(t * WT + q, q, q % 2, t)

        def one_hot(b, tiles):
            for g in range(tiles):
                nc.vector.tensor_scalar(is_place[b][:, g, :], cst.place_no[:], keys[b][:, 1, g:g + 1], None, ALU.is_equal)
            wide = lambda k, n: keys[b][:, k, 0:tiles].unsqueeze(2).to_broadcast([P, tiles, n])
            all_tiles = lambda a, n: a.unsqueeze(1).to_broadcast([P, tiles, n])
            nc.vector.tensor_tensor(is_row[b][:, 0:tiles, :], all_tiles(cst.row_no[:], P), wide(0, P), ALU.is_equal)
            nc.vector.tensor_tensor(is_rel[b][:, 0:tiles, 0:N_REL], all_tiles(cst.rel_no[:], N_REL), wide(3, N_REL),
                                    ALU.is_equal)
            return wide, all_tiles

        def count(b, tiles):
            for g in range(tiles):
                for i, (lo, hi) in enumerate(SPLIT):
                    nc.tensor.matmul(acc[b][i][:, 0:hi - lo], is_row[b][:, g, :], is_place[b][:, g, lo:hi],
                                     start=g == 0, stop=g == tiles - 1, skip_group_check=True)

        with nc.Block() as block:

            @block.sync
            def _(sp):
                sp.wait_ge(zeroed, 1)
                sp.dma_start(dr.x0[0:N_NODES, :], ins["x"]).then_inc(filled, 16)
                sp.dma_start(dr.x0[N_NODES:NP, :], zeros[0:NP - N_NODES, :]).then_inc(filled, 16)
                with sp.Fori(0, dr.slots.shape[0] // P) as q:
                    sp.dma_start(dr.slots[rows(q), :], zeros[:]).then_inc(filled, 16)
                sp.wait_ge(filled, 16 * (2 + dr.slots.shape[0] // P))

            @block.gpsimd
            def _(pool):
                def take(to, w, tile, tiles):
                    return nc.gpsimd.tensor_tensor(
                        to[:, :, 0:tiles], cst.edge[:, :, bass.ds(tile, tiles)],
                        cst.base[:, bass.ds(w, 1), :].rearrange("p w k -> p (w k)").unsqueeze(2).to_broadcast([P, 4, tiles]),
                        ALU.subtract)

                def step(w, q, b, t):
                    first = pool.value_load(cst.ranges[0:1, bass.ds(w, 1), 0:1].rearrange("p w c -> p (w c)"),
                                            min_val=0, max_val=ET - 1)
                    pool.wait_ge(hot, w + 1)
                    take(keys[b], w, first, GROUP).then_inc(keyed, 1)

                windows(pool, step)
                pool.wait_ge(moved, MOVES * (NW + 2))
                total = pool.value_load(cst.ranges[0:1, NW - 1, 2:3], min_val=0, max_val=MOST)
                with pool.Fori(0, nc.s_assert_within(total + 1, 1, MOST + 1, skip_runtime_bounds_check_because=known)) as i:
                    pool.wait_ge(picked, i + 1)
                    pool.sem_inc(part_begun, 1)
                    w = pool.value_load(at_window_i[0:1, 0:1], min_val=0, max_val=NW - 1)
                    t, q = w // WT, w % WT
                    _, (first, before) = nc.values_load_multi_w_load_instructions(
                        cst.ranges[0:1, bass.ds(w, 1), 0:2].rearrange("p w c -> p (w c)"), engines=[pool.engine],
                        min_val=0, max_val=MOST)
                    tile = nc.s_assert_within((i - before) * REST + first + GROUP, 0, EG * P - REST,
                                              skip_runtime_bounds_check_because=known)
                    take(keys[0], w, tile, REST)
                    nc.gpsimd.tensor_copy(nodes[:], cst.win_node[:, bass.ds(q, 1), :].rearrange(
                        "p q n -> p (q n)")).then_inc(part_keyed, 1)
                    pool.drain()
                    pool.wait_ge(part_copied, i + 1)
                    for k, (lo, hi) in enumerate(SPLIT):
                        at = cst.counts[:, bass.ds(t, 1), lo // WIN:hi // WIN, bass.ds(q * WIN, WIN)].rearrange(
                            "p a s n -> p (a s) n")
                        nc.gpsimd.tensor_tensor(at, part_counts[:, lo:hi].rearrange("p (s n) -> p s n", n=WIN), at, ALU.add)
                    at = cst.rel_count[:, bass.ds(t, 1), :].rearrange("p a r -> p (a r)")
                    nc.gpsimd.tensor_tensor(at, part_rel[:], at, ALU.add)
                    pool.drain()
                    pool.sem_inc(part_added, 1)

            @block.vector
            def _(dve):
                dve.sem_inc(hot, 2)
                nc.vector.memset(zeros[:], 0.0).then_inc(zeroed, 1)
                for b in range(2):
                    nc.vector.memset(is_rel[b][:], 1.0)
                nc.vector.memset(part_no[:], 0.0)
                dve.drain()

                def step(w, q, b, t):
                    dve.wait_ge(spent, w + 1)
                    dve.wait_ge(keyed, w + 1)
                    wide, all_tiles = one_hot(b, GROUP)
                    nc.vector.tensor_tensor(is_node[b][:], all_tiles(cst.row_no[:, 0:WIN], WIN), wide(2, WIN),
                                            ALU.is_equal).then_inc(hot, 1)

                windows(dve, step)
                total = dve.value_load(cst.ranges[0:1, NW - 1, 2:3], min_val=0, max_val=MOST)
                with dve.Fori(0, nc.s_assert_within(total + 1, 1, MOST + 1, skip_runtime_bounds_check_because=known)) as i:
                    nc.vector.tensor_scalar(passed[:], cst.upto[:], part_no[:], None, ALU.is_le)
                    dve.drain()
                    nc.vector.tensor_reduce(at_window[:], passed[:], AX.X, ALU.add)
                    nc.vector.tensor_scalar(part_no[:], part_no[:], 1.0, None, ALU.add)
                    dve.drain()
                    nc.vector.tensor_scalar(at_window_i[:], at_window[:], float(NW - 1), None, ALU.min).then_inc(picked, 1)
                    dve.wait_ge(part_keyed, i + 1)
                    wide, all_tiles = one_hot(0, REST)
                    nc.vector.tensor_tensor(is_tile_node[:], all_tiles(nodes[:], P), wide(2, P), ALU.is_equal).then_inc(part_hot, 1)
                    dve.drain()
                    dve.wait_ge(part_added, i + 1)
                nc.vector.tensor_scalar(degree[:], cst.rel_count[:, :, N_REL], 1.0, None, ALU.max)
                nc.vector.tensor_scalar(some[:], cst.rel_count[:, :, N_REL], 1.0, None, ALU.min)
                dve.drain()
                nc.vector.reciprocal(degree[:], degree[:])
                dve.drain()
                nc.vector.tensor_tensor(cst.inv_deg[:], degree[:], some[:], ALU.mult)

            @block.tensor
            def _(pe):
                pe.sem_inc(spent, 2)

                def step(w, q, b, t):
                    pe.wait_ge(hot, w + 3)
                    pe.wait_ge(moved, (w + 1) * MOVES)
                    count(b, GROUP)
                    for g in range(GROUP):
                        last = nc.tensor.matmul(acc_rel[b][q * WIN:(q + 1) * WIN, 0:N_REL + 1], is_node[b][:, g, :],
                                                is_rel[b][:, g, :], start=g == 0, stop=g == GROUP - 1, skip_group_check=True)
                    last.then_inc(spent, 1)

                windows(pe, step)
                pe.wait_ge(moved, MOVES * (NW + 2))
                total = pe.value_load(cst.ranges[0:1, NW - 1, 2:3], min_val=0, max_val=MOST)
                with pe.Fori(0, nc.s_assert_within(total + 1, 1, MOST + 1, skip_runtime_bounds_check_because=known)) as i:
                    pe.wait_ge(part_hot, i + 1)
                    count(0, REST)
                    for g in range(REST):
                        last = nc.tensor.matmul(acc_rel[0][:, 0:N_REL + 1], is_tile_node[:, g, :], is_rel[0][:, g, :],
                                                start=g == 0, stop=g == REST - 1, skip_group_check=True)
                    last.then_inc(part_spent, 1)

            @block.scalar
            def _(act):
                act.sem_inc(moved, MOVES * 2)

                def step(w, q, b, t):
                    act.wait_ge(spent, w + 3)
                    at = slice(q * WIN, (q + 1) * WIN)
                    for i, (lo, hi) in enumerate(SPLIT):
                        nc.scalar.copy(cst.counts[:, bass.ds(t, 1), lo // WIN:hi // WIN, at].rearrange("p a s n -> p (a s) n"),
                                       acc[b][i][:, 0:hi - lo].rearrange("p (s n) -> p s n", n=WIN)).then_inc(moved, 1)
                    nc.scalar.copy(cst.rel_count[at, bass.ds(t, 1), :].rearrange("p a r -> p (a r)"),
                                   acc_rel[b][at, 0:N_REL + 1]).then_inc(moved, 1)

                windows(act, step)
                total = act.value_load(cst.ranges[0:1, NW - 1, 2:3], min_val=0, max_val=MOST)
                with act.Fori(0, nc.s_assert_within(total + 1, 1, MOST + 1, skip_runtime_bounds_check_because=known)) as i:
                    act.wait_ge(part_spent, i + 1)
                    for k, (lo, hi) in enumerate(SPLIT):
                        nc.scalar.copy(part_counts[:, lo:hi], acc[0][k][:, 0:hi - lo])
                    nc.scalar.copy(part_rel[:], acc_rel[0][:, 0:N_REL + 1])
                    act.drain()
                    act.sem_inc(part_copied, 1)


def norm_stats(nc, dve, src, small, var_ready):
    nc.vector.bn_stats(small[:, 0:6], src)
    dve.drain()
    nc.vector.bn_aggr(small[:, 6:8], small[:, 0:6]).then_inc(var_ready, 1)


def norm_root(nc, cst, small):
    return nc.scalar.activation(small[:, 8:9], small[:, 7:8], ACT.Sqrt, bias=cst.eps[:])


def norm_apply(nc, dve, out, src, small):
    nc.vector.reciprocal(small[:, 9:10], small[:, 8:9])
    dve.drain()
    return nc.vector.tensor_scalar(out, src, small[:, 6:7], small[:, 9:10], ALU.subtract, ALU.mult)


def normalize(nc, dve, out, src, small, var_ready, std_ready, count):
    norm_stats(nc, dve, src, small, var_ready)
    dve.drain()
    dve.wait_ge(std_ready, count)
    return norm_apply(nc, dve, out, src, small)


def project(nc, ins, cst, dr, layer, source, parts):
    norm = layer == 0
    with ExitStack() as ctx:
        tag = f"proj{layer}_"
        sb = lambda n, s, d=F32: ctx.enter_context(nc.sbuf_tensor(tag + n, s, d))
        sem = ctx.enter_context(semaphores(nc, tag))
        weights = sb("weights", [P, KD, 2 * D])
        bias = sb("bias", [P, D])
        h = [sb(f"h{b}", [P, D]) for b in range(2)]
        hn = [sb(f"hn{b}", [P, D]) for b in range(2)] if norm else h
        hT = [sb(f"hT{b}", [P, KD, P]) for b in range(2)]
        rest = [sb(f"rest{b}", [P, D]) for b in range(2)]
        own = [sb(f"own{b}", [P, D]) for b in range(2)]
        small = [sb(f"small{b}", [P, 10]) for b in range(2)]
        ps_t = [ctx.enter_context(nc.psum_tensor(tag + f"ps_t{b}", [P, KD, P], F32)) for b in range(2)]
        ps_n, ps_o = ([ctx.enter_context(nc.psum_tensor(tag + f"{n}{b}", [P, BANK], F32)) for b in range(2)]
                      for n in ("ps_n", "ps_o"))
        w_loaded = sem("w_loaded")
        h_loaded = [sem(f"h_loaded{b}") for b in range(2)]
        stored = [sem(f"stored{b}") for b in range(2)]
        var_ready, std_ready, normed = sem("var_ready"), sem("std_ready"), sem("normed")
        turned, hT_ready, part_product, product = sem("turned"), sem("hT_ready"), sem("part_product"), sem("product")
        hi_ready, rest_ready, own_ready, lo_ready = sem("hi_ready"), sem("rest_ready"), sem("own_ready"), sem("lo_ready")

        with nc.Block() as block:

            @block.sync
            def _(sp):
                for k in range(KD):
                    sp.dma_start(weights[:, k, 0:D], ins["L0_gnn_W_self"][layer, rows(k), :]).then_inc(w_loaded, 16)
                    sp.dma_start(weights[:, k, D:2 * D], ins["L0_gnn_W_neigh"][layer, rows(k), :]).then_inc(w_loaded, 16)
                sp.dma_start(bias[:], ins["L0_gnn_bias"][layer].partition_broadcast(P)).then_inc(w_loaded, 16)

                def load(t, b):
                    sp.dma_start(h[b][:], source[rows(t), :]).then_inc(h_loaded[b], 16)

                def step(k, b):
                    t = k * 2 + b
                    if not past(t + 2):
                        sp.wait_ge(normed if norm else turned, t + 1)
                        load(t + 2, b)
                    sp.wait_ge(own_ready, t + 1)
                    sp.dma_start(dr.own[rows(t), :], own[b][:]).then_inc(stored[b], 16)

                load(0, 0)
                load(1, 1)
                tile_loop(sp, step, ahead=2)
                for b in range(2):
                    sp.wait_ge(stored[b], 16 * uses(b))

            @block.tensor
            def _(pe):
                pe.wait_ge(w_loaded, 16 * (2 * KD + 1))

                def turn(t, loads, b):
                    if norm:
                        pe.wait_ge(normed, t + 1)
                    else:
                        pe.wait_ge(h_loaded[b], loads * 16)
                    for c in range(KD):
                        last = nc.tensor.transpose(ps_t[b][:, c, :], hn[b][:, c * P:(c + 1) * P], cst.ident[:])
                    last.then_inc(turned, 1)

                def step(k, b):
                    t = k * 2 + b
                    if not past(t + 1):
                        turn(t + 1, k + 1 + b, 1 - b)
                    pe.wait_ge(hT_ready, t + 1)
                    if not at_start(k):
                        pe.wait_ge(own_ready, t - 1)
                    for ps, lo, done in ((ps_n, D, part_product), (ps_o, 0, product)):
                        for c in range(KD):
                            last = nc.tensor.matmul(ps[b][:, 0:D], hT[b][:, c, :], weights[:, c, lo:lo + D],
                                                    start=c == 0, stop=c == KD - 1)
                        last.then_inc(done, 1)

                turn(0, 1, 0)
                tile_loop(pe, step, ahead=1)

            @block.scalar
            def _(act):
                def copy_turned(t, b):
                    act.wait_ge(turned, t + 1)
                    nc.scalar.copy(hT[b][:], ps_t[b][:]).then_inc(hT_ready, 1)

                def root(t, b):
                    act.wait_ge(var_ready, t + 1)
                    norm_root(nc, cst, small[b]).then_inc(std_ready, 1)

                def step(k, b):
                    t = k * 2 + b
                    if not past(t + 1):
                        if not at_start(k):
                            act.wait_ge(product, t)
                        copy_turned(t + 1, 1 - b)
                    if norm and not past(t + 2):
                        root(t + 2, b)
                    act.wait_ge(part_product, t + 1)
                    nc.scalar.copy(tile_of(parts, t)[:, 0:D], ps_n[b][:, 0:D]).then_inc(hi_ready, 1)

                if norm:
                    root(0, 0)
                    root(1, 1)
                copy_turned(0, 0)
                tile_loop(act, step, ahead=2)

            @block.vector
            def _(dve):
                def apply(t, b):
                    dve.wait_ge(std_ready, t + 1)
                    norm_apply(nc, dve, hn[b][:], h[b][:], small[b]).then_inc(normed, 1)

                def step(k, b):
                    t = k * 2 + b
                    if norm and not past(t + 2):
                        dve.wait_ge(h_loaded[b], (k + 2) * 16)
                        norm_stats(nc, dve, h[b][:], small[b], var_ready)
                    dve.wait_ge(hi_ready, t + 1)
                    if not at_start(k):
                        dve.wait_ge(lo_ready, t - 1)
                    nc.vector.tensor_tensor(rest[b][:], ps_n[b][:, 0:D], tile_of(parts, t)[:, 0:D],
                                            ALU.subtract).then_inc(rest_ready, 1)
                    dve.wait_ge(product, t + 1)
                    if not at_start(k):
                        dve.wait_ge(stored[b], k * 16)
                    nc.vector.tensor_tensor(own[b][:], ps_o[b][:, 0:D], bias[:], ALU.add).then_inc(own_ready, 1)
                    if norm and not past(t + 2):
                        dve.wait_ge(turned, t + 1)
                        apply(t + 2, b)

                dve.wait_ge(w_loaded, 16 * (2 * KD + 1))
                if norm:
                    for b in range(2):
                        dve.wait_ge(h_loaded[b], 16)
                        norm_stats(nc, dve, h[b][:], small[b], var_ready)
                    for b in range(2):
                        apply(b, b)
                tile_loop(dve, step, ahead=2)

            @block.gpsimd
            def _(pool):
                def step(k, b):
                    t = k * 2 + b
                    pool.wait_ge(rest_ready, t + 1)
                    nc.gpsimd.tensor_tensor(parts[:, bass.ds(t, 1), D:2 * D].rearrange("p a d -> p (a d)"),
                                            rest[b][:], cst.lo_scale[:], ALU.mult).then_inc(lo_ready, 1)

                tile_loop(pool, step)


def aggregate(nc, ins, cst, dr, tag, parts, target, relu=False, residual=None, relations=False, mixture=None):
    with ExitStack() as ctx:
        sb = lambda n, s, d=F32: ctx.enter_context(nc.sbuf_tensor(tag + n, s, d))
        pair = lambda n, s, d=F32: [sb(f"{n}{b}", s, d) for b in range(2)]
        bank = lambda n, s: [ctx.enter_context(nc.psum_tensor(tag + f"{n}{b}", s, F32)) for b in range(2)]
        sem = ctx.enter_context(semaphores(nc, tag))
        own, total, out = pair("own", [P, D]), pair("total", [P, D]), pair("out", [P, D])
        ps = bank("ps", [P, 2 * D])
        loaded = [sem(f"loaded{b}") for b in range(2)]
        stored = [sem(f"stored{b}") for b in range(2)]
        summed, taken, ready = sem("summed"), sem("taken"), sem("ready")
        if relations:
            vectors = sb("vectors", [N_REL, D])
            rel_in, rel_T = pair("rel_in", [P, N_REL]), pair("rel_T", [N_REL, P])
            ps_rel = bank("ps_rel", [N_REL, BANK])
            v_loaded, rel_copied, rel_turned, rel_ready = (sem("v_loaded"), sem("rel_copied"), sem("rel_turned"),
                                                           sem("rel_ready"))
        if mixture is not None:
            E, router, router_bias, gamma, beta, logit = mixture
            before, inner, xn = pair("before", [P, D]), pair("inner", [P, D]), pair("xn", [P, D])
            xT = pair("xT", [P, KD, P])
            stats = [pair("outer_stats", [P, 10]), pair("inner_stats", [P, 10])]
            weights, bias, scale, shift = sb("router", [P, KD, E]), sb("bias", [P, E]), sb("gamma", [P, D]), sb("beta", [P, D])
            ps_t, ps_l = bank("ps_t", [P, KD, P]), bank("ps_l", [P, BANK])
            w_loaded = sem("w_loaded")
            tokens_stored = [sem(f"tokens_stored{b}") for b in range(2)]
            var_ready, std_ready = ([sem(f"{n}{i}") for i in range(2)] for n in ("var_ready", "std_ready"))
            normed, turned, xT_ready, scored, logit_ready = (sem("normed"), sem("turned"), sem("xT_ready"),
                                                             sem("scored"), sem("logit_ready"))
        per_tile = 1 + (residual is not None)
        loop = lambda engine, step: tile_loop(engine, step, ahead=2, behind=3 if mixture is not None else 0)

        with nc.Block() as block:

            @block.sync
            def _(sp):
                if relations:
                    sp.dma_start(vectors[:], ins["L1_gnn_relvectors"]).then_inc(v_loaded, 16)

                def load(t, b):
                    sp.dma_start(own[b][:], dr.own[rows(t), :]).then_inc(loaded[b], 16)
                    if residual is not None:
                        sp.dma_start(before[b][:], residual[rows(t), :]).then_inc(loaded[b], 16)

                def store_tokens(u, b):
                    sp.wait_ge(normed, u + 1)
                    sp.dma_start(dr.tokens[rows(u), :], xn[b][:]).then_inc(tokens_stored[b], 16)

                def step(k, b):
                    t = k * 2 + b
                    sp.wait_ge(taken if relations else ready, t + 1)
                    sp.dma_start(target[rows(t), :], out[b][:]).then_inc(stored[b], 16)
                    if not relations and not past(t + 2):
                        load(t + 2, b)
                    if mixture is not None and not early(t - 1):
                        store_tokens(t - 1, 1 - b)

                if not relations:
                    load(0, 0)
                    load(1, 1)
                if mixture is not None:
                    sp.dma_start(weights[:], router.rearrange("(k p) e -> p k e", p=P)).then_inc(w_loaded, 16)
                    for to, row in ((bias, router_bias), (scale, gamma), (shift, beta)):
                        sp.dma_start(to[:], row.partition_broadcast(P)).then_inc(w_loaded, 16)
                loop(sp, step)
                if mixture is not None:
                    store_tokens(NT - 1, (NT - 1) % 2)
                for b in range(2):
                    sp.wait_ge(stored[b], 16 * uses(b))
                    if mixture is not None:
                        sp.wait_ge(tokens_stored[b], 16 * uses(b))

            @block.tensor
            def _(pe):
                if relations:
                    pe.wait_ge(v_loaded, 16)
                if mixture is not None:
                    pe.wait_ge(w_loaded, 64)

                def turn(u, b):
                    pe.wait_ge(normed, u + 1)
                    for c in range(KD):
                        last = nc.tensor.transpose(ps_t[b][:, c, :], xn[b][:, c * P:(c + 1) * P], cst.ident[:])
                    last.then_inc(turned, 1)

                def score(u, b):
                    pe.wait_ge(xT_ready, u + 1)
                    pe.wait_ge(logit_ready, u + 1)
                    for c in range(KD):
                        last = nc.tensor.matmul(ps_l[b][:, 0:E], xT[b][:, c, :], weights[:, c, :],
                                                start=c == 0, stop=c == KD - 1)
                    last.then_inc(scored, 1)

                def step(k, b):
                    t = k * 2 + b
                    if relations:
                        pe.wait_ge(rel_copied, t + 1)
                        nc.tensor.transpose(ps_rel[b][:, 0:P], rel_in[b][:], cst.ident[:]).then_inc(rel_turned, 1)
                    if not at_start(k):
                        pe.wait_ge(taken, t - 1)
                    for s in range(NT):
                        last = nc.tensor.matmul(ps[b][:], cst.counts[:, bass.ds(t, 1), s, :].rearrange("p a n -> p (a n)"),
                                                parts[:, s, :], start=s == 0, stop=s == NT - 1 and not relations,
                                                skip_group_check=True)
                    if relations:
                        pe.wait_ge(rel_ready, t + 1)
                        last = nc.tensor.matmul(ps[b][:, 0:D], rel_T[b][:], vectors[:], start=False, stop=True,
                                                skip_group_check=True)
                    last.then_inc(summed, 1)
                    if mixture is not None:
                        if not early(t - 3):
                            score(t - 3, 1 - b)
                        if not early(t - 2):
                            turn(t - 2, b)

                loop(pe, step)
                if mixture is not None:
                    score(NT - 3, (NT - 3) % 2)
                    for u in (NT - 2, NT - 1):
                        turn(u, u % 2)
                        score(u, u % 2)

            @block.scalar
            def _(act):
                def copy_turned(u, b):
                    act.wait_ge(turned, u + 1)
                    nc.scalar.copy(xT[b][:], ps_t[b][:]).then_inc(xT_ready, 1)

                def step(k, b):
                    t = k * 2 + b
                    if relations:
                        if not at_start(k):
                            act.wait_ge(rel_turned, t - 1)
                        nc.scalar.copy(rel_in[b][:], tile_of(cst.rel_count, t)[:, 0:N_REL]).then_inc(rel_copied, 1)
                        act.wait_ge(rel_turned, t + 1)
                        if not at_start(k):
                            act.wait_ge(summed, t - 1)
                        nc.scalar.copy(rel_T[b][:], ps_rel[b][:, 0:P]).then_inc(rel_ready, 1)
                    else:
                        if not early(t - 2):
                            copy_turned(t - 2, b)
                        for i in range(2):
                            act.wait_ge(var_ready[i], t + 1)
                            norm_root(nc, cst, stats[i][b]).then_inc(std_ready[i], 1)

                if relations or mixture is not None:
                    loop(act, step)
                if mixture is not None:
                    for u in (NT - 2, NT - 1):
                        copy_turned(u, u % 2)

            @block.vector
            def _(dve):
                def token(u, b, stores):
                    dve.wait_ge(std_ready[1], u + 1)
                    norm_apply(nc, dve, inner[b][:], inner[b][:], stats[1][b])
                    dve.drain()
                    nc.vector.tensor_tensor(inner[b][:], inner[b][:], scale[:], ALU.mult)
                    dve.drain()
                    if not early(u - 2):
                        dve.wait_ge(turned, u - 1)
                        dve.wait_ge(tokens_stored[b], stores * 16)
                    nc.vector.tensor_tensor(xn[b][:], inner[b][:], shift[:], ALU.add).then_inc(normed, 1)

                def keep_logit(u, b):
                    dve.wait_ge(scored, u + 1)
                    nc.vector.tensor_tensor(tile_of(logit, u), ps_l[b][:, 0:E], bias[:], ALU.add).then_inc(logit_ready, 1)

                def step(k, b):
                    t = k * 2 + b
                    dve.wait_ge(summed, t + 1)
                    if not at_start(k):
                        dve.wait_ge(stored[b], k * 16)
                    nc.vector.tensor_copy(total[b][:], ps[b][:, 0:D])
                    dve.drain()
                    if relations:
                        nc.vector.scalar_tensor_tensor(out[b][:], ps[b][:, D:2 * D], 1.0 / LO_SCALE, total[b][:],
                                                       ALU.mult, ALU.add).then_inc(taken, 1)
                        return
                    nc.vector.scalar_tensor_tensor(total[b][:], ps[b][:, D:2 * D], 1.0 / LO_SCALE, total[b][:],
                                                   ALU.mult, ALU.add).then_inc(taken, 1)
                    dve.drain()
                    dve.wait_ge(loaded[b], (k + 1) * (16 * per_tile))
                    last = nc.vector.scalar_tensor_tensor(out[b][:], total[b][:], cst.inv_deg[:, bass.ds(t, 1)], own[b][:],
                                                          ALU.mult, ALU.add)
                    if relu:
                        dve.drain()
                        last = nc.vector.tensor_scalar(out[b][:], out[b][:], 0.0, None, ALU.max)
                    if residual is not None:
                        dve.drain()
                        last = nc.vector.tensor_tensor(out[b][:], out[b][:], before[b][:], ALU.add)
                    last.then_inc(ready, 1)
                    if mixture is None:
                        return
                    dve.drain()
                    norm_stats(nc, dve, out[b][:], stats[0][b], var_ready[0])
                    if not early(t - 1):
                        token(t - 1, 1 - b, k - 1 + b)
                    dve.wait_ge(std_ready[0], t + 1)
                    norm_apply(nc, dve, inner[b][:], out[b][:], stats[0][b])
                    dve.drain()
                    norm_stats(nc, dve, inner[b][:], stats[1][b], var_ready[1])
                    if not early(t - 3):
                        keep_logit(t - 3, 1 - b)

                if mixture is not None:
                    dve.sem_inc(logit_ready, 2)
                    dve.wait_ge(w_loaded, 64)
                loop(dve, step)
                if mixture is not None:
                    token(NT - 1, (NT - 1) % 2, uses((NT - 1) % 2) - 1)
                    for u in (NT - 3, NT - 2, NT - 1):
                        keep_logit(u, u % 2)


def score_rows(nc, cst, dr, tag, x, stats, E, router, router_bias, tokens, logit):
    with ExitStack() as ctx:
        sb = lambda n, s, d=F32: ctx.enter_context(nc.sbuf_tensor(tag + n, s, d))
        bank = lambda n, s: [ctx.enter_context(nc.psum_tensor(tag + f"{n}{b}", s, F32)) for b in range(2)]
        sem = ctx.enter_context(semaphores(nc, tag))
        weights, bias = sb("router", [P, KD, E]), sb("bias", [P, E])
        dev, inv = sb("dev", [P, NT]), sb("inv", [P, NT])
        xn = [sb(f"xn{b}", [P, D]) for b in range(2)]
        xT = [sb(f"xT{b}", [P, KD, P]) for b in range(2)]
        ps_t, ps_l = bank("ps_t", [P, KD, P]), bank("ps_l", [P, BANK])
        w_loaded, std_ready, normed, kept, stored = sem("w_loaded"), sem("std_ready"), sem("normed"), sem("kept"), sem("stored")
        turned, xT_ready, scored, logit_ready = sem("turned"), sem("xT_ready"), sem("scored"), sem("logit_ready")
        loop = lambda engine, step: tile_loop(engine, step, behind=2)

        with nc.Block() as block:

            @block.sync
            def _(sp):
                sp.dma_start(weights[:], router.rearrange("(k p) e -> p k e", p=P)).then_inc(w_loaded, 16)
                sp.dma_start(bias[:], router_bias.partition_broadcast(P)).then_inc(w_loaded, 16)

                def step(k, b):
                    t = k * 2 + b
                    sp.wait_ge(kept, t + 1)
                    sp.dma_start(dr.tokens[rows(t), :], tile_of(tokens, t)).then_inc(stored, 16)

                loop(sp, step)
                sp.wait_ge(stored, 16 * NT)

            @block.tensor
            def _(pe):
                pe.wait_ge(w_loaded, 32)

                def score(u, b):
                    pe.wait_ge(xT_ready, u + 1)
                    pe.wait_ge(logit_ready, u + 1)
                    for c in range(KD):
                        last = nc.tensor.matmul(ps_l[b][:, 0:E], xT[b][:, c, :], weights[:, c, :],
                                                start=c == 0, stop=c == KD - 1)
                    last.then_inc(scored, 1)

                def step(k, b):
                    t = k * 2 + b
                    pe.wait_ge(normed, t + 1)
                    for c in range(KD):
                        last = nc.tensor.transpose(ps_t[b][:, c, :], xn[b][:, c * P:(c + 1) * P], cst.ident[:])
                    last.then_inc(turned, 1)
                    if not early(t - 1):
                        score(t - 1, 1 - b)

                loop(pe, step)
                score(NT - 1, (NT - 1) % 2)

            @block.scalar
            def _(act):
                nc.scalar.activation(dev[:], stats[:, :, 1], ACT.Sqrt, bias=cst.eps[:]).then_inc(std_ready, 1)

                def step(k, b):
                    act.wait_ge(turned, k * 2 + b + 1)
                    nc.scalar.copy(xT[b][:], ps_t[b][:]).then_inc(xT_ready, 1)

                loop(act, step)

            @block.vector
            def _(dve):
                dve.sem_inc(logit_ready, 2)
                dve.wait_ge(std_ready, 1)
                nc.vector.reciprocal(inv[:], dev[:])
                dve.drain()
                dve.wait_ge(w_loaded, 32)

                def keep_logit(u, b):
                    dve.wait_ge(scored, u + 1)
                    nc.vector.tensor_tensor(tile_of(logit, u), ps_l[b][:, 0:E], bias[:], ALU.add).then_inc(logit_ready, 1)

                def step(k, b):
                    t = k * 2 + b
                    if not early(t - 2):
                        dve.wait_ge(turned, t - 1)
                        dve.wait_ge(kept, t - 1)
                    nc.vector.tensor_scalar(xn[b][:], tile_of(x, t), stats[:, bass.ds(t, 1), 0], inv[:, bass.ds(t, 1)],
                                            ALU.subtract, ALU.mult).then_inc(normed, 1)
                    if not early(t - 2):
                        keep_logit(t - 2, b)

                loop(dve, step)
                for u in (NT - 2, NT - 1):
                    keep_logit(u, u % 2)

            @block.gpsimd
            def _(pool):
                def step(k, b):
                    t = k * 2 + b
                    pool.wait_ge(normed, t + 1)
                    nc.gpsimd.tensor_copy(tile_of(tokens, t), xn[b][:]).then_inc(kept, 1)

                loop(pool, step)


def route(nc, cst, tag, E, logit, plan):
    with ExitStack() as ctx:
        sb = lambda n, s, d=F32: ctx.enter_context(nc.sbuf_tensor(tag + n, s, d))
        sem = ctx.enter_context(semaphores(nc, tag))
        pb = lambda n, s: ctx.enter_context(nc.psum_tensor(tag + n, s, F32))
        MT = plan.token.shape[1]
        BITS = P.bit_length() - 1
        expert_no = sb("expert_no", [P, NT, E])
        first_of = sb("first_of", [P, E, NT])
        top = [sb(f"top{c}", [P, NT]) for c in range(2)]
        least = sb("least", [P, NT])
        key = sb("key", [P, NT, E])
        chosen = [sb(f"chosen{c}", [P, NT, E]) for c in range(2)]
        either = sb("either", [P, NT, E])
        ratio = sb("ratio", [P, NT])
        sums = sb("sums", [P, E, NT])
        upto = sb("upto", [P, E, NT])
        tiles = sb("tiles", [P, E])
        tiles_i = sb("tiles_i", [P, E], I32)
        ends = sb("ends", [P, E])
        ones = sb("ones_e", [P, E])
        base = sb("base", [P, E])
        slot = sb("slot", [P, NT, E])
        slot_f = [sb(f"slot_f{c}", [P, NT]) for c in range(2)]
        slot_part = [[sb(f"slot_part{c}_{i}", [P, NT], I32) for i in range(2)] for c in range(2)]
        slot_at = [[sb(f"slot_at{c}_{i}", [P, NT]) for i in range(2)] for c in range(2)]
        number = sb("number", [P, P])
        lane = sb("lane", [P, 1])
        tile_no = sb("tile_no", [P, NT], F16)
        at_place = [sb(f"at_place{c}", [P, NT, P], F16) for c in range(2)]
        at_tile = [sb(f"at_tile{c}", [P, NT, MT], F16) for c in range(2)]
        token_at = [sb(f"token_at{c}", [P, NT, 2, MT], F16) for c in range(2)]
        token_tile = sb("token_tile", [P, MT])
        ps_rank, ps_sum, ps_token = pb("ps_rank", [P, BANK]), pb("ps_sum", [P, BANK]), pb("ps_token", [P, BANK])
        consts = sem("consts")
        gap_ready, exp_ready, picked, ranked, placed, tokens_known = (
            sem("gap_ready"), sem("exp_ready"), sem("picked"), sem("ranked"), sem("placed"), sem("tokens_known"))

        with nc.Block() as block:

            @block.scalar
            def _(act):
                act.wait_ge(gap_ready, 1)
                nc.scalar.activation(ratio[:], ratio[:], ACT.Exp).then_inc(exp_ready, 1)

            @block.tensor
            def _(pe):
                pe.wait_ge(picked, 1)
                flat = either[:].rearrange("p t e -> p (t e)")
                nc.tensor.matmul(ps_rank[:, 0:NT * E], cst.before[:], flat, start=True, stop=True)
                nc.tensor.matmul(ps_sum[:, 0:NT * E], cst.ones[:], flat, start=True, stop=True).then_inc(ranked, 1)
                for c in range(2):
                    pe.wait_ge(placed, c + 1)
                    for t in range(NT):
                        last = nc.tensor.matmul(ps_token[:, 0:2 * MT], at_place[c][:, t, :],
                                                token_at[c][:, t].rearrange("p i s -> p (i s)"),
                                                start=c == 0 and t == 0, stop=c == 1 and t == NT - 1, skip_group_check=True)
                last.then_inc(tokens_known, 1)

            @block.vector
            def _(dve):
                dve.wait_ge(consts, 1)
                wide = lambda a: a.unsqueeze(2).to_broadcast([P, NT, E])
                for c in range(2):
                    nc.vector.tensor_reduce(top[c][:], logit[:], AX.X, ALU.max)
                    dve.drain()
                    nc.vector.tensor_tensor(key[:], logit[:], wide(top[c][:]), ALU.is_equal)
                    dve.drain()
                    nc.vector.scalar_tensor_tensor(key[:], key[:], -100.0, expert_no[:], ALU.mult, ALU.add)
                    dve.drain()
                    nc.vector.tensor_reduce(least[:], key[:], AX.X, ALU.min)
                    dve.drain()
                    nc.vector.tensor_tensor(chosen[c][:], key[:], wide(least[:]), ALU.is_equal)
                    dve.drain()
                    if c == 0:
                        nc.vector.scalar_tensor_tensor(logit[:], chosen[c][:], -3e38, logit[:], ALU.mult, ALU.add)
                        dve.drain()
                nc.vector.tensor_tensor(either[:], chosen[0][:], chosen[1][:], ALU.add).then_inc(picked, 1)
                nc.vector.tensor_tensor(ratio[:], top[1][:], top[0][:], ALU.subtract).then_inc(gap_ready, 1)
                dve.wait_ge(ranked, 1)
                nc.vector.tensor_copy(sums[:].rearrange("p e t -> p t e"),
                                      ps_sum[:, 0:NT * E].rearrange("p (t e) -> p t e", e=E))
                dve.drain()
                nc.vector.tensor_tensor_scan(upto[:].rearrange("p e t -> p (e t)"), first_of[:].rearrange("p e t -> p (e t)"),
                                             sums[:].rearrange("p e t -> p (e t)"), 0.0, ALU.mult, ALU.add)
                dve.drain()
                nc.vector.tensor_scalar(tiles_i[:], upto[:, :, NT - 1], float(P - 1), None, ALU.add)
                dve.drain()
                nc.vector.tensor_scalar(tiles_i[:], tiles_i[:], BITS, None, ALU.arith_shift_right)
                dve.drain()
                nc.vector.tensor_scalar(tiles[:], tiles_i[:], 1.0, None, ALU.max)
                dve.drain()
                nc.vector.tensor_tensor_scan(ends[:], ones[:], tiles[:], 0.0, ALU.mult, ALU.add)
                dve.drain()
                nc.vector.tensor_copy(plan.ends[:], ends[0:1, :])
                nc.vector.tensor_tensor(base[:], ends[:], tiles[:], ALU.subtract)
                dve.drain()
                nc.vector.tensor_copy(plan.starts[:], base[0:1, :])
                nc.vector.tensor_tensor(upto[:], upto[:], sums[:], ALU.subtract)
                dve.drain()
                nc.vector.scalar_tensor_tensor(upto[:], base[:].unsqueeze(2).to_broadcast([P, E, NT]), float(P), upto[:],
                                               ALU.mult, ALU.add)
                dve.drain()
                nc.vector.tensor_tensor(slot[:], ps_rank[:, 0:NT * E].rearrange("p (t e) -> p t e", e=E),
                                        upto[:].rearrange("p e t -> p t e"), ALU.add)
                dve.drain()
                to_all = lambda a, n: a.unsqueeze(2).to_broadcast([P, NT, n])
                for c in range(2):
                    nc.vector.tensor_tensor(key[:], slot[:], chosen[c][:], ALU.mult)
                    dve.drain()
                    nc.vector.tensor_reduce(slot_f[c][:], key[:], AX.X, ALU.add)
                    dve.drain()
                    nc.vector.tensor_copy(plan.slot[c][:], slot_f[c][:])
                    dve.drain()
                    nc.vector.tensor_scalar(slot_part[c][0][:], plan.slot[c][:], P - 1, None, ALU.bitwise_and)
                    nc.vector.tensor_scalar(slot_part[c][1][:], plan.slot[c][:], BITS, None, ALU.logical_shift_right)
                    dve.drain()
                    for i in range(2):
                        nc.vector.tensor_copy(slot_at[c][i][:], slot_part[c][i][:])
                    dve.drain()
                    nc.vector.tensor_tensor(at_tile[c][:], number[:, 0:MT].unsqueeze(1).to_broadcast([P, NT, MT]),
                                            to_all(slot_at[c][1][:], MT), ALU.is_equal)
                    nc.vector.tensor_tensor(at_place[c][:], number[:].unsqueeze(1).to_broadcast([P, NT, P]),
                                            to_all(slot_at[c][0][:], P), ALU.is_equal)
                    dve.drain()
                    nc.vector.tensor_scalar(token_at[c][:, :, 0, :], at_tile[c][:], lane[:, 0:1], None, ALU.mult)
                    nc.vector.tensor_tensor(token_at[c][:, :, 1, :], at_tile[c][:], to_all(tile_no[:], MT), ALU.mult)
                    dve.drain()
                    dve.sem_inc(placed, 1)
                dve.wait_ge(exp_ready, 1)
                nc.vector.tensor_scalar(least[:], ratio[:], 1.0, None, ALU.add)
                dve.drain()
                nc.vector.reciprocal(plan.weight[0][:], least[:])
                dve.drain()
                nc.vector.tensor_tensor(plan.weight[1][:], plan.weight[0][:], ratio[:], ALU.mult)
                dve.wait_ge(tokens_known, 1)
                nc.vector.tensor_copy(token_tile[:], ps_token[:, 0:MT])
                dve.drain()
                nc.vector.scalar_tensor_tensor(plan.token[:], ps_token[:, MT:2 * MT], float(P), token_tile[:],
                                               ALU.mult, ALU.add)

            @block.gpsimd
            def _(pool):
                iota = lambda out, pattern, step: nc.gpsimd.iota(out, pattern, base=0, channel_multiplier=step,
                                                                 allow_small_or_imprecise_dtypes=True)
                iota(expert_no[:], [[0, NT], [1, E]], 0)
                iota(number[:], [[1, P]], 0)
                iota(lane[:], [[0, 1]], 1)
                iota(tile_no[:], [[1, NT]], 0)
                nc.gpsimd.memset(ones[:], 1.0)
                nc.gpsimd.memset(first_of[:], 1.0)
                pool.drain()
                nc.gpsimd.memset(first_of[:, :, 0:1], 0.0).then_inc(consts, 1)


def run_experts(nc, cst, dr, tag, experts, w1, b1, w2, b2, function, plan):
    with ExitStack() as ctx:
        sb = lambda n, s, d=F32: ctx.enter_context(nc.sbuf_tensor(tag + n, s, d))
        sem = ctx.enter_context(semaphores(nc, tag))
        pb = lambda n, s: ctx.enter_context(nc.psum_tensor(tag + n, s, F32))
        E = experts
        up = [sb(f"up{b}", [P, KD, HID]) for b in range(2)]
        down = [sb(f"down{b}", [P, KH, D]) for b in range(2)]
        b1_rows = sb("b1_rows", [E * KH, P])
        b1_col = sb("b1_col", [P, E * KH])
        b2_all = sb("b2_all", [P, E, D])
        x = sb("x", [P, D])
        index = sb("index", [P, 1], I32)
        xT = sb("xT", [P, KD, P])
        hT = sb("hT", [P, KH, P])
        y = sb("y", [P, D])
        ps_x, ps_y, ps_b = pb("ps_x", [P, KD, P]), pb("ps_y", [P, BANK]), pb("ps_b", [P, BANK])
        ps_h = [pb(f"ps_h{c}", [P, BANK]) for c in range(KH)]
        b_loaded, b1_turned, b1_ready = sem("b_loaded"), sem("b1_turned"), sem("b1_ready")
        w_loaded = [sem(f"w_loaded{b}") for b in range(2)]
        x_loaded, x_turned, xT_ready = sem("x_loaded"), sem("x_turned"), sem("xT_ready")
        h_ready, hT_ready, y_product, y_ready = sem("h_ready"), sem("hT_ready"), sem("y_product"), sem("y_ready")
        y_stored, y_free = sem("y_stored"), sem("y_free")
        most = max_tiles(E)

        def bounds(engine, e):
            return (engine.value_load(plan.starts[0:1, bass.ds(e, 1)], min_val=0, max_val=most - 1),
                    engine.value_load(plan.ends[0:1, bass.ds(e, 1)], min_val=1, max_val=most))

        def expert_loop(engine, step):
            with engine.Fori(0, E // 2) as k:
                for b in range(2):
                    step(k * 2 + b, k, b, *bounds(engine, k * 2 + b))

        with nc.Block() as block:

            @block.sync
            def _(sp):
                def load(e, b):
                    sp.dma_start(up[b][:], w1[bass.ds(e, 1)].rearrange("a (k p) h -> p (a k) h", p=P)).then_inc(w_loaded[b], 16)
                    sp.dma_start(down[b][:], w2[bass.ds(e, 1)].rearrange("a (k p) d -> p (a k) d", p=P)).then_inc(w_loaded[b], 16)

                def store_tiles(start, end):
                    with sp.Fori(start, end) as q:
                        sp.wait_ge(y_ready, q + 2)
                        sp.dma_start(dr.slots[rows(q), :], y[:]).then_inc(y_stored, 16)
                        sp.wait_ge(y_stored, (q + 1) * 16)
                        sp.sem_inc(y_free, 1)

                sp.sem_inc(y_free, 1)
                load(0, 0)
                sp.dma_start(b1_rows[:], b1.rearrange("e (k p) -> (e k) p", p=P)).then_inc(b_loaded, 16)
                sp.dma_start(b2_all[:], b2.partition_broadcast(P)).then_inc(b_loaded, 16)
                with sp.Fori(0, E // 2 - 1) as k:
                    for b in range(2):
                        load(k * 2 + (b + 1), 1 - b)
                        store_tiles(*bounds(sp, k * 2 + b))
                load(E - 1, 1)
                store_tiles(*bounds(sp, E - 2))
                store_tiles(*bounds(sp, E - 1))

            @block.gpsimd
            def _(pool):
                total = pool.value_load(plan.ends[0:1, E - 1:E], min_val=1, max_val=most)

                def gather(q):
                    nc.gpsimd.tensor_copy(index[:], plan.token[:, bass.ds(q, 1)])
                    pool.drain()
                    pool.indirect_dma_start(x[:], None, dr.tokens, bass.IndirectOffsetOnAxis(ap=index[:], axis=0)).then_inc(x_loaded, 16)

                gather(0)
                with pool.Fori(1, total + 1) as q:
                    pool.wait_ge(x_turned, q)
                    gather(q)
                pool.wait_ge(x_loaded, total * 16 + 16)

            @block.tensor
            def _(pe):
                pe.wait_ge(b_loaded, 32)
                nc.tensor.transpose(ps_b[:, 0:E * KH], b1_rows[:], cst.ident[0:E * KH, 0:E * KH]).then_inc(b1_turned, 1)

                def turn(q):
                    pe.wait_ge(x_loaded, q * 16 + 16)
                    for c in range(KD):
                        last = nc.tensor.transpose(ps_x[:, c, :], x[:, c * P:(c + 1) * P], cst.ident[:])
                    last.then_inc(x_turned, 1)

                turn(0)

                def step(e, k, b, start, end):
                    with pe.Fori(start, end) as q:
                        pe.wait_ge(w_loaded[b], k * 32 + 32)
                        pe.wait_ge(xT_ready, q + 1)
                        for c in range(KH):
                            for i in range(KD):
                                last = nc.tensor.matmul(ps_h[c][:, 0:P], up[b][:, i, c * P:(c + 1) * P], xT[:, i, :],
                                                        start=i == 0, stop=i == KD - 1)
                            last.then_inc(h_ready, 1)
                        turn(q + 1)
                        pe.wait_ge(y_ready, q + 1)
                        for c in range(KH):
                            pe.wait_ge(hT_ready, q * KH + (c + 1))
                            last = nc.tensor.matmul(ps_y[:, 0:D], hT[:, c, :], down[b][:, c, :],
                                                    start=c == 0, stop=c == KH - 1)
                        last.then_inc(y_product, 1)

                expert_loop(pe, step)

            @block.scalar
            def _(act):
                act.wait_ge(b1_turned, 1)
                nc.scalar.copy(b1_col[:], ps_b[:, 0:E * KH])
                act.drain()

                def step(e, k, b, start, end):
                    with act.Fori(start, end) as q:
                        for c in range(KH):
                            act.wait_ge(h_ready, q * KH + (c + 1))
                            nc.scalar.activation(hT[:, c, :], ps_h[c][:, 0:P], function,
                                                 bias=b1_col[:, bass.ds(e * KH + c, 1)]).then_inc(hT_ready, 1)

                expert_loop(act, step)

            @block.vector
            def _(dve):
                dve.sem_inc(y_ready, 1)
                dve.wait_ge(b_loaded, 32)
                dve.wait_ge(x_turned, 1)
                nc.vector.tensor_copy(xT[:], ps_x[:]).then_inc(xT_ready, 1)

                def step(e, k, b, start, end):
                    with dve.Fori(start, end) as q:
                        dve.wait_ge(x_turned, q + 2)
                        nc.vector.tensor_copy(xT[:], ps_x[:]).then_inc(xT_ready, 1)
                        dve.wait_ge(y_product, q + 1)
                        dve.wait_ge(y_free, q + 1)
                        nc.vector.tensor_tensor(y[:], ps_y[:, 0:D], b2_all[:, bass.ds(e, 1), :].rearrange(
                            "p a d -> p (a d)"), ALU.add).then_inc(y_ready, 1)

                expert_loop(dve, step)


def combine(nc, cst, dr, tag, plan, source=None, target=None, parts=None, normed_out=None, tokens=None, before=None,
            gamma=None, beta=None, output=None):
    final = output is not None
    with ExitStack() as ctx:
        sb = lambda n, s, d=F32: ctx.enter_context(nc.sbuf_tensor(tag + n, s, d))
        pair = lambda n, s, d=F32: [sb(f"{n}{b}", s, d) for b in range(2)]
        sem = ctx.enter_context(semaphores(nc, tag))
        B = 4
        y = [[sb(f"y{b}_{c}", [P, D]) for c in range(2)] for b in range(B)]
        mixed, out, small = pair("mixed", [P, D]), pair("out", [P, D]), pair("small", [P, 10])
        got = [sem(f"got{b}") for b in range(B)]
        stored = [sem(f"stored{b}") for b in range(2)]
        var_ready, std_ready, taken, ready = sem("var_ready"), sem("std_ready"), sem("taken"), sem("ready")
        if final:
            normal, base, scale, shift = pair("normal", [P, D]), pair("base", [P, D]), sb("gamma", [P, D]), sb("beta", [P, D])
            w_loaded, base_ready = sem("w_loaded"), sem("base_ready")
        else:
            x, hn, rest = pair("x", [P, D]), pair("hn", [P, D]), pair("rest", [P, D])
            loaded = [sem(f"loaded{b}") for b in range(2)]
            hn_stored = [sem(f"hn_stored{b}") for b in range(2)]
            normed, hi_ready, rest_ready, lo_ready = sem("normed"), sem("hi_ready"), sem("rest_ready"), sem("lo_ready")
        loop = lambda engine, step: tile_loop(engine, step, n=B, ahead=2, behind=2)
        buffer = lambda k, b: (k * 2 + b // 2, b % 2)

        with nc.Block() as block:

            @block.sync
            def _(sp):
                if final:
                    sp.dma_start(scale[:], gamma.partition_broadcast(P)).then_inc(w_loaded, 16)
                    sp.dma_start(shift[:], beta.partition_broadcast(P)).then_inc(w_loaded, 16)

                def load(t, b):
                    sp.dma_start(x[b % 2][:], source[rows(t), :]).then_inc(loaded[b % 2], 16)

                def store_normed(u, b):
                    sp.wait_ge(normed, u + 1)
                    sp.dma_start(normed_out[rows(u), :], hn[b % 2][:]).then_inc(hn_stored[b % 2], 16)

                def step(k, b):
                    t = k * B + b
                    sp.wait_ge(ready, t + 1)
                    if not final:
                        sp.dma_start(target[rows(t), :], out[b % 2][:]).then_inc(stored[b % 2], 16)
                        if not past(t + 2):
                            load(t + 2, b)
                        if not early(t - 1):
                            store_normed(t - 1, b + 1)
                    elif past(t + 1):
                        sp.dma_start(output[t * P:N_NODES, :], out[b % 2][0:LAST, :]).then_inc(stored[b % 2], 16)
                    else:
                        sp.dma_start(output[rows(t), :], out[b % 2][:]).then_inc(stored[b % 2], 16)

                if not final:
                    load(0, 0)
                    load(1, 1)
                loop(sp, step)
                if not final:
                    store_normed(NT - 1, NT - 1)
                for b in range(2):
                    sp.wait_ge(stored[b], 16 * uses(b))
                    if not final:
                        sp.wait_ge(hn_stored[b], 16 * uses(b))

            @block.gpsimd
            def _(pool):
                if final:
                    pool.wait_ge(w_loaded, 32)
                for t in range(NT):
                    if t >= B:
                        pool.wait_ge(taken, t - B + 1)
                    for c in range(2):
                        pool.indirect_dma_start(y[t % B][c][:], None, dr.slots, bass.IndirectOffsetOnAxis(
                            ap=plan.slot[c][:, t:t + 1], axis=0)).then_inc(got[t % B], 16)
                    if final:
                        if t >= 2:
                            pool.wait_ge(ready, t - 1)
                        nc.gpsimd.tensor_tensor(base[t % 2][:], before[:, t, :], shift[:], ALU.add).then_inc(base_ready, 1)

            @block.scalar
            def _(act):
                def step(k, b):
                    t = k * B + b
                    act.wait_ge(var_ready, t + 1)
                    norm_root(nc, cst, small[b % 2]).then_inc(std_ready, 1)
                    if final:
                        return
                    if not early(t - 1):
                        split(t - 1, b + 1)

                def split(u, b):
                    act.wait_ge(normed, u + 1)
                    nc.scalar.copy(tile_of(parts, u)[:, 0:D], hn[b % 2][:]).then_inc(hi_ready, 1)
                    if not early(u - 1):
                        low(u - 1, b + 1)

                def low(u, b):
                    act.wait_ge(rest_ready, u + 1)
                    nc.scalar.activation(tile_of(parts, u)[:, D:2 * D], rest[b % 2][:], ACT.Copy, scale=LO_SCALE).then_inc(lo_ready, 1)

                loop(act, step)
                if not final:
                    split(NT - 1, NT - 1)
                    low(NT - 1, NT - 1)

            @block.vector
            def _(dve):
                if final:
                    dve.wait_ge(w_loaded, 32)

                def finish(u, use, b):
                    dve.wait_ge(std_ready, u + 1)
                    if final:
                        norm_apply(nc, dve, normal[b][:], mixed[b][:], small[b])
                        dve.drain()
                        nc.vector.tensor_tensor(normal[b][:], normal[b][:], scale[:], ALU.mult)
                        dve.drain()
                        dve.wait_ge(base_ready, u + 1)
                        if not early(u - 2):
                            dve.wait_ge(stored[b], use * 16)
                        nc.vector.tensor_tensor(out[b][:], normal[b][:], base[b][:], ALU.add).then_inc(ready, 1)
                    else:
                        if not early(u - 2):
                            dve.wait_ge(hn_stored[b], use * 16)
                        norm_apply(nc, dve, hn[b][:], out[b][:], small[b]).then_inc(normed, 1)

                def remain(u, b):
                    dve.wait_ge(hi_ready, u + 1)
                    if not early(u - 2):
                        dve.wait_ge(lo_ready, u - 1)
                    nc.vector.tensor_tensor(rest[b][:], hn[b][:], tile_of(parts, u)[:, 0:D], ALU.subtract).then_inc(rest_ready, 1)

                def step(k, b):
                    t = k * B + b
                    use, d = buffer(k, b)
                    dve.wait_ge(got[b], k * 32 + 32)
                    if final:
                        start = tile_of(tokens, t)
                    else:
                        dve.wait_ge(loaded[d], use * 16 + 16)
                        start = x[d][:]
                    nc.vector.scalar_tensor_tensor(mixed[d][:], y[b][0][:], plan.weight[0][:, bass.ds(t, 1)], start,
                                                   ALU.mult, ALU.add)
                    dve.drain()
                    whole = mixed if final else out
                    if not final and not early(t - 2):
                        dve.wait_ge(stored[d], use * 16)
                    last = nc.vector.scalar_tensor_tensor(whole[d][:], y[b][1][:], plan.weight[1][:, bass.ds(t, 1)], mixed[d][:],
                                                          ALU.mult, ALU.add)
                    last.then_inc(taken, 1)
                    dve.drain()
                    if not final:
                        dve.sem_inc(ready, 1)
                    norm_stats(nc, dve, whole[d][:], small[d], var_ready)
                    if not early(t - 1):
                        before_use, before_d = buffer(k, b - 1) if b > 0 else buffer(k - 1, B - 1)
                        finish(t - 1, before_use, before_d)
                    if not final and not early(t - 2):
                        remain(t - 2, d)

                loop(dve, step)
                finish(NT - 1, (NT - 1) // 2, (NT - 1) % 2)
                if not final:
                    for u in (NT - 2, NT - 1):
                        remain(u, u % 2)


def gru(nc, ins, cst, dr, sums, states, source, result, stats):
    G = 3 * D
    GC = G // P
    with ExitStack() as ctx:
        sb = lambda n, s, d=F32: ctx.enter_context(nc.sbuf_tensor("gru_" + n, s, d))
        sem = ctx.enter_context(semaphores(nc, "gru_"))
        pb = lambda n, s: ctx.enter_context(nc.psum_tensor("gru_" + n, s, F32))
        B = 4
        w_rows = sb("w_rows", [P, 2, GC, D])
        wT = sb("wT", [P, 2, KD, G])
        bias = sb("bias", [P, 2, G])
        both = sb("both", [P, 2 * D])
        x = [[sb(f"x{b}_{i}", [P, D]) for i in range(2)] for b in range(B)]
        before = [sb(f"before{b}", [P, D]) for b in range(B)]
        xT = [sb(f"xT{b}", [P, 2, KD, P]) for b in range(2)]
        pre = [sb(f"pre{b}", [P, 2 * D]) for b in range(2)]
        gate = [sb(f"gate{b}", [P, 2 * D]) for b in range(2)]
        hidden = [sb(f"hidden{b}", [P, D]) for b in range(2)]
        cand = [sb(f"cand{b}", [P, D]) for b in range(2)]
        new = [sb(f"new{b}", [P, D]) for b in range(2)]
        kept = [sb(f"kept{b}", [P, D]) for b in range(2)]
        taken = [sb(f"taken{b}", [P, D]) for b in range(2)]
        partial = sb("partial", [P, 6])
        moments = [sb(f"moments{b}", [P, 2]) for b in range(2)]
        ps_t = [pb(f"ps_t{b}", [P, 2, KD, P]) for b in range(2)]
        ps_g = [pb(f"ps_g{b}", [P, 2 * D]) for b in range(2)]
        ps_n = [pb(f"ps_n{b}", [P, 2, D]) for b in range(2)]
        w_loaded, w_turned, w_ready = sem("w_loaded"), sem("w_turned"), sem("w_ready")
        loaded = [sem(f"loaded{b}") for b in range(B)]
        turned, xT_ready, product = sem("turned"), sem("xT_ready"), sem("product")
        pre_ready, gate_ready, cand_ready, new_ready, used = (sem("pre_ready"), sem("gate_ready"), sem("cand_ready"),
                                                             sem("new_ready"), sem("used"))
        loop = lambda engine, step: tile_loop(engine, step, n=B, ahead=1)

        with nc.Block() as block:

            @block.sync
            def _(sp):
                for i, n in enumerate(("L1_gnn_w_ih", "L1_gnn_w_hh")):
                    sp.dma_start(w_rows[:, i], ins[n].rearrange("(g p) d -> p g d", p=P)).then_inc(w_loaded, 16)
                for i, n in enumerate(("L1_gnn_b_ih", "L1_gnn_b_hh")):
                    sp.dma_start(bias[:, i], ins[n].partition_broadcast(P)).then_inc(w_loaded, 16)

                def step(k, b):
                    t = k * B + b
                    if not at_start(k):
                        sp.wait_ge(used, t - (B - 1))
                    sp.dma_start(x[b][0][:], sums[rows(t), :]).then_inc(loaded[b], 16)
                    sp.dma_start(x[b][1][:], states[rows(t), :]).then_inc(loaded[b], 16)
                    sp.dma_start(before[b][:], source[rows(t), :]).then_inc(loaded[b], 16)

                loop(sp, step)

            @block.tensor
            def _(pe):
                pe.wait_ge(w_loaded, 64)
                n = 0
                for i in range(2):
                    for g in range(GC):
                        if n >= 2:
                            pe.wait_ge(w_ready, n - 1)
                        for c in range(KD):
                            last = nc.tensor.transpose(ps_t[n % 2][:, 0, c, :], w_rows[:, i, g, c * P:(c + 1) * P], cst.ident[:])
                        last.then_inc(w_turned, 1)
                        n += 1
                pe.wait_ge(w_ready, 2 * GC)

                def turn(b, loads):
                    pe.wait_ge(loaded[b], loads * 48)
                    for i in range(2):
                        for c in range(KD):
                            last = nc.tensor.transpose(ps_t[b % 2][:, i, c, :], x[b][i][:, c * P:(c + 1) * P], cst.ident[:])
                    last.then_inc(turned, 1)

                def step(k, b):
                    t, d = k * B + b, b % 2
                    if not past(t + 1):
                        turn((b + 1) % B, k + 1 + (b + 1) // B)
                    pe.wait_ge(xT_ready, t + 1)
                    if not (at_start(k) and b < 2):
                        pe.wait_ge(pre_ready, t - 1)
                    for i in range(2):
                        for c in range(KD):
                            nc.tensor.matmul(ps_g[d][:], xT[d][:, i, c, :], wT[:, i, c, 0:2 * D],
                                             start=i == 0 and c == 0, stop=i == 1 and c == KD - 1)
                    for i in range(2):
                        for c in range(KD):
                            last = nc.tensor.matmul(ps_n[d][:, i, :], xT[d][:, i, c, :], wT[:, i, c, 2 * D:G],
                                                    start=c == 0, stop=c == KD - 1)
                    last.then_inc(product, 1)

                turn(0, 1)
                loop(pe, step)

            @block.scalar
            def _(act):
                n = 0
                for i in range(2):
                    for g in range(GC):
                        act.wait_ge(w_turned, n + 1)
                        nc.scalar.copy(wT[:, i, :, g * P:(g + 1) * P], ps_t[n % 2][:, 0]).then_inc(w_ready, 1)
                        n += 1

                def copy_turned(t, d):
                    act.wait_ge(turned, t + 1)
                    nc.scalar.copy(xT[d][:], ps_t[d][:]).then_inc(xT_ready, 1)

                def step(k, b):
                    t, d = k * B + b, b % 2
                    if not past(t + 1):
                        if not (at_start(k) and b == 0):
                            act.wait_ge(product, t)
                        copy_turned(t + 1, 1 - d)
                    act.wait_ge(pre_ready, t + 1)
                    nc.scalar.activation(gate[d][:], pre[d][:], ACT.Sigmoid).then_inc(gate_ready, 1)
                    act.wait_ge(cand_ready, t + 1)
                    nc.scalar.activation(new[d][:], cand[d][:], ACT.Tanh).then_inc(new_ready, 1)

                copy_turned(0, 0)
                loop(act, step)

            @block.vector
            def _(dve):
                dve.wait_ge(w_loaded, 64)
                nc.vector.tensor_tensor(both[:], bias[:, 0, 0:2 * D], bias[:, 1, 0:2 * D], ALU.add)
                dve.drain()

                def finish(t, d):
                    dve.wait_ge(new_ready, t + 1)
                    nc.vector.tensor_tensor(taken[d][:], taken[d][:], new[d][:], ALU.mult)
                    dve.drain()
                    out = result[:, bass.ds(t, 1), :].rearrange("p a d -> p (a d)")
                    nc.vector.tensor_tensor(out, taken[d][:], kept[d][:], ALU.add)
                    dve.drain()
                    nc.vector.bn_stats(partial[:], out)
                    dve.drain()
                    nc.vector.bn_aggr(moments[d][:], partial[:])
                    dve.drain()
                    nc.vector.tensor_copy(tile_of(stats, t), moments[d][:])

                def step(k, b):
                    t, d = k * B + b, b % 2
                    dve.wait_ge(product, t + 1)
                    nc.vector.tensor_tensor(pre[d][:], ps_g[d][:], both[:], ALU.add)
                    nc.vector.tensor_tensor(hidden[d][:], ps_n[d][:, 1, :], bias[:, 1, 2 * D:G], ALU.add)
                    nc.vector.tensor_tensor(cand[d][:], ps_n[d][:, 0, :], bias[:, 0, 2 * D:G], ALU.add)
                    dve.drain()
                    dve.sem_inc(pre_ready, 1)
                    if not (at_start(k) and b == 0):
                        finish(t - 1, 1 - d)
                    dve.wait_ge(gate_ready, t + 1)
                    nc.vector.tensor_tensor(hidden[d][:], hidden[d][:], gate[d][:, 0:D], ALU.mult)
                    dve.wait_ge(loaded[b], (k + 1) * 48)
                    nc.vector.tensor_tensor(kept[d][:], gate[d][:, D:2 * D], x[b][1][:], ALU.mult)
                    dve.drain()
                    nc.vector.tensor_tensor(cand[d][:], cand[d][:], hidden[d][:], ALU.add).then_inc(cand_ready, 1)
                    nc.vector.tensor_scalar(taken[d][:], gate[d][:, D:2 * D], -1.0, 1.0, ALU.mult, ALU.add)
                    nc.vector.tensor_tensor(kept[d][:], kept[d][:], before[b][:], ALU.add).then_inc(used, 1)

                loop(dve, step)
                dve.drain()
                finish(NT - 1, (NT - 1) % 2)


def four_blocks(nc, ins, out):
    scratch = lambda n, r, c=D: nc.dram_tensor(n, [r, c], F32, kind="Internal").ap()
    dr = Scratch()
    dr.x0, dr.x1, dr.x2 = (scratch(f"x{i}", NP) for i in range(3))
    dr.h1, dr.h2 = scratch("h1", NP), scratch("h2", NP)
    dr.own, dr.hn, dr.red = scratch("own", NP), scratch("hn", NP), scratch("red", NP)
    dr.tokens, dr.slots = scratch("tokens", NP), scratch("slots", max_tiles(16) * P)
    with ExitStack() as ctx:
        sb = lambda n, s, d=F32: ctx.enter_context(nc.sbuf_tensor(n, s, d))
        cst = Resident()
        cst.ident, cst.ones, cst.before = sb("ident", [P, P]), sb("ones", [P, P]), sb("before", [P, P])
        cst.lo_scale, cst.eps = sb("lo_scale", [P, D]), sb("eps", [P, 1])
        with ExitStack() as graph:
            gb = lambda n, s, d=F32: graph.enter_context(nc.sbuf_tensor(n, s, d))
            cst.counts = gb("counts", [P, NT, NT, P], F16)
            cst.rel_count = gb("rel_count", [P, NT, N_REL + 1])
            cst.inv_deg = gb("inv_deg", [P, NT])
            E0 = ins["L0_ffn_Wr"].shape[1]
            logit0 = gb("logit0", [P, NT, E0])
            with ExitStack() as edges:
                eb = lambda n, s, d=F32: edges.enter_context(nc.sbuf_tensor(n, s, d))
                cst.edge = eb("edge", [P, 4, EG * P])
                cst.place_no, cst.row_no = eb("place_no", [P, NT * WIN], F16), eb("row_no", [P, P])
                cst.rel_no = eb("rel_no", [P, N_REL])
                cst.base = eb("base", [P, NW, 4])
                cst.win_node = eb("win_node", [P, WT, P])
                cst.ranges, cst.upto = eb("ranges", [1, P, 3], I32), eb("upto", [1, NW])
                index_edges(nc, ins, cst, dr)
                build_counts(nc, ins, cst, dr)
            with nc.sbuf_tensor("parts", [P, NT, 2 * D], F16) as parts:
                sources, targets = (dr.x0, dr.h1, dr.h2), (dr.h1, dr.h2, dr.x1)
                for layer in range(LAYERS):
                    project(nc, ins, cst, dr, layer, sources[layer], parts)
                    last = layer == LAYERS - 1
                    aggregate(nc, ins, cst, dr, f"agg{layer}_", parts, targets[layer], relu=not last,
                              residual=dr.x0 if last else None,
                              mixture=(E0, ins["L0_ffn_Wr"], ins["L0_ffn_br"], ins["L0_ffn_gamma"], ins["L0_ffn_beta"],
                                       logit0) if last else None)

            def plan_for(stack, tag, experts):
                pb = lambda n, s, d=F32: stack.enter_context(nc.sbuf_tensor(tag + n, s, d))
                plan = Plan()
                plan.weight = [pb(f"weight{c}", [P, NT]) for c in range(2)]
                plan.slot = [pb(f"slot{c}", [P, NT], I32) for c in range(2)]
                plan.starts, plan.ends = pb("starts", [1, experts], I32), pb("ends", [1, experts], I32)
                plan.token = pb("token", [P, max_tiles(experts) + 1], I32)
                return plan

            with ExitStack() as mix:
                plan = plan_for(mix, "mix0_", E0)
                route(nc, cst, "route0_", E0, logit0, plan)
                run_experts(nc, cst, dr, "experts0_", E0, ins["L0_ffn_W1"], ins["L0_ffn_b1"], ins["L0_ffn_W2"],
                            ins["L0_ffn_b2"], ACT.Gelu, plan)
                with nc.sbuf_tensor("parts_rel", [P, NT, 2 * D], F16) as parts:
                    combine(nc, cst, dr, "combine0_", plan, source=dr.x1, target=dr.x2, parts=parts, normed_out=dr.hn)
                    aggregate(nc, ins, cst, dr, "agg_rel_", parts, dr.red, relations=True)
        E1 = ins["L1_ffn_gate_w"].shape[1]
        x3, stats3 = sb("x3", [P, NT, D]), sb("x3_stats", [P, NT, 2])
        gru(nc, ins, cst, dr, dr.red, dr.hn, dr.x2, x3, stats3)
        with ExitStack() as mix:
            plan = plan_for(mix, "mix1_", E1)
            tokens = mix.enter_context(nc.sbuf_tensor("tokens1", [P, NT, D], F32))
            logit1 = mix.enter_context(nc.sbuf_tensor("logit1", [P, NT, E1], F32))
            score_rows(nc, cst, dr, "score1_", x3, stats3, E1, ins["L1_ffn_gate_w"], ins["L1_ffn_gate_b"], tokens, logit1)
            route(nc, cst, "route1_", E1, logit1, plan)
            run_experts(nc, cst, dr, "experts1_", E1, ins["L1_ffn_w1"], ins["L1_ffn_b1"], ins["L1_ffn_w2"],
                        ins["L1_ffn_b2"], ACT.Relu, plan)
            combine(nc, cst, dr, "combine1_", plan, tokens=tokens, before=x3, gamma=ins["L1_ffn_gamma"],
                    beta=ins["L1_ffn_beta"], output=out)


_OUTPUT = "blocks_out"


def kernel(**inputs):
    from concourse import bacc
    from concourse.bass_utils import run_bass_kernel_spmd

    nc = bacc.Bacc("TRN2", target_bir_lowering=False, num_devices=1)
    arrays, ins = {}, {}
    for name, value in inputs.items():
        a = np.ascontiguousarray(value)
        arrays[f"in_{name}"] = a
        ins[name] = nc.dram_tensor(f"in_{name}", a.shape, mybir.dt.from_np(a.dtype), kind="ExternalInput").ap()
    out = nc.dram_tensor(_OUTPUT, (N_NODES, D), F32, kind="ExternalOutput").ap()
    four_blocks(nc, ins, out)
    ran = run_bass_kernel_spmd(nc, [arrays], core_ids=[0])
    return ran.results[0][_OUTPUT]
```

```python
from contextlib import ExitStack

import numpy as np

import concourse.bass as bass
from concourse import mybir

F32 = mybir.dt.float32
F16 = mybir.dt.float16
I32 = mybir.dt.int32
ALU = mybir.AluOpType
ACT = mybir.ActivationFunctionType
AX = mybir.AxisListType

P = 128
N_NODES = 3125
D = 256
KD = D // P
N_EDGES = 50000
N_REL = 16
NT = -(-N_NODES // P)
NP = NT * P
LAST = N_NODES - (NT - 1) * P
REL_ROW = -(-LAST // 32) * 32
ET = -(-N_EDGES // P)
EG = 4
FULL_ET = N_EDGES // P
EDGE_TAIL = N_EDGES - FULL_ET * P
WIN = 32
WT = P // WIN
NW = NP // WIN
GROUP = 6
REST_BITS = 0
REST = 1 << REST_BITS
EDGE_TILES = ET + GROUP + REST
NOWHERE = 4000
HID = 512
KH = HID // P
LAYERS = 3
EPS = 1e-5
LO_SCALE = 2048.0
BANK = 512


class Scratch:
    pass


class Resident:
    pass


class Weights:
    pass


class Plan:
    pass


def max_tiles(experts):
    return 2 * NP // P + experts


class Semaphores:

    def __init__(self, nc):
        self.nc, self.held = nc, []

    def clear(self):
        self.nc.clear_and_free_semaphores(self.held)
        self.nc.all_engine_barrier()
        self.held = []

    def stage(self, tag):
        def sem(name):
            self.held.append(self.nc.alloc_semaphore(tag + name))
            return self.held[-1]

        return sem


def at_start(k):
    return isinstance(k, int) and k == 0


def tile_loop(engine, step, n=2, ahead=0, behind=0):
    first = max(1, -(-behind // n))
    whole = (NT - ahead) // n
    for t in range(first * n):
        step(t // n, t % n)
    with engine.Fori(first, whole) as k:
        for b in range(n):
            step(k, b)
    for t in range(whole * n, NT):
        step(t // n, t % n)


def past(t):
    return isinstance(t, int) and t >= NT


def early(t):
    return isinstance(t, int) and t < 0


def rows(t):
    return bass.ds(t * P, P)


def tile_of(a, t):
    return a[:, bass.ds(t, 1), :].rearrange("p a d -> p (a d)")


def uses(b, n=2):
    return (NT - b + n - 1) // n


def index_edges(nc, ins, cst, dr):
    with ExitStack() as ctx:
        sb = lambda n, s, d=F32: ctx.enter_context(nc.sbuf_tensor(n, s, d))
        sem = cst.semaphores.stage("edge_")
        free = cst.counts[:].rearrange("p t s n -> p (t s n)").bitcast(I32)
        words = EG * P
        columns = lambda first, n: free[:, first * words:(first + n) * words].rearrange("p (a g e) -> p a g e", a=n, g=EG)
        raw, part, val = columns(0, 3), columns(3, 4), columns(7, 4).bitcast(F32)
        low = sb("dst_low", [P, EG])
        high = sb("dst_high", [P, EG])
        diag = columns(11, 2).bitcast(F32)
        number = sb("range_number", [P, EG * P])
        first_node = sb("first_node", [P, 1])
        last_node = sb("last_node", [P, 1])
        inside = sb("range_inside", [P, EG * P])
        key = sb("range_key", [P, EG * P])
        after = sb("range_after", [P, 1])
        left = sb("range_left", [P, 1])
        left_i = sb("range_left_i", [P, 1], I32)
        beyond = sb("range_beyond", [P, 1])
        table = sb("range_table", [P, 3, P])
        col = sb("range_col", [P, 3])
        ps_edges = ctx.enter_context(nc.psum_tensor("ps_edges", [P, 4, EG * P], F32))
        ps_low = ctx.enter_context(nc.psum_tensor("ps_low", [P, EG * P], F32))
        ps_high = ctx.enter_context(nc.psum_tensor("ps_high", [P, EG * P], F32))
        ps_before = ctx.enter_context(nc.psum_tensor("ps_before", [P, BANK], F32))
        ps_tab = ctx.enter_context(nc.psum_tensor("ps_tab", [P, BANK], F32))

        padded, loaded, consts = sem("padded"), sem("loaded"), sem("consts")
        valued, ranged = sem("valued"), sem("ranged")
        turned, spread, counted = sem("turned"), sem("spread"), sem("counted")
        summed, tabled, turned_tab = sem("summed"), sem("tabled"), sem("turned_tab")
        names = ("src", "dst", "edge_type_16")
        FG = FULL_ET // P
        LEFT = FULL_ET - FG * P

        with nc.Block() as block:

            @block.sync
            def _(sp):
                sp.wait_ge(padded, 1)
                for a, n in enumerate(names):
                    sp.dma_start(raw[:, a, 0:FG, :], ins[n][0:FG * P * P].rearrange(
                        "(g p e) -> p g e", g=FG, p=P)).then_inc(loaded, 16)
                    sp.dma_start(raw[0:LEFT, a, FG, :], ins[n][FG * P * P:FULL_ET * P].rearrange(
                        "(p e) -> p e", e=P)).then_inc(loaded, 16)
                    sp.dma_start(raw[LEFT:LEFT + 1, a, FG, 0:EDGE_TAIL], ins[n][FULL_ET * P:N_EDGES].rearrange(
                        "(p e) -> p e", p=1)).then_inc(loaded, 16)

            @block.gpsimd
            def _(pool):
                iota = lambda out, pattern, base, step: nc.gpsimd.iota(
                    out, pattern, base=base, channel_multiplier=step, allow_small_or_imprecise_dtypes=True)
                nc.gpsimd.memset(raw[:, :, FG, :], NOWHERE).then_inc(padded, 1)
                nc.gpsimd.memset(cst.ident[:], 0.0)
                nc.gpsimd.memset(cst.ones[:], 1.0)
                nc.gpsimd.memset(cst.before[:], 1.0)
                nc.gpsimd.memset(cst.lo_scale[:], LO_SCALE)
                nc.gpsimd.memset(cst.eps[:], EPS)
                nc.gpsimd.memset(cst.base[:], 0.0)
                nc.gpsimd.memset(cst.win_node[:], -2.0 * NOWHERE)
                pool.drain()
                nc.gpsimd.affine_select(out=cst.ident[:], in_=cst.ident[:], compare_op=ALU.not_equal, fill=1.0,
                                        base=0, pattern=[[-1, P]], channel_multiplier=1)
                nc.gpsimd.affine_select(out=cst.before[:], in_=cst.before[:], compare_op=ALU.is_gt, fill=0.0,
                                        base=0, pattern=[[1, P]], channel_multiplier=-1)
                iota(cst.place_no[:], [[1, NT * WIN]], 0, 0)
                iota(cst.row_no[:], [[1, P], [0, GROUP]], 0, 0)
                iota(cst.base[:, :, 0], [[P, NW]], 0, 0)
                iota(cst.base[:, :, 2], [[WIN, NW]], 0, 0)
                for q in range(WT):
                    iota(cst.win_node[:, q, q * WIN:(q + 1) * WIN], [[1, WIN]], 0, 0)
                iota(number[:], [[1, EG * P]], 0, 0)
                iota(first_node[:], [[0, 1]], 0, WIN)
                iota(last_node[:], [[0, 1]], WIN - 1, WIN).then_inc(consts, 1)

            @block.vector
            def _(dve):
                dve.wait_ge(loaded, 16 * 9)
                bits, wbits = P.bit_length() - 1, WIN.bit_length() - 1
                shift = (ALU.logical_shift_right, ALU.logical_shift_left)
                nc.vector.tensor_copy(val[:, 2], raw[:, 1])
                nc.vector.tensor_scalar(part[:, 0], raw[:, 0], P - 1, None, ALU.bitwise_and)
                nc.vector.tensor_scalar(part[:, 1], raw[:, 1], wbits, bits, *shift)
                nc.vector.tensor_scalar(part[:, 2], raw[:, 0], bits, wbits, *shift)
                nc.vector.tensor_scalar(part[:, 3], raw[:, 1], WIN - 1, None, ALU.bitwise_and)
                nc.vector.tensor_copy(val[:, 3], raw[:, 2])
                dve.drain()
                nc.vector.tensor_tensor(val[:, 0], part[:, 0], part[:, 1], ALU.add)
                nc.vector.tensor_tensor(val[:, 1], part[:, 2], part[:, 3], ALU.add).then_inc(valued, 1)
                nc.vector.tensor_reduce(low[:], val[:, 2], AX.X, ALU.min)
                nc.vector.tensor_reduce(high[:], val[:, 2], AX.X, ALU.max)
                dve.drain()
                dve.wait_ge(consts, 1)
                for side, v in enumerate((low, high)):
                    for g in range(EG):
                        last = nc.vector.tensor_scalar(diag[:, side, g, :], cst.ident[:], v[:, g:g + 1], None, ALU.mult)
                last.then_inc(ranged, 1)
                dve.wait_ge(turned, 1)
                nc.vector.tensor_copy(cst.edge[:], ps_edges[:, :, 0:EDGE_TILES])
                dve.wait_ge(spread, 1)
                nc.vector.tensor_scalar(key[:], ps_high[:], first_node[:, 0:1], None, ALU.is_ge)
                dve.drain()
                nc.vector.scalar_tensor_tensor(inside[:], ps_low[:], last_node[:, 0:1], key[:], ALU.is_le, ALU.mult)
                dve.drain()
                nc.vector.scalar_tensor_tensor(key[:], inside[:], -1000.0, number[:], ALU.mult, ALU.add)
                dve.drain()
                nc.vector.tensor_reduce(left[:], key[:], AX.X, ALU.min)
                dve.drain()
                nc.vector.tensor_scalar(col[:, 0:1], left[:], 1000.0, float(ET - 1), ALU.add, ALU.min)
                nc.vector.scalar_tensor_tensor(key[:], number[:], 1.0, inside[:], ALU.add, ALU.mult)
                dve.drain()
                nc.vector.tensor_reduce(after[:], key[:], AX.X, ALU.max)
                dve.drain()
                nc.vector.scalar_tensor_tensor(left[:], col[:, 0:1], -1.0, after[:], ALU.mult, ALU.add)
                dve.drain()
                nc.vector.tensor_scalar(left_i[:], left[:], float(REST - 1 - GROUP), None, ALU.add)
                dve.drain()
                nc.vector.tensor_scalar(left_i[:], left_i[:], REST_BITS, None, ALU.arith_shift_right)
                dve.drain()
                nc.vector.tensor_scalar(beyond[:], left_i[:], 0.0, None, ALU.max).then_inc(counted, 1)
                dve.wait_ge(summed, 1)
                nc.vector.tensor_copy(col[:, 1:2], ps_before[:, 0:1])
                nc.vector.tensor_tensor(col[:, 2:3], ps_before[:, 0:1], beyond[:], ALU.add)
                dve.drain()
                for c in range(3):
                    last = nc.vector.tensor_scalar(table[:, c, :], cst.ident[:], col[:, c:c + 1], None, ALU.mult)
                last.then_inc(tabled, 1)
                dve.wait_ge(turned_tab, 1)
                rows_of = ps_tab[0:1, 0:3 * P].rearrange("p (c w) -> p w c", c=3)
                nc.vector.tensor_copy(cst.ranges[:], rows_of)
                nc.vector.tensor_copy(cst.upto[:], ps_tab[0:1, 2 * P:2 * P + NW])

            @block.tensor
            def _(pe):
                pe.wait_ge(consts, 1)
                pe.wait_ge(valued, 1)
                for a in range(4):
                    for g in range(EG):
                        last = nc.tensor.transpose(ps_edges[:, a, g * P:(g + 1) * P], val[:, a, g, :], cst.ident[:])
                last.then_inc(turned, 1)
                pe.wait_ge(ranged, 1)
                for side, ps in enumerate((ps_low, ps_high)):
                    for g in range(EG):
                        last = nc.tensor.matmul(ps[:, g * P:(g + 1) * P], cst.ones[:], diag[:, side, g, :],
                                                start=True, stop=True)
                last.then_inc(spread, 1)
                pe.wait_ge(counted, 1)
                nc.tensor.matmul(ps_before[:, 0:1], cst.before[:], beyond[:], start=True, stop=True).then_inc(summed, 1)
                pe.wait_ge(tabled, 1)
                nc.tensor.matmul(ps_tab[:, 0:3 * P], cst.ones[:], table[:].rearrange("p c w -> p (c w)"),
                                 start=True, stop=True).then_inc(turned_tab, 1)


def build_counts(nc, ins, cst, dr):
    with ExitStack() as ctx:
        sb = lambda n, s, d=F32: ctx.enter_context(nc.sbuf_tensor(n, s, d))
        sem = cst.semaphores.stage("graph_")
        PLACES = NT * WIN
        keys = [sb(f"keys{b}", [P, 4, GROUP]) for b in range(2)]
        is_place = [sb(f"is_place{b}", [P, GROUP, PLACES], F16) for b in range(2)]
        small_keys = [sb(f"small_keys{b}", [P, 4, GROUP], F16) for b in range(2)]
        is_row = [sb(f"is_row{b}", [P, P, GROUP], F16) for b in range(2)]
        is_node = [sb(f"is_node{b}", [P, WIN, GROUP], F16) for b in range(2)]
        is_rel = [sb(f"is_rel{b}", [P, N_REL + 1, GROUP], F16) for b in range(2)]
        is_tile_node = sb("is_tile_node", [P, P, REST], F16)
        nodes = sb("nodes", [P, P], F16)
        part_no, passed = sb("part_no", [1, 1]), sb("passed", [1, NW])
        at_window, at_window_i = sb("at_window", [1, 1]), sb("at_window_i", [1, 1], I32)
        zeros = sb("zeros", [P, D])
        degree = sb("degree", [P, NT])
        some = sb("degree_some", [P, NT])
        acc = [[ctx.enter_context(nc.psum_tensor(f"ps_counts{b}_{i}", [P, BANK], F32)) for i in range(2)] for b in range(2)]
        acc_rel = [ctx.enter_context(nc.psum_tensor(f"ps_rel{b}", [P, BANK], F32)) for b in range(2)]
        SPLIT = ((0, BANK), (BANK, PLACES))
        MOVES = len(SPLIT) + 1
        keyed, hot, last_hot, spent, moved = sem("keyed"), sem("hot"), sem("last_hot"), sem("spent"), sem("moved")
        picked, part_keyed, part_hot, part_spent, part_added = (sem("picked"), sem("part_keyed"), sem("part_hot"),
                                                                sem("part_spent"), sem("part_added"))
        last_used = sem("last_used")
        part_begun, part_copied = sem("part_begun"), sem("part_copied")
        distance = sb("distance", [P, PLACES], F16)
        part_counts, part_rel = distance, sb("part_rel", [P, N_REL + 1])
        zeroed, filled = sem("zeroed"), sem("filled")
        known = "the table is made on the chip"
        MOST = NW * (ET // REST)

        def windows(engine, step, first=0):
            with engine.Fori(first, NT) as t:
                for q in range(WT):
                    step(t * WT + q, q, q % 2, t)

        def key_of(b, k, n, tiles):
            return small_keys[b][:, k, 0:tiles].unsqueeze(1).to_broadcast([P, n, tiles])

        def one_hot(b, tiles):
            for g in range(min(tiles, GROUP - 1)):
                nc.vector.tensor_scalar(is_place[b][:, g, :], cst.place_no[:], keys[b][:, 1, g:g + 1], None, ALU.is_equal)
            nc.vector.tensor_tensor(is_row[b][:, :, 0:tiles], cst.row_no[:, :, 0:tiles], key_of(b, 0, P, tiles), ALU.is_equal)
            nc.vector.tensor_tensor(is_rel[b][:, 0:N_REL, 0:tiles], cst.row_no[:, 0:N_REL, 0:tiles],
                                    key_of(b, 3, N_REL, tiles), ALU.is_equal)

        def count(b, tiles):
            for g in range(tiles):
                for i, (lo, hi) in enumerate(SPLIT):
                    nc.tensor.matmul(acc[b][i][:, 0:hi - lo], is_row[b][:, :, g], is_place[b][:, g, lo:hi],
                                     start=g == 0, stop=g == tiles - 1, skip_group_check=True)

        with nc.Block() as block:

            @block.sync
            def _(sp):
                sp.wait_ge(zeroed, 1)
                load_layer(sp, ins, cst, 0)
                sp.dma_start(dr.x0[0:N_NODES, :], ins["x"]).then_inc(filled, 16)
                sp.dma_start(dr.x0[N_NODES:NP, :], zeros[0:NP - N_NODES, :]).then_inc(filled, 16)
                with sp.Fori(0, dr.slots.shape[0] // P) as q:
                    sp.dma_start(dr.slots[rows(q), :], zeros[:]).then_inc(filled, 16)
                sp.wait_ge(filled, 16 * (2 + dr.slots.shape[0] // P))

            @block.gpsimd
            def _(pool):
                def take(to, w, tile, tiles):
                    for out in to:
                        last = nc.gpsimd.tensor_tensor(
                            out[:, :, 0:tiles], cst.edge[:, :, bass.ds(tile, tiles)],
                            cst.base[:, bass.ds(w, 1), :].rearrange("p w k -> p (w k)").unsqueeze(2).to_broadcast([P, 4, tiles]),
                            ALU.subtract)
                    return last

                def step(w, q, b, t):
                    first = pool.value_load(cst.ranges[0:1, bass.ds(w, 1), 0:1].rearrange("p w c -> p (w c)"),
                                            min_val=0, max_val=ET - 1)
                    pool.wait_ge(hot, w + 1)
                    pool.wait_ge(last_used, w + 1)
                    take((keys[b], small_keys[b]), w, first, GROUP).then_inc(keyed, 1)

                windows(pool, step)
                pool.wait_ge(moved, MOVES * (NW + 2))
                total = pool.value_load(cst.ranges[0:1, NW - 1, 2:3], min_val=0, max_val=MOST)
                with pool.Fori(0, nc.s_assert_within(total + 1, 1, MOST + 1, skip_runtime_bounds_check_because=known)) as i:
                    pool.wait_ge(picked, i + 1)
                    pool.sem_inc(part_begun, 1)
                    w = pool.value_load(at_window_i[0:1, 0:1], min_val=0, max_val=NW - 1)
                    t, q = w // WT, w % WT
                    _, (first, before) = nc.values_load_multi_w_load_instructions(
                        cst.ranges[0:1, bass.ds(w, 1), 0:2].rearrange("p w c -> p (w c)"), engines=[pool.engine],
                        min_val=0, max_val=MOST)
                    tile = nc.s_assert_within((i - before) * REST + first + GROUP, 0, EDGE_TILES - REST,
                                              skip_runtime_bounds_check_because=known)
                    take((keys[0], small_keys[0]), w, tile, REST)
                    nc.gpsimd.tensor_copy(nodes[:], cst.win_node[:, bass.ds(q, 1), :].rearrange(
                        "p q n -> p (q n)")).then_inc(part_keyed, 1)
                    pool.drain()
                    pool.wait_ge(part_copied, i + 1)
                    for k, (lo, hi) in enumerate(SPLIT):
                        at = cst.counts[:, bass.ds(t, 1), lo // WIN:hi // WIN, bass.ds(q * WIN, WIN)].rearrange(
                            "p a s n -> p (a s) n")
                        nc.gpsimd.tensor_tensor(at, part_counts[:, lo:hi].rearrange("p (s n) -> p s n", n=WIN), at, ALU.add)
                    at = cst.rel_count[:, bass.ds(t, 1), :].rearrange("p a r -> p (a r)")
                    nc.gpsimd.tensor_tensor(at, part_rel[:], at, ALU.add)
                    pool.drain()
                    pool.sem_inc(part_added, 1)

            @block.vector
            def _(dve):
                dve.sem_inc(hot, 2)
                nc.vector.memset(zeros[:], 0.0).then_inc(zeroed, 1)
                for b in range(2):
                    nc.vector.memset(is_rel[b][:], 1.0)
                nc.vector.memset(part_no[:], 0.0)
                dve.drain()

                def step(w, q, b, t):
                    dve.wait_ge(spent, w + 1)
                    dve.wait_ge(keyed, w + 1)
                    one_hot(b, GROUP)
                    nc.vector.tensor_tensor(is_node[b][:], cst.row_no[:, 0:WIN, :], key_of(b, 2, WIN, GROUP), ALU.is_equal).then_inc(hot, 1)

                windows(dve, step)
                total = dve.value_load(cst.ranges[0:1, NW - 1, 2:3], min_val=0, max_val=MOST)
                with dve.Fori(0, nc.s_assert_within(total + 1, 1, MOST + 1, skip_runtime_bounds_check_because=known)) as i:
                    nc.vector.tensor_scalar(passed[:], cst.upto[:], part_no[:], None, ALU.is_le)
                    dve.drain()
                    nc.vector.tensor_reduce(at_window[:], passed[:], AX.X, ALU.add)
                    nc.vector.tensor_scalar(part_no[:], part_no[:], 1.0, None, ALU.add)
                    dve.drain()
                    nc.vector.tensor_scalar(at_window_i[:], at_window[:], float(NW - 1), None, ALU.min).then_inc(picked, 1)
                    dve.wait_ge(part_keyed, i + 1)
                    one_hot(0, REST)
                    nc.vector.tensor_tensor(is_tile_node[:], nodes[:].unsqueeze(2), key_of(0, 2, P, REST), ALU.is_equal).then_inc(part_hot, 1)
                    dve.drain()
                    dve.wait_ge(part_added, i + 1)
                nc.vector.tensor_scalar(degree[:], cst.rel_count[:, :, N_REL], 1.0, None, ALU.max)
                nc.vector.tensor_scalar(some[:], cst.rel_count[:, :, N_REL], 1.0, None, ALU.min)
                dve.drain()
                nc.vector.reciprocal(degree[:], degree[:])
                dve.drain()
                nc.vector.tensor_tensor(cst.inv_deg[:], degree[:], some[:], ALU.mult)

            @block.tensor
            def _(pe):
                pe.sem_inc(spent, 2)

                def step(w, q, b, t):
                    pe.wait_ge(hot, w + 3)
                    pe.wait_ge(last_hot, w + 1)
                    pe.wait_ge(moved, (w + 1) * MOVES)
                    count(b, GROUP)
                    for g in range(GROUP):
                        last = nc.tensor.matmul(acc_rel[b][q * WIN:(q + 1) * WIN, 0:N_REL + 1], is_node[b][:, :, g],
                                                is_rel[b][:, :, g], start=g == 0, stop=g == GROUP - 1, skip_group_check=True)
                    last.then_inc(spent, 1)

                windows(pe, step)
                pe.wait_ge(moved, MOVES * (NW + 2))
                total = pe.value_load(cst.ranges[0:1, NW - 1, 2:3], min_val=0, max_val=MOST)
                with pe.Fori(0, nc.s_assert_within(total + 1, 1, MOST + 1, skip_runtime_bounds_check_because=known)) as i:
                    pe.wait_ge(part_hot, i + 1)
                    count(0, REST)
                    for g in range(REST):
                        last = nc.tensor.matmul(acc_rel[0][:, 0:N_REL + 1], is_tile_node[:, :, g], is_rel[0][:, :, g],
                                                start=g == 0, stop=g == REST - 1, skip_group_check=True)
                    last.then_inc(part_spent, 1)

            @block.scalar
            def _(act):
                nc.scalar.preload_act_table(ACT.Copy)
                act.sem_inc(moved, MOVES * 2)
                act.sem_inc(last_used, 2)

                def keep(i, q, b, t):
                    at, (lo, hi) = slice(q * WIN, (q + 1) * WIN), SPLIT[i]
                    nc.scalar.copy(cst.counts[:, bass.ds(t, 1), lo // WIN:hi // WIN, at].rearrange("p a s n -> p (a s) n"),
                                   acc[b][i][:, 0:hi - lo].rearrange("p (s n) -> p s n", n=WIN)).then_inc(moved, 1)

                def keep_relations(q, b, t):
                    at = slice(q * WIN, (q + 1) * WIN)
                    nc.scalar.copy(cst.rel_count[at, bass.ds(t, 1), :].rearrange("p a r -> p (a r)"),
                                   acc_rel[b][at, 0:N_REL + 1]).then_inc(moved, 1)

                def step(w, q, b, t):
                    kept = None if early(w - 2) else ((q - 2) % WT, b, t if q > 1 else t - 1)
                    if kept:
                        act.wait_ge(spent, w + 1)
                        keep(0, *kept)
                    act.wait_ge(keyed, w + 1)
                    if kept or not early(w - 1):
                        act.wait_ge(last_hot, w)
                    nc.scalar.activation(distance[:], cst.place_no[:], ACT.Abs, bias=keys[b][:, 1, GROUP - 1:GROUP],
                                         scale=-1.0).then_inc(last_used, 1)
                    if kept:
                        keep(1, *kept)
                        keep_relations(*kept)
                    act.wait_ge(last_used, w + 3)
                    act.wait_ge(spent, w + 1)
                    nc.scalar.activation(is_place[b][:, GROUP - 1, :], distance[:], ACT.Relu, bias=1.0, scale=-1.0).then_inc(
                        last_hot, 1)

                for q in range(WT):
                    step(q, q, q % 2, 0)
                windows(act, step, 1)
                for w in (NW - 2, NW - 1):
                    act.wait_ge(spent, w + 3)
                    for i in range(len(SPLIT)):
                        keep(i, w % WT, w % 2, NT - 1)
                    keep_relations(w % WT, w % 2, NT - 1)
                total = act.value_load(cst.ranges[0:1, NW - 1, 2:3], min_val=0, max_val=MOST)
                with act.Fori(0, nc.s_assert_within(total + 1, 1, MOST + 1, skip_runtime_bounds_check_because=known)) as i:
                    act.wait_ge(part_spent, i + 1)
                    for k, (lo, hi) in enumerate(SPLIT):
                        nc.scalar.copy(part_counts[:, lo:hi], acc[0][k][:, 0:hi - lo])
                    nc.scalar.copy(part_rel[:], acc_rel[0][:, 0:N_REL + 1])
                    act.drain()
                    act.sem_inc(part_copied, 1)


def norm_stats(nc, dve, src, small, var_ready):
    nc.vector.bn_stats(small[:, 0:6], src)
    dve.drain()
    nc.vector.bn_aggr(small[:, 6:8], small[:, 0:6]).then_inc(var_ready, 1)


def norm_root(nc, cst, small):
    return nc.scalar.activation(small[:, 8:9], small[:, 7:8], ACT.Sqrt, bias=cst.eps[:])


def norm_apply(nc, dve, out, src, small):
    nc.vector.reciprocal(small[:, 9:10], small[:, 8:9])
    dve.drain()
    return nc.vector.tensor_scalar(out, src, small[:, 6:7], small[:, 9:10], ALU.subtract, ALU.mult)


def normalize(nc, dve, out, src, small, var_ready, std_ready, count):
    norm_stats(nc, dve, src, small, var_ready)
    dve.drain()
    dve.wait_ge(std_ready, count)
    return norm_apply(nc, dve, out, src, small)


LAYER_LOADS = 2 * KD + 1


def load_layer(sp, ins, cst, layer):
    for k in range(KD):
        sp.dma_start(cst.layer_weights[:, k, 0:D], ins["L0_gnn_W_self"][layer, rows(k), :]).then_inc(cst.layer_loaded, 16)
        sp.dma_start(cst.layer_weights[:, k, D:2 * D], ins["L0_gnn_W_neigh"][layer, rows(k), :]).then_inc(cst.layer_loaded, 16)
    sp.dma_start(cst.layer_bias[:], ins["L0_gnn_bias"][layer].partition_broadcast(P)).then_inc(cst.layer_loaded, 16)


def project(nc, ins, cst, dr, layer, source, parts):
    norm = layer == 0
    with ExitStack() as ctx:
        tag = f"proj{layer}_"
        sb = lambda n, s, d=F32: ctx.enter_context(nc.sbuf_tensor(tag + n, s, d))
        sem = cst.semaphores.stage(tag)
        weights, bias, w_loaded = cst.layer_weights, cst.layer_bias, cst.layer_loaded
        w_count = 16 * LAYER_LOADS * (layer + 1)
        B = 4
        h = [sb(f"h{b}", [P, D]) for b in range(B)]
        hn = [sb(f"hn{b}", [P, D]) for b in range(2)] if norm else h
        hT = [sb(f"hT{b}", [P, KD, P]) for b in range(2)]
        rest = [sb(f"rest{b}", [P, D]) for b in range(2)]
        own = [sb(f"own{b}", [P, D]) for b in range(2)]
        small = [sb(f"small{b}", [P, 10]) for b in range(2)]
        ps_t = [ctx.enter_context(nc.psum_tensor(tag + f"ps_t{b}", [P, KD, P], F32)) for b in range(2)]
        ps_n, ps_o = ([ctx.enter_context(nc.psum_tensor(tag + f"{n}{b}", [P, BANK], F32)) for b in range(2)]
                      for n in ("ps_n", "ps_o"))
        h_loaded = [sem(f"h_loaded{b}") for b in range(B)]
        stored = [sem(f"stored{b}") for b in range(2)]
        var_ready, std_ready, normed = sem("var_ready"), sem("std_ready"), sem("normed")
        turned, hT_ready, part_product, product = sem("turned"), sem("hT_ready"), sem("part_product"), sem("product")
        hi_ready, rest_ready, own_ready, lo_ready = sem("hi_ready"), sem("rest_ready"), sem("own_ready"), sem("lo_ready")

        loop = lambda engine, step, ahead=3: tile_loop(engine, step, n=B, ahead=ahead, behind=2)

        with nc.Block() as block:

            @block.sync
            def _(sp):
                def load(t, b):
                    sp.dma_start(h[b][:], source[rows(t), :]).then_inc(h_loaded[b], 16)

                def step(k, b):
                    t = k * B + b
                    if not past(t + B):
                        sp.wait_ge(normed if norm else turned, t + 1)
                        load(t + B, b)
                    sp.wait_ge(own_ready, t + 1)
                    sp.dma_start(dr.own[rows(t), :], own[b % 2][:]).then_inc(stored[b % 2], 16)

                for b in range(B):
                    load(b, b)
                loop(sp, step, B)
                for b in range(2):
                    sp.wait_ge(stored[b], 16 * uses(b))

            @block.tensor
            def _(pe):
                pe.wait_ge(w_loaded, w_count)

                def turn(t, use, b):
                    if norm:
                        pe.wait_ge(normed, t + 1)
                    else:
                        pe.wait_ge(h_loaded[b], use * 16 + 16)
                    for c in range(KD):
                        last = nc.tensor.transpose(ps_t[b % 2][:, c, :], hn[b % len(hn)][:, c * P:(c + 1) * P], cst.ident[:])
                    last.then_inc(turned, 1)

                def step(k, buf):
                    t, b = k * B + buf, buf % 2
                    if not past(t + 1):
                        turn(t + 1, k + (buf + 1) // B, (buf + 1) % B)
                    pe.wait_ge(hT_ready, t + 1)
                    if not early(t - 2):
                        pe.wait_ge(own_ready, t - 1)
                    for ps, lo, done in ((ps_n, D, part_product), (ps_o, 0, product)):
                        for c in range(KD):
                            last = nc.tensor.matmul(ps[b][:, 0:D], hT[b][:, c, :], weights[:, c, lo:lo + D],
                                                    start=c == 0, stop=c == KD - 1)
                        last.then_inc(done, 1)

                turn(0, 0, 0)
                loop(pe, step)

            @block.scalar
            def _(act):
                nc.scalar.preload_act_table(ACT.Sqrt if norm else ACT.Copy)
                def copy_turned(t, b):
                    act.wait_ge(turned, t + 1)
                    nc.scalar.copy(hT[b][:], ps_t[b][:]).then_inc(hT_ready, 1)

                def root(t, b):
                    act.wait_ge(var_ready, t + 1)
                    norm_root(nc, cst, small[b]).then_inc(std_ready, 1)

                def step(k, buf):
                    t, b = k * B + buf, buf % 2
                    if not past(t + 1):
                        if not early(t - 1):
                            act.wait_ge(product, t)
                        copy_turned(t + 1, 1 - b)
                    act.wait_ge(part_product, t + 1)
                    nc.scalar.copy(tile_of(parts, t)[:, 0:D], ps_n[b][:, 0:D]).then_inc(hi_ready, 1)
                    if norm and not past(t + 3):
                        root(t + 3, 1 - b)

                if norm:
                    for t in range(3):
                        root(t, t % 2)
                copy_turned(0, 0)
                loop(act, step)

            @block.vector
            def _(dve):
                def measure(use, b):
                    dve.wait_ge(h_loaded[b], use * 16 + 16)
                    norm_stats(nc, dve, h[b][:], small[b % 2], var_ready)

                def apply(t, b):
                    dve.wait_ge(std_ready, t + 1)
                    norm_apply(nc, dve, hn[b % 2][:], h[b][:], small[b % 2]).then_inc(normed, 1)

                def step(k, buf):
                    t, b = k * B + buf, buf % 2
                    if norm and not past(t + 2):
                        dve.wait_ge(turned, t + 1)
                        apply(t + 2, (buf + 2) % B)
                    if norm and not past(t + 3):
                        measure(k + (buf + 3) // B, (buf + 3) % B)
                    dve.wait_ge(hi_ready, t + 1)
                    if not early(t - 2):
                        dve.wait_ge(lo_ready, t - 1)
                    nc.vector.tensor_tensor(rest[b][:], ps_n[b][:, 0:D], tile_of(parts, t)[:, 0:D],
                                            ALU.subtract).then_inc(rest_ready, 1)
                    dve.wait_ge(product, t + 1)
                    if not early(t - 2):
                        dve.wait_ge(stored[b], (k * 2 + buf // 2) * 16)
                    nc.vector.tensor_tensor(own[b][:], ps_o[b][:, 0:D], bias[:], ALU.add).then_inc(own_ready, 1)

                dve.wait_ge(w_loaded, w_count)
                if norm:
                    measure(0, 0)
                    measure(0, 1)
                    apply(0, 0)
                    measure(0, 2)
                    apply(1, 1)
                loop(dve, step)

            @block.gpsimd
            def _(pool):
                def step(k, b):
                    t = k * 2 + b
                    pool.wait_ge(rest_ready, t + 1)
                    nc.gpsimd.tensor_tensor(parts[:, bass.ds(t, 1), D:2 * D].rearrange("p a d -> p (a d)"),
                                            rest[b][:], cst.lo_scale[:], ALU.mult).then_inc(lo_ready, 1)

                tile_loop(pool, step)


def aggregate(nc, ins, cst, dr, tag, parts, target, relu=False, residual=None, relations=False, mixture=None,
              next_layer=None):
    with ExitStack() as ctx:
        sb = lambda n, s, d=F32: ctx.enter_context(nc.sbuf_tensor(tag + n, s, d))
        pair = lambda n, s, d=F32: [sb(f"{n}{b}", s, d) for b in range(2)]
        bank = lambda n, s: [ctx.enter_context(nc.psum_tensor(tag + f"{n}{b}", s, F32)) for b in range(2)]
        sem = cst.semaphores.stage(tag)
        own, total, out = pair("own", [P, D]), pair("total", [P, D]), pair("out", [P, D])
        ps = bank("ps", [P, 2 * D])
        loaded = [sem(f"loaded{b}") for b in range(2)]
        stored = [sem(f"stored{b}") for b in range(2)]
        summed, taken, ready = sem("summed"), sem("taken"), sem("ready")
        if mixture is not None:
            E, router, router_bias, gamma, beta, logit = mixture
            before, inner, xn = pair("before", [P, D]), pair("inner", [P, D]), pair("xn", [P, D])
            xT = pair("xT", [P, KD, P])
            stats = [pair("outer_stats", [P, 10]), pair("inner_stats", [P, 10])]
            weights, bias, scale, shift = sb("router", [P, KD, E]), sb("bias", [P, E]), sb("gamma", [P, D]), sb("beta", [P, D])
            ps_t, ps_l = bank("ps_t", [P, KD, P]), bank("ps_l", [P, BANK])
            w_loaded = sem("w_loaded")
            tokens_stored = [sem(f"tokens_stored{b}") for b in range(2)]
            var_ready, std_ready = ([sem(f"{n}{i}") for i in range(2)] for n in ("var_ready", "std_ready"))
            normed, turned, xT_ready, scored, logit_ready = (sem("normed"), sem("turned"), sem("xT_ready"),
                                                             sem("scored"), sem("logit_ready"))
        per_tile = 1 + (residual is not None)
        loop = lambda engine, step: tile_loop(engine, step, ahead=2, behind=3 if mixture is not None else 0)

        with nc.Block() as block:

            @block.sync
            def _(sp):
                def load(t, b):
                    sp.dma_start(own[b][:], dr.own[rows(t), :]).then_inc(loaded[b], 16)
                    if residual is not None:
                        sp.dma_start(before[b][:], residual[rows(t), :]).then_inc(loaded[b], 16)

                def store_tokens(u, b):
                    sp.wait_ge(normed, u + 1)
                    sp.dma_start(dr.tokens[rows(u), :], xn[b][:]).then_inc(tokens_stored[b], 16)

                def step(k, b):
                    t = k * 2 + b
                    sp.wait_ge(taken if relations else ready, t + 1)
                    sp.dma_start(target[rows(t), :], out[b][:]).then_inc(stored[b], 16)
                    if not relations and not past(t + 2):
                        load(t + 2, b)
                    if mixture is not None and not early(t - 1):
                        store_tokens(t - 1, 1 - b)

                if not relations:
                    load(0, 0)
                    load(1, 1)
                if next_layer is not None:
                    load_layer(sp, ins, cst, next_layer)
                if mixture is not None:
                    sp.dma_start(weights[:], router.rearrange("(k p) e -> p k e", p=P)).then_inc(w_loaded, 16)
                    for to, row in ((bias, router_bias), (scale, gamma), (shift, beta)):
                        sp.dma_start(to[:], row.partition_broadcast(P)).then_inc(w_loaded, 16)
                loop(sp, step)
                if mixture is not None:
                    store_tokens(NT - 1, (NT - 1) % 2)
                for b in range(2):
                    sp.wait_ge(stored[b], 16 * uses(b))
                    if mixture is not None:
                        sp.wait_ge(tokens_stored[b], 16 * uses(b))

            @block.tensor
            def _(pe):
                def turn(u, b):
                    pe.wait_ge(normed, u + 1)
                    for c in range(KD):
                        last = nc.tensor.transpose(ps_t[b][:, c, :], xn[b][:, c * P:(c + 1) * P], cst.ident[:])
                    last.then_inc(turned, 1)

                def score(u, b):
                    pe.wait_ge(w_loaded, 64)
                    pe.wait_ge(xT_ready, u + 1)
                    pe.wait_ge(logit_ready, u + 1)
                    for c in range(KD):
                        last = nc.tensor.matmul(ps_l[b][:, 0:E], xT[b][:, c, :], weights[:, c, :],
                                                start=c == 0, stop=c == KD - 1)
                    last.then_inc(scored, 1)

                def step(k, b):
                    t = k * 2 + b
                    if not at_start(k):
                        pe.wait_ge(taken, t - 1)
                    for s in range(NT):
                        last = nc.tensor.matmul(ps[b][:], cst.counts[:, bass.ds(t, 1), s, :].rearrange("p a n -> p (a n)"),
                                                parts[:, s, :], start=s == 0, stop=s == NT - 1)
                    last.then_inc(summed, 1)
                    if mixture is not None:
                        if not early(t - 3):
                            score(t - 3, 1 - b)
                        if not early(t - 2):
                            turn(t - 2, b)

                loop(pe, step)
                if mixture is not None:
                    score(NT - 3, (NT - 3) % 2)
                    for u in (NT - 2, NT - 1):
                        turn(u, u % 2)
                        score(u, u % 2)

            @block.scalar
            def _(act):
                def copy_turned(u, b):
                    act.wait_ge(turned, u + 1)
                    nc.scalar.copy(xT[b][:], ps_t[b][:]).then_inc(xT_ready, 1)

                def step(k, b):
                    t = k * 2 + b
                    if not early(t - 2):
                        copy_turned(t - 2, b)
                    for i in range(2):
                        act.wait_ge(var_ready[i], t + 1)
                        norm_root(nc, cst, stats[i][b]).then_inc(std_ready[i], 1)

                if mixture is not None:
                    nc.scalar.preload_act_table(ACT.Sqrt)
                    loop(act, step)
                    for u in (NT - 2, NT - 1):
                        copy_turned(u, u % 2)

            @block.vector
            def _(dve):
                def token(u, b, stores):
                    dve.wait_ge(std_ready[1], u + 1)
                    norm_apply(nc, dve, inner[b][:], inner[b][:], stats[1][b])
                    dve.drain()
                    dve.wait_ge(w_loaded, 64)
                    nc.vector.tensor_tensor(inner[b][:], inner[b][:], scale[:], ALU.mult)
                    dve.drain()
                    if not early(u - 2):
                        dve.wait_ge(turned, u - 1)
                        dve.wait_ge(tokens_stored[b], stores * 16)
                    nc.vector.tensor_tensor(xn[b][:], inner[b][:], shift[:], ALU.add).then_inc(normed, 1)

                def keep_logit(u, b):
                    dve.wait_ge(scored, u + 1)
                    nc.vector.tensor_tensor(tile_of(logit, u), ps_l[b][:, 0:E], bias[:], ALU.add).then_inc(logit_ready, 1)

                def step(k, b):
                    t = k * 2 + b
                    dve.wait_ge(summed, t + 1)
                    if not at_start(k):
                        dve.wait_ge(stored[b], k * 16)
                    nc.vector.tensor_copy(total[b][:], ps[b][:, 0:D])
                    dve.drain()
                    if relations:
                        nc.vector.scalar_tensor_tensor(out[b][:], ps[b][:, D:2 * D], 1.0 / LO_SCALE, total[b][:],
                                                       ALU.mult, ALU.add).then_inc(taken, 1)
                        return
                    nc.vector.scalar_tensor_tensor(total[b][:], ps[b][:, D:2 * D], 1.0 / LO_SCALE, total[b][:],
                                                   ALU.mult, ALU.add).then_inc(taken, 1)
                    dve.drain()
                    dve.wait_ge(loaded[b], (k + 1) * (16 * per_tile))
                    last = nc.vector.scalar_tensor_tensor(out[b][:], total[b][:], cst.inv_deg[:, bass.ds(t, 1)], own[b][:],
                                                          ALU.mult, ALU.add)
                    if relu:
                        dve.drain()
                        last = nc.vector.tensor_scalar(out[b][:], out[b][:], 0.0, None, ALU.max)
                    if residual is not None:
                        dve.drain()
                        last = nc.vector.tensor_tensor(out[b][:], out[b][:], before[b][:], ALU.add)
                    last.then_inc(ready, 1)
                    if mixture is None:
                        return
                    dve.drain()
                    norm_stats(nc, dve, out[b][:], stats[0][b], var_ready[0])
                    if not early(t - 1):
                        token(t - 1, 1 - b, k - 1 + b)
                    dve.wait_ge(std_ready[0], t + 1)
                    norm_apply(nc, dve, inner[b][:], out[b][:], stats[0][b])
                    dve.drain()
                    norm_stats(nc, dve, inner[b][:], stats[1][b], var_ready[1])
                    if not early(t - 3):
                        keep_logit(t - 3, 1 - b)

                if mixture is not None:
                    dve.sem_inc(logit_ready, 2)
                loop(dve, step)
                if mixture is not None:
                    token(NT - 1, (NT - 1) % 2, uses((NT - 1) % 2) - 1)
                    for u in (NT - 3, NT - 2, NT - 1):
                        keep_logit(u, u % 2)


def score_rows(nc, cst, dr, tag, x, stats, E, router, router_bias, tokens, logit, beta):
    with ExitStack() as ctx:
        sb = lambda n, s, d=F32: ctx.enter_context(nc.sbuf_tensor(tag + n, s, d))
        bank = lambda n, s: [ctx.enter_context(nc.psum_tensor(tag + f"{n}{b}", s, F32)) for b in range(2)]
        sem = cst.semaphores.stage(tag)
        weights, bias = sb("router", [P, KD, E]), sb("bias", [P, E])
        dev, inv = sb("dev", [P, NT]), sb("inv", [P, NT])
        B = 4
        xn = [sb(f"xn{b}", [P, D]) for b in range(B)]
        xT = [sb(f"xT{b}", [P, KD, P]) for b in range(2)]
        ps_t, ps_l = bank("ps_t", [P, KD, P]), bank("ps_l", [P, BANK])
        shift = sb("shift", [P, D])
        w_loaded, std_ready, normed, kept, stored = sem("w_loaded"), sem("std_ready"), sem("normed"), sem("kept"), sem("stored")
        shift_loaded = sem("shift_loaded")
        turned, xT_ready, scored, logit_ready = sem("turned"), sem("xT_ready"), sem("scored"), sem("logit_ready")
        loop = lambda engine, step: tile_loop(engine, step, n=B, behind=B)

        with nc.Block() as block:

            @block.sync
            def _(sp):
                sp.dma_start(weights[:], router.rearrange("(k p) e -> p k e", p=P)).then_inc(w_loaded, 16)
                sp.dma_start(bias[:], router_bias.partition_broadcast(P)).then_inc(w_loaded, 16)
                sp.dma_start(shift[:], beta.partition_broadcast(P)).then_inc(shift_loaded, 16)

                def step(k, b):
                    t = k * B + b
                    sp.wait_ge(kept, t + 1)
                    sp.dma_start(dr.tokens[rows(t), :], tile_of(tokens, t)).then_inc(stored, 16)

                loop(sp, step)
                sp.wait_ge(stored, 16 * NT)

            @block.tensor
            def _(pe):
                pe.wait_ge(w_loaded, 32)

                def score(u, b):
                    pe.wait_ge(xT_ready, u + 1)
                    pe.wait_ge(logit_ready, u + 1)
                    for c in range(KD):
                        last = nc.tensor.matmul(ps_l[b][:, 0:E], xT[b][:, c, :], weights[:, c, :],
                                                start=c == 0, stop=c == KD - 1)
                    last.then_inc(scored, 1)

                def step(k, b):
                    t = k * B + b
                    pe.wait_ge(normed, t + 1)
                    for c in range(KD):
                        last = nc.tensor.transpose(ps_t[b % 2][:, c, :], xn[b][:, c * P:(c + 1) * P], cst.ident[:])
                    last.then_inc(turned, 1)
                    if not early(t - 1):
                        score(t - 1, (b + 1) % 2)

                loop(pe, step)
                score(NT - 1, (NT - 1) % 2)

            @block.scalar
            def _(act):
                nc.scalar.preload_act_table(ACT.Sqrt)
                nc.scalar.activation(dev[:], stats[:, :, 1], ACT.Sqrt, bias=cst.eps[:]).then_inc(std_ready, 1)

                def step(k, b):
                    t = k * B + b
                    act.wait_ge(turned, t + 1)
                    nc.scalar.copy(xT[b % 2][:], ps_t[b % 2][:]).then_inc(xT_ready, 1)
                    nc.scalar.copy(tile_of(tokens, t), xn[b][:]).then_inc(kept, 1)

                loop(act, step)

            @block.vector
            def _(dve):
                dve.sem_inc(logit_ready, 2)
                dve.wait_ge(std_ready, 1)
                nc.vector.reciprocal(inv[:], dev[:])
                dve.drain()
                dve.wait_ge(w_loaded, 32)

                def keep_logit(u, b):
                    dve.wait_ge(scored, u + 1)
                    nc.vector.tensor_tensor(tile_of(logit, u), ps_l[b][:, 0:E], bias[:], ALU.add).then_inc(logit_ready, 1)

                def step(k, b):
                    t = k * B + b
                    if not early(t - B):
                        dve.wait_ge(turned, t - B + 1)
                        dve.wait_ge(kept, t - B + 1)
                    nc.vector.tensor_scalar(xn[b][:], tile_of(x, t), stats[:, bass.ds(t, 1), 0], inv[:, bass.ds(t, 1)],
                                            ALU.subtract, ALU.mult).then_inc(normed, 1)
                    if not early(t - 2):
                        keep_logit(t - 2, b % 2)

                loop(dve, step)
                for u in (NT - 2, NT - 1):
                    keep_logit(u, u % 2)

            @block.gpsimd
            def _(pool):
                pool.wait_ge(shift_loaded, 16)

                def step(k, b):
                    t = k * B + b
                    pool.wait_ge(normed, t + 1)
                    nc.gpsimd.tensor_tensor(tile_of(x, t), tile_of(x, t), shift[:], ALU.add)

                loop(pool, step)


def route(nc, cst, dr, tag, E, logit, plan, expert_weights):
    with ExitStack() as ctx:
        sb = lambda n, s, d=F32: ctx.enter_context(nc.sbuf_tensor(tag + n, s, d))
        sem = cst.semaphores.stage(tag)
        pb = lambda n, s: ctx.enter_context(nc.psum_tensor(tag + n, s, F32))
        MT = plan.token.shape[1]
        BITS = P.bit_length() - 1
        HALF = NP // 2
        expert_no = sb("expert_no", [P, NT, E])
        first_of = sb("first_of", [P, E, NT])
        top = [sb(f"top{c}", [P, NT]) for c in range(2)]
        least = sb("least", [P, NT])
        key = sb("key", [P, NT, E])
        chosen = [sb(f"chosen{c}", [P, NT, E]) for c in range(2)]
        either = sb("either", [P, NT, E])
        ratio = sb("ratio", [P, NT])
        sums = sb("sums", [P, E, NT])
        upto = sb("upto", [P, E, NT])
        tiles = sb("tiles", [P, E])
        tiles_i = sb("tiles_i", [P, E], I32)
        ends = sb("ends", [P, E])
        ones = sb("ones_e", [P, E])
        base = sb("base", [P, E])
        slot = either
        slot_f = [sb(f"slot_f{c}", [P, NT]) for c in range(2)]
        slot_part = [[sb(f"slot_part{c}_{i}", [P, NT], I32) for i in range(2)] for c in range(2)]
        slot_at = [[sb(f"slot_at{c}_{i}", [P, NT], F16) for i in range(2)] for c in range(2)]
        number = sb("number", [P, P, NT], F16)
        token_no = sb("token_no", [P, NT], F16)
        at_place = sb("at_place", [P, P, NT], F16)
        token_at = sb("token_at", [P, MT, NT], F16)
        ps_rank, ps_sum, ps_token = pb("ps_rank", [P, BANK]), pb("ps_sum", [P, BANK]), pb("ps_token", [P, BANK])
        consts, numbered = sem("consts"), sem("numbered")
        gap_ready, exp_ready, picked, ranked, placed, tokens_known = (
            sem("gap_ready"), sem("exp_ready"), sem("picked"), sem("ranked"), sem("placed"), sem("tokens_known"))
        token_ready = sem("token_ready")

        with nc.Block() as block:

            @block.sync
            def _(sp):
                sp.dma_start(expert_weights.b1_rows[:], expert_weights.b1.rearrange("e (k p) -> (e k) p", p=P)).then_inc(
                    expert_weights.b1_loaded, 16)
                for b in range(expert_weights.buffers):
                    load_expert(sp, expert_weights, b, b)

            @block.scalar
            def _(act):
                nc.scalar.preload_act_table(ACT.Exp)
                act.wait_ge(gap_ready, 1)
                nc.scalar.activation(ratio[:], ratio[:], ACT.Exp).then_inc(exp_ready, 1)

            @block.tensor
            def _(pe):
                pe.wait_ge(picked, 1)
                flat = either[:].rearrange("p t e -> p (t e)")
                nc.tensor.matmul(ps_rank[:, 0:NT * E], cst.before[:], flat, start=True, stop=True)
                nc.tensor.matmul(ps_sum[:, 0:NT * E], cst.ones[:], flat, start=True, stop=True).then_inc(ranked, 1)
                for c in range(2):
                    pe.wait_ge(placed, c + 1)
                    for t in range(NT):
                        last = nc.tensor.matmul(ps_token[:, 0:MT], at_place[:, :, t], token_at[:, :, t],
                                                start=c == 0 and t == 0, stop=c == 1 and t == NT - 1, skip_group_check=True)
                    last.then_inc(tokens_known, 1)

            @block.vector
            def _(dve):
                dve.wait_ge(consts, 1)
                wide = lambda a: a.unsqueeze(2).to_broadcast([P, NT, E])
                for c in range(2):
                    nc.vector.tensor_reduce(top[c][:], logit[:], AX.X, ALU.max)
                    dve.drain()
                    nc.vector.tensor_tensor(key[:], logit[:], wide(top[c][:]), ALU.is_equal)
                    dve.drain()
                    nc.vector.scalar_tensor_tensor(key[:], key[:], -100.0, expert_no[:], ALU.mult, ALU.add)
                    dve.drain()
                    nc.vector.tensor_reduce(least[:], key[:], AX.X, ALU.min)
                    dve.drain()
                    nc.vector.tensor_tensor(chosen[c][:], key[:], wide(least[:]), ALU.is_equal)
                    dve.drain()
                    if c == 0:
                        nc.vector.scalar_tensor_tensor(logit[:], chosen[c][:], -3e38, logit[:], ALU.mult, ALU.add)
                        dve.drain()
                nc.vector.tensor_tensor(either[:], chosen[0][:], chosen[1][:], ALU.add).then_inc(picked, 1)
                nc.vector.tensor_tensor(ratio[:], top[1][:], top[0][:], ALU.subtract).then_inc(gap_ready, 1)
                dve.wait_ge(ranked, 1)
                nc.vector.tensor_copy(sums[:].rearrange("p e t -> p t e"),
                                      ps_sum[:, 0:NT * E].rearrange("p (t e) -> p t e", e=E))
                dve.drain()
                nc.vector.tensor_tensor_scan(upto[:].rearrange("p e t -> p (e t)"), first_of[:].rearrange("p e t -> p (e t)"),
                                             sums[:].rearrange("p e t -> p (e t)"), 0.0, ALU.mult, ALU.add)
                dve.drain()
                nc.vector.tensor_scalar(tiles_i[:], upto[:, :, NT - 1], float(P - 1), None, ALU.add)
                dve.drain()
                nc.vector.tensor_scalar(tiles_i[:], tiles_i[:], BITS, None, ALU.arith_shift_right)
                dve.drain()
                nc.vector.tensor_scalar(tiles[:], tiles_i[:], 1.0, None, ALU.max)
                dve.drain()
                nc.vector.tensor_tensor_scan(ends[:], ones[:], tiles[:], 0.0, ALU.mult, ALU.add)
                dve.drain()
                nc.vector.tensor_copy(plan.bounds[:, :, 1], ends[0:1, :])
                nc.vector.tensor_tensor(base[:], ends[:], tiles[:], ALU.subtract)
                dve.drain()
                nc.vector.tensor_copy(plan.bounds[:, :, 0], base[0:1, :])
                nc.vector.tensor_tensor(upto[:], upto[:], sums[:], ALU.subtract)
                dve.drain()
                nc.vector.scalar_tensor_tensor(upto[:], base[:].unsqueeze(2).to_broadcast([P, E, NT]), float(P), upto[:],
                                               ALU.mult, ALU.add)
                dve.drain()
                nc.vector.tensor_tensor(slot[:], ps_rank[:, 0:NT * E].rearrange("p (t e) -> p t e", e=E),
                                        upto[:].rearrange("p e t -> p t e"), ALU.add)
                dve.drain()
                to_all = lambda a, n: a.unsqueeze(1).to_broadcast([P, n, NT])
                dve.wait_ge(numbered, 1)
                for c in range(2):
                    nc.vector.tensor_tensor(key[:], slot[:], chosen[c][:], ALU.mult)
                    dve.drain()
                    nc.vector.tensor_reduce(slot_f[c][:], key[:], AX.X, ALU.add)
                    dve.drain()
                    nc.vector.tensor_copy(plan.slot[c][:], slot_f[c][:])
                    dve.drain()
                    nc.vector.tensor_scalar(slot_part[c][0][:], plan.slot[c][:], P - 1, None, ALU.bitwise_and)
                    nc.vector.tensor_scalar(slot_part[c][1][:], plan.slot[c][:], BITS, None, ALU.logical_shift_right)
                    dve.drain()
                    for i in range(2):
                        nc.vector.tensor_copy(slot_at[c][i][:], slot_part[c][i][:])
                    dve.drain()
                    if c > 0:
                        dve.wait_ge(tokens_known, c)
                    nc.vector.tensor_tensor(token_at[:], number[:, 0:MT, :], to_all(slot_at[c][1][:], MT), ALU.is_equal)
                    nc.vector.tensor_tensor(at_place[:], number[:], to_all(slot_at[c][0][:], P), ALU.is_equal)
                    dve.drain()
                    nc.vector.tensor_tensor(token_at[:], token_at[:], to_all(token_no[:], MT), ALU.mult)
                    dve.drain()
                    dve.sem_inc(placed, 1)
                dve.wait_ge(exp_ready, 1)
                nc.vector.tensor_scalar(least[:], ratio[:], 1.0, None, ALU.add)
                dve.drain()
                nc.vector.reciprocal(plan.weight[0][:], least[:])
                dve.drain()
                nc.vector.tensor_tensor(plan.weight[1][:], plan.weight[0][:], ratio[:], ALU.mult)
                dve.wait_ge(tokens_known, 2)
                nc.vector.tensor_scalar(plan.token[:], ps_token[:, 0:MT], float(HALF), None, ALU.add).then_inc(token_ready, 1)

            @block.gpsimd
            def _(pool):
                iota = lambda out, pattern, step, base=0: nc.gpsimd.iota(out, pattern, base=base, channel_multiplier=step,
                                                                         allow_small_or_imprecise_dtypes=True)
                iota(expert_no[:], [[0, NT], [1, E]], 0)
                nc.gpsimd.memset(ones[:], 1.0)
                nc.gpsimd.memset(first_of[:], 1.0)
                pool.drain()
                nc.gpsimd.memset(first_of[:, :, 0:1], 0.0).then_inc(consts, 1)
                iota(token_no[:], [[P, NT]], 1, -HALF)
                iota(number[:], [[1, P], [0, NT]], 0).then_inc(numbered, 1)
                pool.wait_ge(token_ready, 1)
                pool.indirect_dma_start(expert_weights.x[:], None, dr.tokens, bass.IndirectOffsetOnAxis(
                    ap=plan.token[:, 0:1], axis=0)).then_inc(expert_weights.x_loaded, 16)


def open_experts(ctx, nc, cst, tag, experts, w1, w2, b1, buffers):
    weights = Weights()
    sb = lambda n, s: ctx.enter_context(nc.sbuf_tensor(tag + n, s, F32))
    sem = cst.semaphores.stage(tag)
    weights.up = [sb(f"up{b}", [P, KD, HID]) for b in range(buffers)]
    weights.down = [sb(f"down{b}", [P, KH, D]) for b in range(buffers)]
    weights.b1, weights.b1_rows, weights.b1_loaded = b1, sb("b1_rows", [experts * KH, P]), sem("b1_loaded")
    weights.x, weights.x_loaded = sb("x", [P, D]), sem("x_loaded")
    weights.loaded = [sem(f"w_loaded{b}") for b in range(buffers)]
    weights.w1, weights.w2, weights.buffers, weights.experts = w1, w2, buffers, experts
    return weights


def load_expert(sp, weights, e, b):
    sp.dma_start(weights.up[b][:], weights.w1[bass.ds(e, 1)].rearrange("a (k p) h -> p (a k) h", p=P)).then_inc(
        weights.loaded[b], 16)
    sp.dma_start(weights.down[b][:], weights.w2[bass.ds(e, 1)].rearrange("a (k p) d -> p (a k) d", p=P)).then_inc(
        weights.loaded[b], 16)


def run_experts(nc, cst, dr, tag, weights, b2, function, plan):
    with ExitStack() as ctx:
        sb = lambda n, s, d=F32: ctx.enter_context(nc.sbuf_tensor(tag + n, s, d))
        sem = cst.semaphores.stage(tag)
        pb = lambda n, s: ctx.enter_context(nc.psum_tensor(tag + n, s, F32))
        E, B = weights.experts, weights.buffers
        up, down, w_loaded = weights.up, weights.down, weights.loaded
        b1_rows, b1_loaded = weights.b1_rows, weights.b1_loaded
        b1_col = sb("b1_col", [P, E * KH])
        b2_all = sb("b2_all", [P, E, D])
        x, x_loaded = weights.x, weights.x_loaded
        index = sb("index", [P, 1], I32)
        xT = sb("xT", [P, KD, P])
        hT = sb("hT", [P, KH, P])
        y = sb("y", [P, D])
        ps_x, ps_y, ps_b = pb("ps_x", [P, KD, P]), pb("ps_y", [P, BANK]), pb("ps_b", [P, BANK])
        ps_h = [pb(f"ps_h{c}", [P, BANK]) for c in range(KH)]
        b1_turned, b2_loaded = sem("b1_turned"), sem("b2_loaded")
        x_turned, xT_ready = sem("x_turned"), sem("xT_ready")
        h_ready, hT_ready, y_product, y_ready = sem("h_ready"), sem("hT_ready"), sem("y_product"), sem("y_ready")
        y_stored, y_free = sem("y_stored"), sem("y_free")
        most = max_tiles(E)

        def bounds(engine, e):
            _, (start, end) = nc.values_load_multi_w_load_instructions(
                plan.bounds[0:1, bass.ds(e, 1), :].rearrange("p e c -> p (e c)"), engines=[engine.engine],
                min_val=0, max_val=most)
            return start, nc.s_assert_within(end, 1, most, skip_runtime_bounds_check_because="an expert has a tile")

        def expert_loop(engine, step):
            with engine.Fori(0, E // B) as k:
                for b in range(B):
                    step(k * B + b, k, b, *bounds(engine, k * B + b))

        with nc.Block() as block:

            @block.sync
            def _(sp):
                def store_tiles(e):
                    start, end = bounds(sp, e)
                    with sp.Fori(start, end) as q:
                        sp.wait_ge(y_ready, q + 2)
                        sp.dma_start(dr.slots[rows(q), :], y[:]).then_inc(y_stored, 16)
                        sp.wait_ge(y_stored, (q + 1) * 16)
                        sp.sem_inc(y_free, 1)

                sp.sem_inc(y_free, 1)
                sp.dma_start(b2_all[:], b2.partition_broadcast(P)).then_inc(b2_loaded, 16)
                with sp.Fori(0, E // B - 1) as k:
                    for b in range(B):
                        store_tiles(k * B + b)
                        load_expert(sp, weights, k * B + (b + B), b)
                for b in range(B):
                    store_tiles(E - B + b)

            @block.gpsimd
            def _(pool):
                total = pool.value_load(plan.bounds[0:1, E - 1, 1:2], min_val=1, max_val=most)

                def gather(q):
                    nc.gpsimd.tensor_copy(index[:], plan.token[:, bass.ds(q, 1)])
                    pool.drain()
                    pool.indirect_dma_start(x[:], None, dr.tokens, bass.IndirectOffsetOnAxis(ap=index[:], axis=0)).then_inc(x_loaded, 16)

                with pool.Fori(1, total + 1) as q:
                    pool.wait_ge(x_turned, q)
                    gather(q)
                pool.wait_ge(x_loaded, total * 16 + 16)

            @block.tensor
            def _(pe):
                pe.wait_ge(b1_loaded, 16)
                nc.tensor.transpose(ps_b[:, 0:E * KH], b1_rows[:], cst.ident[0:E * KH, 0:E * KH]).then_inc(b1_turned, 1)

                def turn(q):
                    pe.wait_ge(x_loaded, q * 16 + 16)
                    for c in range(KD):
                        last = nc.tensor.transpose(ps_x[:, c, :], x[:, c * P:(c + 1) * P], cst.ident[:])
                    last.then_inc(x_turned, 1)

                turn(0)

                def step(e, k, b, start, end):
                    with pe.Fori(start, end) as q:
                        pe.wait_ge(w_loaded[b], k * 32 + 32)
                        pe.wait_ge(xT_ready, q + 1)
                        for c in range(KH):
                            for i in range(KD):
                                last = nc.tensor.matmul(ps_h[c][:, 0:P], up[b][:, i, c * P:(c + 1) * P], xT[:, i, :],
                                                        start=i == 0, stop=i == KD - 1)
                            last.then_inc(h_ready, 1)
                        turn(q + 1)
                        pe.wait_ge(y_ready, q + 1)
                        for c in range(KH):
                            if c % 2 == 0:
                                pe.wait_ge(hT_ready, q * KH + (c + 2))
                            last = nc.tensor.matmul(ps_y[:, 0:D], hT[:, c, :], down[b][:, c, :],
                                                    start=c == 0, stop=c == KH - 1)
                        last.then_inc(y_product, 1)

                expert_loop(pe, step)

            @block.scalar
            def _(act):
                nc.scalar.preload_act_table(function)
                act.wait_ge(b1_turned, 1)
                nc.scalar.copy(b1_col[:], ps_b[:, 0:E * KH])
                act.drain()

                def step(e, k, b, start, end):
                    with act.Fori(start, end) as q:
                        for c in range(KH):
                            act.wait_ge(h_ready, q * KH + (c + 1))
                            nc.scalar.activation(hT[:, c, :], ps_h[c][:, 0:P], function,
                                                 bias=b1_col[:, bass.ds(e * KH + c, 1)]).then_inc(hT_ready, 1)

                expert_loop(act, step)

            @block.vector
            def _(dve):
                dve.sem_inc(y_ready, 1)
                dve.wait_ge(x_turned, 1)
                nc.vector.tensor_copy(xT[:], ps_x[:]).then_inc(xT_ready, 1)
                dve.wait_ge(b2_loaded, 16)

                def step(e, k, b, start, end):
                    with dve.Fori(start, end) as q:
                        dve.wait_ge(x_turned, q + 2)
                        nc.vector.tensor_copy(xT[:], ps_x[:]).then_inc(xT_ready, 1)
                        dve.wait_ge(y_product, q + 1)
                        dve.wait_ge(y_free, q + 1)
                        nc.vector.tensor_tensor(y[:], ps_y[:, 0:D], b2_all[:, bass.ds(e, 1), :].rearrange(
                            "p a d -> p (a d)"), ALU.add).then_inc(y_ready, 1)

                expert_loop(dve, step)


def combine(nc, cst, dr, tag, plan, source=None, target=None, parts=None, normed_out=None, relvectors=None, tokens=None,
            base=None, gamma=None, output=None):
    final = output is not None
    with ExitStack() as ctx:
        sb = lambda n, s, d=F32: ctx.enter_context(nc.sbuf_tensor(tag + n, s, d))
        pair = lambda n, s, d=F32: [sb(f"{n}{b}", s, d) for b in range(2)]
        sem = cst.semaphores.stage(tag)
        B = 4
        y = [[sb(f"y{b}_{c}", [P, D]) for c in range(2)] for b in range(B)]
        mixed, out, small = pair("mixed", [P, D]), pair("out", [P, D]), pair("small", [P, 10])
        got = [sem(f"got{b}") for b in range(B)]
        stored = [sem(f"stored{b}") for b in range(2)]
        var_ready, std_ready, taken = sem("var_ready"), sem("std_ready"), sem("taken")
        begun, inverted = sem("begun"), sem("inverted")
        if final:
            normal, scale, w_loaded = pair("normal", [P, D]), sb("gamma", [P, D]), sem("w_loaded")
            centred, ready = sem("centred"), sem("ready")
        else:
            x, hn, rest = pair("x", [P, D]), pair("hn", [P, D]), pair("rest", [P, D])
            loaded = [sem(f"loaded{b}") for b in range(2)]
            hn_stored = [sem(f"hn_stored{b}") for b in range(2)]
            normed, hi_ready, rest_ready, lo_ready = sem("normed"), sem("hi_ready"), sem("rest_ready"), sem("lo_ready")
            rels = slice(REL_ROW, REL_ROW + N_REL)
            wide, vectors = pair("wide", [P, P]), sb("vectors", [P, D])
            ps_rel = [ctx.enter_context(nc.psum_tensor(tag + f"ps_rel{b}", [P, BANK], F32)) for b in range(2)]
            v_loaded, cleared, rel_copied, rel_turned = sem("v_loaded"), sem("cleared"), sem("rel_copied"), sem("rel_turned")
            v_hi_ready, v_rest_ready = sem("v_hi_ready"), sem("v_rest_ready")
        loop = lambda engine, step: tile_loop(engine, step, n=B, ahead=2, behind=2)
        buffer = lambda k, b: (k * 2 + b // 2, b % 2)

        with nc.Block() as block:

            @block.sync
            def _(sp):
                if final:
                    sp.dma_start(scale[:], gamma.partition_broadcast(P)).then_inc(w_loaded, 16)

                def load(t, b):
                    sp.dma_start(x[b % 2][:], source[rows(t), :]).then_inc(loaded[b % 2], 16)

                def store_normed(u, b):
                    sp.wait_ge(normed, u + 1)
                    sp.dma_start(normed_out[rows(u), :], hn[b % 2][:]).then_inc(hn_stored[b % 2], 16)

                def step(k, b):
                    t = k * B + b
                    sp.wait_ge(ready if final else taken, t + 1)
                    if not final:
                        sp.dma_start(target[rows(t), :], out[b % 2][:]).then_inc(stored[b % 2], 16)
                        if not past(t + 2):
                            load(t + 2, b)
                        if not early(t - 1):
                            store_normed(t - 1, b + 1)
                    elif past(t + 1):
                        sp.dma_start(output[t * P:N_NODES, :], out[b % 2][0:LAST, :]).then_inc(stored[b % 2], 16)
                    else:
                        sp.dma_start(output[rows(t), :], out[b % 2][:]).then_inc(stored[b % 2], 16)

                if not final:
                    load(0, 0)
                    load(1, 1)
                    sp.dma_start(vectors[rels, :], relvectors).then_inc(v_loaded, 16)
                loop(sp, step)
                if not final:
                    store_normed(NT - 1, NT - 1)
                for b in range(2):
                    sp.wait_ge(stored[b], 16 * uses(b))
                    if not final:
                        sp.wait_ge(hn_stored[b], 16 * uses(b))

            @block.gpsimd
            def _(pool):
                if not final:
                    for b in range(2):
                        nc.gpsimd.memset(wide[b][:], 0.0).then_inc(cleared, 1)

                def gather(t):
                    if t >= B:
                        pool.wait_ge(taken, t - B + 1)
                    for c in range(2):
                        pool.indirect_dma_start(y[t % B][c][:], None, dr.slots, bass.IndirectOffsetOnAxis(
                            ap=plan.slot[c][:, t:t + 1], axis=0)).then_inc(got[t % B], 16)

                gather(0)
                gather(1)
                for t in range(NT):
                    if t + 2 < NT:
                        gather(t + 2)

            if not final:
                @block.tensor
                def _(pe):
                    def step(k, b):
                        t = k * B + b
                        pe.wait_ge(rel_copied, t + 1)
                        nc.tensor.transpose(ps_rel[b % 2][:, 0:P], wide[b % 2][:], cst.ident[:]).then_inc(rel_turned, 1)

                    loop(pe, step)

            @block.scalar
            def _(act):
                nc.scalar.preload_act_table(ACT.Sqrt)

                def split(u, b):
                    act.wait_ge(normed, u + 1)
                    nc.scalar.copy(tile_of(parts, u)[:, 0:D], hn[b % 2][:]).then_inc(hi_ready, 1)

                def low(u, b):
                    act.wait_ge(rest_ready, u + 1)
                    nc.scalar.activation(tile_of(parts, u)[:, D:2 * D], rest[b % 2][:], ACT.Copy, scale=LO_SCALE).then_inc(lo_ready, 1)

                def keep_relations(u, b):
                    act.wait_ge(rel_turned, u + 1)
                    nc.scalar.copy(cst.counts[rels, bass.ds(u, 1), NT - 1, :].rearrange("p a n -> p (a n)"), ps_rel[b % 2][rels, 0:P])

                def step(k, b):
                    t = k * B + b
                    if not final:
                        if not early(t - 1):
                            keep_relations(t - 1, b + 1)
                        nc.scalar.copy(wide[b % 2][:, rels], tile_of(cst.rel_count, t)[:, 0:N_REL]).then_inc(rel_copied, 1)
                        if not early(t - 1):
                            split(t - 1, b + 1)
                        if not early(t - 2):
                            low(t - 2, b)
                    act.wait_ge(var_ready, t + 1)
                    norm_root(nc, cst, small[b % 2]).then_inc(std_ready, 1)

                if not final:
                    act.wait_ge(cleared, 2)
                loop(act, step)
                if not final:
                    keep_relations(NT - 1, NT - 1)
                    split(NT - 1, NT - 1)
                    low(NT - 2, NT - 2)
                    low(NT - 1, NT - 1)
                    act.drain()
                    act.wait_ge(v_loaded, 16)
                    nc.scalar.copy(parts[rels, NT - 1, 0:D], vectors[rels, :]).then_inc(v_hi_ready, 1)
                    act.wait_ge(v_rest_ready, 1)
                    nc.scalar.activation(parts[rels, NT - 1, D:2 * D], rest[0][rels, :], ACT.Copy, scale=LO_SCALE)

            @block.vector
            def _(dve):
                if final:
                    dve.wait_ge(w_loaded, 16)

                def norm_of(u, use, b):
                    mean, inv = small[b][:, 6:7], small[b][:, 9:10]
                    if final:
                        nc.vector.scalar_tensor_tensor(normal[b][:], mixed[b][:], mean, scale[:], ALU.subtract,
                                                       ALU.mult).then_inc(centred, 1)
                    else:
                        if not early(u - 2):
                            dve.wait_ge(hn_stored[b], use * 16)
                        nc.vector.tensor_scalar(hn[b][:], out[b][:], mean, inv, ALU.subtract, ALU.mult).then_inc(normed, 1)

                def inverse_of(u, b):
                    dve.wait_ge(std_ready, u + 1)
                    nc.vector.reciprocal(small[b][:, 9:10], small[b][:, 8:9]).then_inc(inverted, 1)

                def last_of(u, use, b):
                    if not early(u - 2):
                        dve.wait_ge(stored[b], use * 16)
                    nc.vector.scalar_tensor_tensor(out[b][:], normal[b][:], small[b][:, 9:10], tile_of(base, u), ALU.mult,
                                                   ALU.add).then_inc(ready, 1)

                def remain(u, b):
                    dve.wait_ge(hi_ready, u + 1)
                    if not early(u - 2):
                        dve.wait_ge(lo_ready, u - 1)
                    nc.vector.tensor_tensor(rest[b][:], hn[b][:], tile_of(parts, u)[:, 0:D], ALU.subtract).then_inc(rest_ready, 1)

                def step(k, b):
                    t = k * B + b
                    use, d = buffer(k, b)
                    behind = not early(t - 1)
                    before_use, before_d = buffer(k, b - 1) if b > 0 else buffer(k - 1, B - 1)
                    dve.wait_ge(got[b], k * 32 + 32)
                    if final:
                        start = tile_of(tokens, t)
                    else:
                        dve.wait_ge(loaded[d], use * 16 + 16)
                        start = x[d][:]
                    nc.vector.scalar_tensor_tensor(mixed[d][:], y[b][0][:], plan.weight[0][:, bass.ds(t, 1)], start,
                                                   ALU.mult, ALU.add).then_inc(begun, 1)
                    if behind:
                        inverse_of(t - 1, before_d)
                        if final:
                            norm_of(t - 1, before_use, before_d)
                    whole = mixed if final else out
                    if not final and not early(t - 2):
                        dve.wait_ge(stored[d], use * 16)
                    dve.wait_ge(begun, t + 1)
                    nc.vector.scalar_tensor_tensor(whole[d][:], y[b][1][:], plan.weight[1][:, bass.ds(t, 1)], mixed[d][:],
                                                   ALU.mult, ALU.add).then_inc(taken, 1)
                    if behind:
                        dve.wait_ge(inverted, t)
                        if final:
                            dve.wait_ge(centred, t)
                            last_of(t - 1, before_use, before_d)
                        else:
                            norm_of(t - 1, before_use, before_d)
                    dve.wait_ge(taken, t + 1)
                    nc.vector.bn_stats(small[d][:, 0:6], whole[d][:])
                    if not final and not early(t - 2):
                        remain(t - 2, d)
                    dve.drain()
                    nc.vector.bn_aggr(small[d][:, 6:8], small[d][:, 0:6]).then_inc(var_ready, 1)

                loop(dve, step)
                u, use, d = NT - 1, (NT - 1) // 2, (NT - 1) % 2
                inverse_of(u, d)
                dve.drain()
                norm_of(u, use, d)
                if final:
                    dve.drain()
                    last_of(u, use, d)
                else:
                    remain(NT - 2, 1 - d)
                    dve.drain()
                    remain(NT - 1, d)
                    dve.wait_ge(v_hi_ready, 1)
                    dve.wait_ge(v_loaded, 16)
                    nc.vector.tensor_tensor(rest[0][rels, :], vectors[rels, :], parts[rels, NT - 1, 0:D],
                                            ALU.subtract).then_inc(v_rest_ready, 1)


def gru(nc, ins, cst, dr, sums, states, source, result, stats):
    G = 3 * D
    GC = G // P
    with ExitStack() as ctx:
        sb = lambda n, s, d=F32: ctx.enter_context(nc.sbuf_tensor("gru_" + n, s, d))
        sem = cst.semaphores.stage("gru_")
        pb = lambda n, s: ctx.enter_context(nc.psum_tensor("gru_" + n, s, F32))
        B = 4
        w_rows = sb("w_rows", [P, 2, GC, D])
        wT = sb("wT", [P, 2, KD, G])
        bias = sb("bias", [P, 2, G])
        both = sb("both", [P, 2 * D])
        x = [[sb(f"x{b}_{i}", [P, D]) for i in range(2)] for b in range(B)]
        before = [sb(f"before{b}", [P, D]) for b in range(B)]
        xT = [sb(f"xT{b}", [P, 2, KD, P]) for b in range(2)]
        pre = [sb(f"pre{b}", [P, 2 * D]) for b in range(2)]
        gate = [sb(f"gate{b}", [P, 2 * D]) for b in range(2)]
        hidden = [sb(f"hidden{b}", [P, D]) for b in range(2)]
        cand = [sb(f"cand{b}", [P, D]) for b in range(2)]
        new = [sb(f"new{b}", [P, D]) for b in range(2)]
        kept = [sb(f"kept{b}", [P, D]) for b in range(2)]
        taken = [sb(f"taken{b}", [P, D]) for b in range(2)]
        partial = sb("partial", [P, 6])
        moments = [sb(f"moments{b}", [P, 2]) for b in range(2)]
        ps_t = [pb(f"ps_t{b}", [P, 2, KD, P]) for b in range(2)]
        ps_g = [pb(f"ps_g{b}", [P, 2 * D]) for b in range(2)]
        ps_n = [pb(f"ps_n{b}", [P, 2, D]) for b in range(2)]
        w_loaded, b_loaded, w_turned = sem("w_loaded"), sem("b_loaded"), sem("w_turned")
        w_ready = [sem(f"w_ready{b}") for b in range(2)]
        w_banks = [a[:].rearrange("p i c d -> p (i c d)") for a in ps_t] + [a[:] for a in ps_g]

        def chunk(n):
            i, g = n // GC, n % GC
            return wT[:, i, :, g * P:(g + 1) * P], w_banks[n % len(w_banks)][:, 0:D].rearrange("p (c d) -> p c d", c=KD)

        loaded = [sem(f"loaded{b}") for b in range(B)]
        turned, xT_ready, product = sem("turned"), sem("xT_ready"), sem("product")
        pre_ready, gate_ready, cand_ready, new_ready, used = (sem("pre_ready"), sem("gate_ready"), sem("cand_ready"),
                                                             sem("new_ready"), sem("used"))
        loop = lambda engine, step: tile_loop(engine, step, n=B, ahead=1)

        with nc.Block() as block:

            @block.sync
            def _(sp):
                for i, n in enumerate(("L1_gnn_w_ih", "L1_gnn_w_hh")):
                    sp.dma_start(w_rows[:, i], ins[n].rearrange("(g p) d -> p g d", p=P)).then_inc(w_loaded, 16)
                for i, n in enumerate(("L1_gnn_b_ih", "L1_gnn_b_hh")):
                    sp.dma_start(bias[:, i], ins[n].partition_broadcast(P)).then_inc(b_loaded, 16)

                def step(k, b):
                    t = k * B + b
                    if not at_start(k):
                        sp.wait_ge(used, t - (B - 1))
                    sp.dma_start(x[b][0][:], sums[rows(t), :]).then_inc(loaded[b], 16)
                    sp.dma_start(x[b][1][:], states[rows(t), :]).then_inc(loaded[b], 16)
                    sp.dma_start(before[b][:], source[rows(t), :]).then_inc(loaded[b], 16)

                loop(sp, step)

            @block.tensor
            def _(pe):
                pe.wait_ge(w_loaded, 32)
                for n in range(2 * GC):
                    i, g = n // GC, n % GC
                    if n >= len(w_banks):
                        pe.wait_ge(w_ready[n % 2], (n - len(w_banks)) // 2 + 1)
                    for c in range(KD):
                        last = nc.tensor.transpose(w_banks[n % len(w_banks)][:, c * P:(c + 1) * P],
                                                   w_rows[:, i, g, c * P:(c + 1) * P], cst.ident[:])
                    last.then_inc(w_turned, 1)
                for done in w_ready:
                    pe.wait_ge(done, GC)

                def turn(b, loads):
                    pe.wait_ge(loaded[b], loads * 48)
                    for i in range(2):
                        for c in range(KD):
                            last = nc.tensor.transpose(ps_t[b % 2][:, i, c, :], x[b][i][:, c * P:(c + 1) * P], cst.ident[:])
                    last.then_inc(turned, 1)

                def step(k, b):
                    t, d = k * B + b, b % 2
                    if not past(t + 1):
                        turn((b + 1) % B, k + 1 + (b + 1) // B)
                    pe.wait_ge(xT_ready, t + 1)
                    if not (at_start(k) and b < 2):
                        pe.wait_ge(pre_ready, t - 1)
                    for i in range(2):
                        for c in range(KD):
                            nc.tensor.matmul(ps_g[d][:], xT[d][:, i, c, :], wT[:, i, c, 0:2 * D],
                                             start=i == 0 and c == 0, stop=i == 1 and c == KD - 1)
                    for i in range(2):
                        for c in range(KD):
                            last = nc.tensor.matmul(ps_n[d][:, i, :], xT[d][:, i, c, :], wT[:, i, c, 2 * D:G],
                                                    start=c == 0, stop=c == KD - 1)
                    last.then_inc(product, 1)

                turn(0, 1)
                loop(pe, step)

            @block.scalar
            def _(act):
                nc.scalar.preload_act_table(ACT.Sigmoid)
                for n in range(0, 2 * GC, 2):
                    act.wait_ge(w_turned, n + 1)
                    nc.scalar.copy(*chunk(n)).then_inc(w_ready[0], 1)

                def copy_turned(t, d):
                    act.wait_ge(turned, t + 1)
                    nc.scalar.copy(xT[d][:], ps_t[d][:]).then_inc(xT_ready, 1)

                def step(k, b):
                    t, d = k * B + b, b % 2
                    if not past(t + 1):
                        if not (at_start(k) and b == 0):
                            act.wait_ge(product, t)
                        copy_turned(t + 1, 1 - d)
                    act.wait_ge(pre_ready, t + 1)
                    nc.scalar.activation(gate[d][:], pre[d][:], ACT.Sigmoid).then_inc(gate_ready, 1)
                    act.wait_ge(cand_ready, t + 1)
                    nc.scalar.activation(new[d][:], cand[d][:], ACT.Tanh).then_inc(new_ready, 1)

                copy_turned(0, 0)
                loop(act, step)

            @block.vector
            def _(dve):
                for n in range(1, 2 * GC, 2):
                    dve.wait_ge(w_turned, n + 1)
                    nc.vector.tensor_copy(*chunk(n)).then_inc(w_ready[1], 1)
                dve.wait_ge(b_loaded, 32)
                nc.vector.tensor_tensor(both[:], bias[:, 0, 0:2 * D], bias[:, 1, 0:2 * D], ALU.add)
                dve.drain()

                def finish(t, d):
                    dve.wait_ge(new_ready, t + 1)
                    nc.vector.tensor_tensor(taken[d][:], taken[d][:], new[d][:], ALU.mult)
                    dve.drain()
                    out = result[:, bass.ds(t, 1), :].rearrange("p a d -> p (a d)")
                    nc.vector.tensor_tensor(out, taken[d][:], kept[d][:], ALU.add)
                    dve.drain()
                    nc.vector.bn_stats(partial[:], out)
                    dve.drain()
                    nc.vector.bn_aggr(moments[d][:], partial[:])
                    dve.drain()
                    nc.vector.tensor_copy(tile_of(stats, t), moments[d][:])

                def step(k, b):
                    t, d = k * B + b, b % 2
                    dve.wait_ge(product, t + 1)
                    nc.vector.tensor_tensor(pre[d][:], ps_g[d][:], both[:], ALU.add)
                    nc.vector.tensor_tensor(hidden[d][:], ps_n[d][:, 1, :], bias[:, 1, 2 * D:G], ALU.add)
                    nc.vector.tensor_tensor(cand[d][:], ps_n[d][:, 0, :], bias[:, 0, 2 * D:G], ALU.add)
                    dve.drain()
                    dve.sem_inc(pre_ready, 1)
                    if not (at_start(k) and b == 0):
                        finish(t - 1, 1 - d)
                    dve.wait_ge(gate_ready, t + 1)
                    nc.vector.tensor_tensor(hidden[d][:], hidden[d][:], gate[d][:, 0:D], ALU.mult)
                    dve.wait_ge(loaded[b], (k + 1) * 48)
                    nc.vector.tensor_tensor(kept[d][:], gate[d][:, D:2 * D], x[b][1][:], ALU.mult)
                    dve.drain()
                    nc.vector.tensor_tensor(cand[d][:], cand[d][:], hidden[d][:], ALU.add).then_inc(cand_ready, 1)
                    nc.vector.tensor_scalar(taken[d][:], gate[d][:, D:2 * D], -1.0, 1.0, ALU.mult, ALU.add)
                    nc.vector.tensor_tensor(kept[d][:], kept[d][:], before[b][:], ALU.add).then_inc(used, 1)

                loop(dve, step)
                dve.drain()
                finish(NT - 1, (NT - 1) % 2)


def four_blocks(nc, ins, out):
    scratch = lambda n, r, c=D: nc.dram_tensor(n, [r, c], F32, kind="Internal").ap()
    dr = Scratch()
    dr.x0, dr.x1, dr.x2 = (scratch(f"x{i}", NP) for i in range(3))
    dr.h1, dr.h2 = scratch("h1", NP), scratch("h2", NP)
    dr.own, dr.hn, dr.red = scratch("own", NP), scratch("hn", NP), scratch("red", NP)
    dr.tokens, dr.slots = scratch("tokens", NP), scratch("slots", max_tiles(16) * P)
    with ExitStack() as ctx:
        sb = lambda n, s, d=F32: ctx.enter_context(nc.sbuf_tensor(n, s, d))
        cst = Resident()
        cst.semaphores = Semaphores(nc)
        cst.ident, cst.ones, cst.before = sb("ident", [P, P]), sb("ones", [P, P]), sb("before", [P, P])
        cst.lo_scale, cst.eps = sb("lo_scale", [P, D]), sb("eps", [P, 1])
        with ExitStack() as graph:
            gb = lambda n, s, d=F32: graph.enter_context(nc.sbuf_tensor(n, s, d))
            cst.counts = gb("counts", [P, NT, NT, P], F16)
            cst.rel_count = gb("rel_count", [P, NT, N_REL + 1])
            cst.inv_deg = gb("inv_deg", [P, NT])
            E0 = ins["L0_ffn_Wr"].shape[1]
            logit0 = gb("logit0", [P, NT, E0])
            with ExitStack() as gnn:
                layers = lambda n, s: gnn.enter_context(nc.sbuf_tensor(n, s, F32))
                cst.layer_weights, cst.layer_bias = layers("layer_weights", [P, KD, 2 * D]), layers("layer_bias", [P, D])
                cst.layer_loaded = cst.semaphores.stage("layer_")("loaded")
                with ExitStack() as edges:
                    eb = lambda n, s, d=F32: edges.enter_context(nc.sbuf_tensor(n, s, d))
                    cst.edge = eb("edge", [P, 4, EDGE_TILES])
                    cst.place_no, cst.row_no = eb("place_no", [P, NT * WIN], F16), eb("row_no", [P, P, GROUP], F16)
                    cst.base = eb("base", [P, NW, 4])
                    cst.win_node = eb("win_node", [P, WT, P], F16)
                    cst.ranges, cst.upto = eb("ranges", [1, P, 3], I32), eb("upto", [1, NW])
                    index_edges(nc, ins, cst, dr)
                    build_counts(nc, ins, cst, dr)
                with nc.sbuf_tensor("parts", [P, NT, 2 * D], F16) as parts:
                    sources, targets = (dr.x0, dr.h1, dr.h2), (dr.h1, dr.h2, dr.x1)
                    for layer in range(LAYERS):
                        project(nc, ins, cst, dr, layer, sources[layer], parts)
                        last = layer == LAYERS - 1
                        aggregate(nc, ins, cst, dr, f"agg{layer}_", parts, targets[layer], relu=not last,
                                  residual=dr.x0 if last else None, next_layer=None if last else layer + 1,
                                  mixture=(E0, ins["L0_ffn_Wr"], ins["L0_ffn_br"], ins["L0_ffn_gamma"], ins["L0_ffn_beta"],
                                           logit0) if last else None)

            def plan_for(stack, tag, experts):
                pb = lambda n, s, d=F32: stack.enter_context(nc.sbuf_tensor(tag + n, s, d))
                plan = Plan()
                plan.weight = [pb(f"weight{c}", [P, NT]) for c in range(2)]
                plan.slot = [pb(f"slot{c}", [P, NT], I32) for c in range(2)]
                plan.bounds = pb("bounds", [1, experts, 2], I32)
                plan.token = pb("token", [P, max_tiles(experts) + 1], I32)
                return plan

            with ExitStack() as mix:
                plan = plan_for(mix, "mix0_", E0)
                cst.semaphores.clear()
                with ExitStack() as matrices:
                    weights = open_experts(matrices, nc, cst, "experts0_", E0, ins["L0_ffn_W1"], ins["L0_ffn_W2"],
                                           ins["L0_ffn_b1"], 2)
                    route(nc, cst, dr, "route0_", E0, logit0, plan, weights)
                    run_experts(nc, cst, dr, "experts0_", weights, ins["L0_ffn_b2"], ACT.Gelu, plan)
                with nc.sbuf_tensor("parts_rel", [P, NT, 2 * D], F16) as parts:
                    combine(nc, cst, dr, "combine0_", plan, source=dr.x1, target=dr.x2, parts=parts, normed_out=dr.hn,
                            relvectors=ins["L1_gnn_relvectors"])
                    aggregate(nc, ins, cst, dr, "agg_rel_", parts, dr.red, relations=True)
        E1 = ins["L1_ffn_gate_w"].shape[1]
        x3, stats3 = sb("x3", [P, NT, D]), sb("x3_stats", [P, NT, 2])
        gru(nc, ins, cst, dr, dr.red, dr.hn, dr.x2, x3, stats3)
        with ExitStack() as mix:
            plan = plan_for(mix, "mix1_", E1)
            tokens = mix.enter_context(nc.sbuf_tensor("tokens1", [P, NT, D], F32))
            logit1 = mix.enter_context(nc.sbuf_tensor("logit1", [P, NT, E1], F32))
            score_rows(nc, cst, dr, "score1_", x3, stats3, E1, ins["L1_ffn_gate_w"], ins["L1_ffn_gate_b"], tokens, logit1,
                       ins["L1_ffn_beta"])
            cst.semaphores.clear()
            weights = open_experts(mix, nc, cst, "experts1_", E1, ins["L1_ffn_w1"], ins["L1_ffn_w2"], ins["L1_ffn_b1"], 4)
            route(nc, cst, dr, "route1_", E1, logit1, plan, weights)
            run_experts(nc, cst, dr, "experts1_", weights, ins["L1_ffn_b2"], ACT.Relu, plan)
            combine(nc, cst, dr, "combine1_", plan, tokens=tokens, base=x3, gamma=ins["L1_ffn_gamma"], output=out)
        cst.semaphores.clear()


_OUTPUT = "blocks_out"


def kernel(**inputs):
    from concourse import bacc
    from concourse.bass_utils import run_bass_kernel_spmd

    nc = bacc.Bacc("TRN2", target_bir_lowering=False, num_devices=1)
    arrays, ins = {}, {}
    for name, value in inputs.items():
        a = np.ascontiguousarray(value)
        arrays[f"in_{name}"] = a
        ins[name] = nc.dram_tensor(f"in_{name}", a.shape, mybir.dt.from_np(a.dtype), kind="ExternalInput").ap()
    out = nc.dram_tensor(_OUTPUT, (N_NODES, D), F32, kind="ExternalOutput").ap()
    four_blocks(nc, ins, out)
    ran = run_bass_kernel_spmd(nc, [arrays], core_ids=[0])
    return ran.results[0][_OUTPUT]
```
